# Optimizing a Trainium2 kernel written in Bass

```python
import numpy as np
import jax
import jax.numpy as jnp

def _softmax(x, axis=-1):
    return jax.nn.softmax(x, axis=axis)

def _gelu(x):
    return jax.nn.gelu(x, approximate=True)

def _silu(x):
    return jax.nn.silu(x)

def _sigmoid(x):
    return jax.nn.sigmoid(x)

def _layernorm(x, axis=-1, eps=1e-05):
    m = jnp.mean(x, axis=axis, keepdims=True)
    v = jnp.var(x, axis=axis, keepdims=True)
    return (x - m) / jnp.sqrt(v + eps)

def _scatter_add(tgt, idx, src, axis=0):
    return tgt.at[idx].add(src)

def _segment_sum(src, seg, n):
    return jax.ops.segment_sum(src, seg, n)
kernel_name = 'mk_vit_tower_cls_d2_tok_img1024_r4_944701'

def setup_inputs(seed: int=0):
    np.random.seed(seed)
    _w = jnp.asarray

    def _rec_inputs():
        import jax
        import jax.numpy as jnp
        _rk = jax.random.key(seed)
        x = -0.00150118 + 0.499729 * jax.random.normal(jax.random.fold_in(_rk, 1), (8, 256, 64, 2), jnp.float32)
        cls_tok = 0.02 * jax.random.normal(jax.random.fold_in(_rk, 5), (1, 1, 256), jnp.float32)
        return (x, cls_tok)
    x, cls_tok = _rec_inputs()

    def _L0_tok_setup():
        import jax, jax.numpy as jnp
        import numpy as np
        import math
        H = 256
        N = 64
        CH = 1
        SEQ_L = 256
        key = jax.random.key(seed)
        k1, k2, k3, k4 = jax.random.split(key, 4)
        log_dt = jax.random.uniform(k1, (H,), dtype=jnp.float32, minval=math.log(0.001), maxval=math.log(0.1))
        inv_A_real = jnp.log(0.5 * jnp.ones((H, N), jnp.float32)) + 0.1 * jax.random.normal(k2, (H, N), dtype=jnp.float32)
        A_imag = jnp.broadcast_to(math.pi * jnp.arange(N, dtype=jnp.float32), (H, N)).copy()
        B_ri = jax.random.normal(k3, (H, N, 2), dtype=jnp.float32) * 0.5
        C_ri = jax.random.normal(k4, (CH, H, N, 2), dtype=jnp.float32) * 0.5
        return {'log_dt': log_dt, 'inv_A_real': inv_A_real, 'A_imag': A_imag, 'B_ri': B_ri, 'C_ri': C_ri, 'L': SEQ_L}
    _L0_tok_all = _L0_tok_setup()
    _L0_tok_in = {k: v for k, v in _L0_tok_all.items() if k in ('log_dt', 'inv_A_real', 'A_imag', 'B_ri')}
    del _L0_tok_all

    def _L0_attn_setup():
        import jax, jax.numpy as jnp
        import numpy as np
        B, T, D, H = (2, 512, 256, 16)
        HD = D // H
        REG = 16
        WIN = 64
        ROPE_BASE = 10000.0

        def _rope_cos_sin(t, hd):
            theta = 1.0 / ROPE_BASE ** (jnp.arange(0, hd, 2, dtype=jnp.float32) / hd)
            idx_theta = jnp.arange(t, dtype=jnp.float32)[:, None] * theta[None, :]
            return (jnp.cos(idx_theta), jnp.sin(idx_theta))

        def _apply_rope(x, cos, sin):
            xs = x.reshape(*x.shape[:-1], HD // 2, 2)
            x0, x1 = (xs[..., 0], xs[..., 1])
            c = cos[None, :, None, :]
            s = sin[None, :, None, :]
            out = jnp.stack([x0 * c - x1 * s, x1 * c + x0 * s], axis=-1)
            return out.reshape(x.shape)

        def _keep_mask(t):
            i = jnp.arange(t)[:, None]
            j = jnp.arange(t)[None, :]
            half = WIN // 2
            window_block = (i >= REG) & (j >= jnp.maximum(REG, i - half)) & (j <= i + half)
            blocked = (j < REG) | (i < REG) | window_block
            return ~blocked
        key = jax.random.key(seed)
        k1, k2, k3 = jax.random.split(key, 3)
        x = jax.random.normal(k1, (B, T, D), dtype=jnp.float32)
        w_attn = jax.random.normal(k2, (3 * D, D), dtype=jnp.float32) * 0.02
        w_proj = jax.random.normal(k3, (D, D), dtype=jnp.float32) * 0.02
        return {'x': x, 'w_attn': w_attn, 'w_proj': w_proj}
    _L0_attn_all = _L0_attn_setup()
    _L0_attn_in = {k: v for k, v in _L0_attn_all.items() if k in ('w_attn', 'w_proj')}
    del _L0_attn_all

    def _L0_ffn_setup():
        import jax, jax.numpy as jnp
        import numpy as np
        B, S, D, F, E, NS, K = (2, 256, 256, 1024, 8, 8, 2)
        FS = F // NS
        key = jax.random.key(seed)
        ks = jax.random.split(key, 8)
        scale = 0.02
        return {'hidden_states': jax.random.normal(ks[0], (B, S, D), jnp.float32), 'gate_W': jax.random.normal(ks[1], (E, D), jnp.float32) * scale, 'w1_e': jax.random.normal(ks[2], (E, D, F), jnp.float32) * scale, 'w3_e': jax.random.normal(ks[3], (E, D, F), jnp.float32) * scale, 'w2_e': jax.random.normal(ks[4], (E, F, D), jnp.float32) * scale, 'w1_s': jax.random.normal(ks[5], (NS, D, FS), jnp.float32) * scale, 'w3_s': jax.random.normal(ks[6], (NS, D, FS), jnp.float32) * scale, 'w2_s': jax.random.normal(ks[7], (NS, FS, D), jnp.float32) * scale}
    _L0_ffn_all = _L0_ffn_setup()
    _L0_ffn_in = {k: v for k, v in _L0_ffn_all.items() if k in ('gate_W', 'w1_e', 'w3_e', 'w2_e', 'w1_s', 'w3_s', 'w2_s')}
    del _L0_ffn_all

    def _L1_attn_setup():
        import jax, jax.numpy as jnp
        import numpy as np
        INDIM = 256
        NHEADS = 16
        DK = INDIM // NHEADS
        DV = INDIM // NHEADS
        B, S = (4, 512)
        key = jax.random.key(seed)
        ks = jax.random.split(key, 5)
        x = jax.random.normal(ks[0], (B, S, INDIM), dtype=jnp.float32)
        std_qk = np.sqrt(2.0 / (INDIM + DK)).astype(np.float32)
        std_v = np.sqrt(2.0 / (INDIM + DV)).astype(np.float32)
        Wq = jax.random.normal(ks[1], (NHEADS * DK, INDIM), dtype=jnp.float32) * std_qk
        Wk = jax.random.normal(ks[2], (NHEADS * DK, INDIM), dtype=jnp.float32) * std_qk
        Wv = jax.random.normal(ks[3], (NHEADS * DV, INDIM), dtype=jnp.float32) * std_v
        std_o = np.sqrt(2.0 / (NHEADS * DV + INDIM)).astype(np.float32)
        Wo = jax.random.normal(ks[4], (INDIM, NHEADS * DV), dtype=jnp.float32) * std_o
        bq = jnp.zeros((NHEADS * DK,), jnp.float32)
        bk = jnp.zeros((NHEADS * DK,), jnp.float32)
        bv = jnp.zeros((NHEADS * DV,), jnp.float32)
        bo = jnp.zeros((INDIM,), jnp.float32)
        return {'x': x, 'Wq': Wq, 'bq': bq, 'Wk': Wk, 'bk': bk, 'Wv': Wv, 'bv': bv, 'Wo': Wo, 'bo': bo}
    _L1_attn_all = _L1_attn_setup()
    _L1_attn_in = {k: v for k, v in _L1_attn_all.items() if k in ('Wq', 'bq', 'Wk', 'bk', 'Wv', 'bv', 'Wo', 'bo')}
    del _L1_attn_all

    def _L1_ffn_setup():
        import jax, jax.numpy as jnp
        import numpy as np
        D = 256
        H = 512
        E = 8
        TOP_K = 2
        N_SHARED = 1
        B, S = (2, 256)
        key = jax.random.key(seed)
        ks = jax.random.split(key, 12)
        sc = 0.02
        return {'hidden': jax.random.normal(ks[0], (B, S, D), jnp.float32), 'router_w': jax.random.normal(ks[1], (D, E), jnp.float32) * sc, 'router_b': jnp.zeros((E,), jnp.float32), 'sw1': jax.random.normal(ks[2], (D, H), jnp.float32) * sc, 'sb1': jnp.zeros((H,), jnp.float32), 'sw2': jax.random.normal(ks[3], (H, D), jnp.float32) * sc, 'sb2': jnp.zeros((D,), jnp.float32), 'rw1': jax.random.normal(ks[4], (E, D, H), jnp.float32) * sc, 'rb1': jnp.zeros((E, H), jnp.float32), 'rw2': jax.random.normal(ks[5], (E, H, D), jnp.float32) * sc, 'rb2': jnp.zeros((E, D), jnp.float32)}
    _L1_ffn_all = _L1_ffn_setup()
    _L1_ffn_in = {k: v for k, v in _L1_ffn_all.items() if k in ('router_w', 'router_b', 'sw1', 'sb1', 'sw2', 'sb2', 'rw1', 'rb1', 'rw2', 'rb2')}
    del _L1_ffn_all
    return {'x': x, 'cls_tok': cls_tok, 'L0_tok_log_dt': _L0_tok_in['log_dt'], 'L0_tok_inv_A_real': _L0_tok_in['inv_A_real'], 'L0_tok_A_imag': _L0_tok_in['A_imag'], 'L0_tok_B_ri': _L0_tok_in['B_ri'], 'L0_attn_w_attn': _L0_attn_in['w_attn'], 'L0_attn_w_proj': _L0_attn_in['w_proj'], 'L0_ffn_gate_W': _L0_ffn_in['gate_W'], 'L0_ffn_w1_e': _L0_ffn_in['w1_e'], 'L0_ffn_w3_e': _L0_ffn_in['w3_e'], 'L0_ffn_w2_e': _L0_ffn_in['w2_e'], 'L0_ffn_w1_s': _L0_ffn_in['w1_s'], 'L0_ffn_w3_s': _L0_ffn_in['w3_s'], 'L0_ffn_w2_s': _L0_ffn_in['w2_s'], 'L1_attn_Wq': _L1_attn_in['Wq'], 'L1_attn_bq': _L1_attn_in['bq'], 'L1_attn_Wk': _L1_attn_in['Wk'], 'L1_attn_bk': _L1_attn_in['bk'], 'L1_attn_Wv': _L1_attn_in['Wv'], 'L1_attn_bv': _L1_attn_in['bv'], 'L1_attn_Wo': _L1_attn_in['Wo'], 'L1_attn_bo': _L1_attn_in['bo'], 'L1_ffn_router_w': _L1_ffn_in['router_w'], 'L1_ffn_router_b': _L1_ffn_in['router_b'], 'L1_ffn_sw1': _L1_ffn_in['sw1'], 'L1_ffn_sb1': _L1_ffn_in['sb1'], 'L1_ffn_sw2': _L1_ffn_in['sw2'], 'L1_ffn_sb2': _L1_ffn_in['sb2'], 'L1_ffn_rw1': _L1_ffn_in['rw1'], 'L1_ffn_rb1': _L1_ffn_in['rb1'], 'L1_ffn_rw2': _L1_ffn_in['rw2'], 'L1_ffn_rb2': _L1_ffn_in['rb2']}

def reference(x, cls_tok, L0_tok_log_dt, L0_tok_inv_A_real, L0_tok_A_imag, L0_tok_B_ri, L0_attn_w_attn, L0_attn_w_proj, L0_ffn_gate_W, L0_ffn_w1_e, L0_ffn_w3_e, L0_ffn_w2_e, L0_ffn_w1_s, L0_ffn_w3_s, L0_ffn_w2_s, L1_attn_Wq, L1_attn_bq, L1_attn_Wk, L1_attn_bk, L1_attn_Wv, L1_attn_bv, L1_attn_Wo, L1_attn_bo, L1_ffn_router_w, L1_ffn_router_b, L1_ffn_sw1, L1_ffn_sb1, L1_ffn_sw2, L1_ffn_sb2, L1_ffn_rw1, L1_ffn_rb1, L1_ffn_rw2, L1_ffn_rb2):
    import jax
    import jax.numpy as jnp

    def _L0_tok_ref(log_dt, inv_A_real, A_imag, B_ri, C_ri, L):
        import jax, jax.numpy as jnp
        import numpy as np
        import math
        H = 256
        N = 64
        CH = 1
        SEQ_L = 256
        dt = jnp.exp(log_dt)
        A = -jnp.exp(inv_A_real) + 1j * A_imag
        B = B_ri[..., 0] + 1j * B_ri[..., 1]
        C = C_ri[..., 0] + 1j * C_ri[..., 1]
        dtA = A * dt[:, None]
        dA = (1.0 + dtA / 2) / (1.0 - dtA / 2)
        C_term = C * B[None]
        log_dA = jnp.log(dA)
        V = jnp.exp(log_dA[:, :, None] * jnp.arange(L))
        K = 2.0 * jnp.einsum('chn,hnl->chl', C_term, V).real
        return K.astype(jnp.float32)

    def _L0_attn_ref(x, w_attn, w_proj):
        import jax, jax.numpy as jnp
        import numpy as np
        B, T, D, H = (2, 512, 256, 16)
        HD = D // H
        REG = 16
        WIN = 64
        ROPE_BASE = 10000.0

        def _rope_cos_sin(t, hd):
            theta = 1.0 / ROPE_BASE ** (jnp.arange(0, hd, 2, dtype=jnp.float32) / hd)
            idx_theta = jnp.arange(t, dtype=jnp.float32)[:, None] * theta[None, :]
            return (jnp.cos(idx_theta), jnp.sin(idx_theta))

        def _apply_rope(x, cos, sin):
            xs = x.reshape(*x.shape[:-1], HD // 2, 2)
            x0, x1 = (xs[..., 0], xs[..., 1])
            c = cos[None, :, None, :]
            s = sin[None, :, None, :]
            out = jnp.stack([x0 * c - x1 * s, x1 * c + x0 * s], axis=-1)
            return out.reshape(x.shape)

        def _keep_mask(t):
            i = jnp.arange(t)[:, None]
            j = jnp.arange(t)[None, :]
            half = WIN // 2
            window_block = (i >= REG) & (j >= jnp.maximum(REG, i - half)) & (j <= i + half)
            blocked = (j < REG) | (i < REG) | window_block
            return ~blocked
        b, t, d = x.shape
        qkv = jnp.einsum('btd,ed->bte', x, w_attn)
        q, k, v = jnp.split(qkv, 3, axis=-1)
        q = q.reshape(b, t, H, HD)
        k = k.reshape(b, t, H, HD)
        v = v.reshape(b, t, H, HD)
        cos, sin = _rope_cos_sin(t, HD)
        q = _apply_rope(q, cos, sin)
        k = _apply_rope(k, cos, sin)
        q = q.transpose(0, 2, 1, 3)
        k = k.transpose(0, 2, 1, 3)
        v = v.transpose(0, 2, 1, 3)
        keep = _keep_mask(t)
        scores = jnp.einsum('bhqd,bhkd->bhqk', q, k) / jnp.sqrt(jnp.float32(HD))
        scores = jnp.where(keep[None, None], scores, -jnp.inf)
        m = jnp.max(scores, axis=-1, keepdims=True)
        m = jnp.where(jnp.isfinite(m), m, 0.0)
        e = jnp.exp(scores - m)
        s = jnp.sum(e, axis=-1, keepdims=True)
        probs = e / jnp.maximum(s, 1e-20)
        y = jnp.einsum('bhqk,bhkd->bhqd', probs, v)
        y = y.transpose(0, 2, 1, 3).reshape(b, t, d)
        return jnp.einsum('btd,ed->bte', y, w_proj)

    def _L0_ffn_ref(hidden_states, gate_W, w1_e, w3_e, w2_e, w1_s, w3_s, w2_s):
        import jax, jax.numpy as jnp
        import numpy as np
        B, S, D, F, E, NS, K = (2, 256, 256, 1024, 8, 8, 2)
        FS = F // NS
        b, s, d = hidden_states.shape
        e = gate_W.shape[0]
        flat = hidden_states.reshape(-1, d)
        T = flat.shape[0]
        logits = (flat @ gate_W.T).astype(jnp.float32)
        probs = jax.nn.softmax(logits, axis=-1)
        top_v, top_i = jax.lax.top_k(probs, K)
        gates = jnp.zeros((T, e), probs.dtype).at[jnp.arange(T)[:, None], top_i].set(top_v)
        g = jax.nn.silu(jnp.einsum('td,edf->etf', flat, w1_e))
        u = jnp.einsum('td,edf->etf', flat, w3_e)
        out_e = jnp.einsum('etf,efd->etd', g * u, w2_e)
        routed = jnp.einsum('te,etd->td', gates, out_e).reshape(b, s, d)
        gs = jax.nn.silu(jnp.einsum('bsd,ndf->nbsf', hidden_states, w1_s))
        us = jnp.einsum('bsd,ndf->nbsf', hidden_states, w3_s)
        shared = jnp.einsum('nbsf,nfd->bsd', gs * us, w2_s) / w1_s.shape[0]
        alpha = 0.5
        return alpha * shared + (1.0 - alpha) * routed

    def _L1_attn_ref(x, Wq, bq, Wk, bk, Wv, bv, Wo, bo):
        import jax, jax.numpy as jnp
        import numpy as np
        INDIM = 256
        NHEADS = 16
        DK = INDIM // NHEADS
        DV = INDIM // NHEADS
        B, S = (4, 512)
        b, s, _ = x.shape
        q = (x @ Wq.T + bq).reshape(b, s, NHEADS, DK)
        k = (x @ Wk.T + bk).reshape(b, s, NHEADS, DK)
        v = (x @ Wv.T + bv).reshape(b, s, NHEADS, DV)
        w = jnp.einsum('bshd,bzhd->bhsz', q, k)
        w = w / jnp.sqrt(jnp.float32(DV))
        w = jax.nn.softmax(w, axis=-1)
        vw = jnp.einsum('bhsz,bzhd->bshd', w, v)
        vw = vw.reshape(b, s, NHEADS * DV)
        out = vw @ Wo.T + bo
        return out

    def _L1_ffn_ref(hidden, router_w, router_b, sw1, sb1, sw2, sb2, rw1, rb1, rw2, rb2):
        import jax, jax.numpy as jnp
        import numpy as np
        D = 256
        H = 512
        E = 8
        TOP_K = 2
        N_SHARED = 1
        B, S = (2, 256)
        b, s, d = hidden.shape
        T = b * s
        flat = hidden.reshape(T, d)
        router_logits = flat @ router_w + router_b
        router_probs = jax.nn.softmax(router_logits, axis=-1)
        topk_probs, topk_idx = jax.lax.top_k(router_probs, TOP_K)
        weights = jnp.zeros_like(router_probs).at[jnp.arange(T)[:, None], topk_idx].add(topk_probs)
        sh = jax.nn.gelu(flat @ sw1 + sb1, approximate=False)
        shared_out = (sh @ sw2 + sb2) / N_SHARED
        h1 = jax.nn.gelu(jnp.einsum('td,edh->teh', flat, rw1) + rb1[None], approximate=False)
        expert_out = jnp.einsum('teh,ehd->ted', h1, rw2) + rb2[None]
        mixed = jnp.einsum('ted,te->td', expert_out, weights)
        return (shared_out + mixed).reshape(b, s, d)
    h = _L0_tok_ref(L0_tok_log_dt, L0_tok_inv_A_real, L0_tok_A_imag, L0_tok_B_ri, x, 256)
    h = jnp.concatenate([jnp.broadcast_to(cls_tok, (h.shape[0], 1, h.shape[2])), h], axis=1)
    h = h + _L0_attn_ref(_layernorm(h, axis=-1), L0_attn_w_attn, L0_attn_w_proj)
    h = h + _L0_ffn_ref(_layernorm(h, axis=-1), L0_ffn_gate_W, L0_ffn_w1_e, L0_ffn_w3_e, L0_ffn_w2_e, L0_ffn_w1_s, L0_ffn_w3_s, L0_ffn_w2_s)
    h = h + _L1_attn_ref(_layernorm(h, axis=-1), L1_attn_Wq, L1_attn_bq, L1_attn_Wk, L1_attn_bk, L1_attn_Wv, L1_attn_bv, L1_attn_Wo, L1_attn_bo)
    h = h + _L1_ffn_ref(_layernorm(h, axis=-1), L1_ffn_router_w, L1_ffn_router_b, L1_ffn_sw1, L1_ffn_sb1, L1_ffn_sw2, L1_ffn_sb2, L1_ffn_rw1, L1_ffn_rb1, L1_ffn_rw2, L1_ffn_rb2)
    return h

_drawn_inputs = setup_inputs


def setup_inputs(seed=0):
    import zlib

    import numpy as np

    out = dict(_drawn_inputs(seed))
    spreads = {'L1_attn_bq': (0.0, 0.8),
     'L1_attn_bk': (0.0, 2.0),
     'L1_attn_bv': (0.0, 0.345),
     'L1_attn_bo': (0.0, 0.353),
     'L1_ffn_router_b': (0.0, 0.8),
     'L1_ffn_sb1': (0.0, 0.8),
     'L1_ffn_sb2': (0.0, 0.963),
     'L1_ffn_rb1': (0.0, 0.8),
     'L1_ffn_rb2': (0.0, 0.8)}
    factors = {'cls_tok': 7.68,
     'L0_attn_w_attn': 8.0,
     'L0_attn_w_proj': 8.0,
     'L0_ffn_gate_W': 8.0,
     'L0_ffn_w1_e': 8.0,
     'L0_ffn_w3_e': 8.0,
     'L0_ffn_w2_e': 8.0,
     'L0_ffn_w1_s': 8.0,
     'L0_ffn_w3_s': 8.0,
     'L0_ffn_w2_s': 8.0,
     'L1_ffn_router_w': 8.0,
     'L1_ffn_sw1': 3.186,
     'L1_ffn_sw2': 2.997,
     'L1_ffn_rw1': 8.0,
     'L1_ffn_rw2': 8.0}
    for name, (base, spread) in spreads.items():
        noise = np.random.default_rng([zlib.crc32(name.encode()), seed]).standard_normal(out[name].shape)
        drawn = base * np.exp(spread * noise) if base else spread * noise
        out[name] = jnp.asarray(drawn.astype(out[name].dtype))
    for name, factor in factors.items():
        out[name] = (out[name] * factor).astype(out[name].dtype)
    return out
```

```python
from contextlib import ExitStack

import numpy as np
import concourse.bass as bass
from concourse import mybir

F32 = mybir.dt.float32
F32R = mybir.dt.float32r
BF16 = mybir.dt.bfloat16
ACT = mybir.ActivationFunctionType
ALU = mybir.AluOpType
AX = mybir.AxisListType.X

P = 128
NB, T, D = 8, 257, 256
DT = D // P
TOK = NB * T
CH = 412
NCH = 5
COLS = CH * NCH
HEADS, HD = 16, 16
QT = 2
GRP = 4
BAND_REG, BAND_HALF = 16, 32
E = 8
S4_HP = 16
S4_NB = P // S4_HP
S4_DVE = 11
EPS = 1e-5


def constant_layout():
    widths = [("mean", P), ("ident", P), ("maskq", QT * 256), ("cq", 256), ("sq", 256), ("ck", 256),
              ("sk", 256), ("headmask", 8), ("spread", 4 * P), ("diag", 16), ("clspick", 4 * 16),
              ("clsheads", 2 * 16), ("tri", 64), ("eps", 1), ("valid", QT)]
    at, out = 0, {}
    for name, w in widths:
        out[name] = (at, at + w)
        at += w
    return out, at


def constants():
    where, width = constant_layout()
    c = np.zeros((P, width), np.float32)

    def put(name, value):
        a, b = where[name]
        c[:, a:b] = np.asarray(value, np.float32).reshape(P, b - a)

    p = np.arange(P)
    put("mean", np.full((P, P), 1.0 / D))
    put("ident", np.eye(P))
    t = np.arange(1, 257)
    q = (p[:, None] + P * np.arange(QT)[None, :] + 1)[:, :, None]
    j = t[None, None, :]
    near = (q >= BAND_REG) & (j >= np.maximum(BAND_REG, q - BAND_HALF)) & (j <= q + BAND_HALF)
    put("maskq", np.where((j < BAND_REG) | (q < BAND_REG) | near, -1e30, 0.0))
    theta = (np.float32(1.0) / np.float32(10000.0) ** (np.arange(0, HD, 2, dtype=np.float32) / np.float32(HD)))
    ang = (t.astype(np.float32)[None, :] * theta[(p % HD) // 2][:, None]).astype(np.float32)
    cos = np.cos(ang)
    sin = np.where((p % 2 == 0)[:, None], -np.sin(ang), np.sin(ang))
    put("ck", cos)
    put("sk", sin)
    put("cq", cos * np.float32(0.25))
    put("sq", sin * np.float32(0.25))
    put("headmask", p[:, None] // HD == np.arange(8)[None, :])
    g, m = np.arange(4)[None, :, None], np.arange(P)[None, None, :]
    put("spread", p[:, None, None] == GRP * g + m // 32)
    put("diag", p[:, None] == np.arange(16)[None, :])
    put("clspick", np.arange(16)[None, None, :] == GRP * np.arange(4)[None, :, None] + p[:, None, None] // 32)
    put("clsheads", np.arange(16)[None, None, :] == 8 * np.arange(2)[None, :, None] + p[:, None, None] // HD)
    put("tri", np.broadcast_to(np.arange(E)[None, :] < np.arange(E)[:, None], (P, E, E)))
    put("eps", np.full(P, EPS))
    put("valid", (q[:, :, 0] >= BAND_REG))
    return c


class Own:

    def __init__(self, eng, sem, apart=None):
        self.eng, self.sem, self.base, self.n, self.apart = eng, sem, 0, 0, apart

    def did(self, ins):
        ins.then_inc(self.sem, 1)
        self.n += 1
        return ins

    def wait(self):
        self.eng.wait_ge(self.sem, self.base + self.n)
        if self.apart:
            self.eng.nop().then_inc(self.apart, 1)

    def enter(self, i, per):
        self.outer, self.per, self.start = self.base, per, self.n
        self.base, self.n = self.outer + self.start + i * per, 0

    def leave(self, passes):
        assert self.n == self.per, (self.sem, self.n, self.per)
        self.base, self.n = self.outer, self.start + passes * self.per


class Tower:
    def __init__(self, nc, A, out, stop=99):
        self.nc, self.A, self.out, self.stop = nc, A, out, stop
        self.engines = {}

    def sem(self, name):
        return self.top.enter_context(self.nc.semaphore(name))

    def sb(self, scope, name, shape, dt=F32):
        return scope.enter_context(self.nc.sbuf_tensor(name, shape, dt))

    def const(self, name, *dims):
        a, b = constant_layout()[0][name]
        return self.cst[:, a:b]

    def build(self):
        nc = self.nc
        with ExitStack() as self.top:
            sb, top = self.sb, self.top
            self.xT = sb(top, "xT", [P, DT, COLS])
            self.cst = sb(top, "cst", [P, constant_layout()[1]])
            self.psS = top.enter_context(nc.psum_tensor("psS", [P, 4, 512], F32))
            self.psT = top.enter_context(nc.psum_tensor("psT", [P, 2, 512], F32))
            self.psY = top.enter_context(nc.psum_tensor("psY", [P, 2, 512], F32))
            self.gates_dram = nc.dram_tensor("gates_dram", [2, E + 1, COLS], F32, kind="Internal").ap()
            with ExitStack() as s4:
                self.memory_s4(s4)
            with ExitStack() as a:
                self.memory_attention(a)
            with ExitStack() as f:
                self.memory_weights(f)
                self.memory_ffn(f)
                self.memory_ln_out(f)
            self.stage_done = self.sem("stage_done")
            self.loaded = self.sem("loaded")
            self.paced = self.sem("paced")
            self.program()

    def memory_s4(self, s):
        sb = self.sb
        self.s4_small = sb(s, "s4_small", [P, 5, P])
        self.s4_c = sb(s, "s4_c", [P, 2, NB, P])
        self.s4_w = sb(s, "s4_w", [P, 8, 2, P])
        self.s4_tmp = sb(s, "s4_tmp", [P, 8, P])
        self.s4_cb = sb(s, "s4_cb", [P, 2, 2, NB, P])
        self.s4_prod = sb(s, "s4_prod", [P, 2, NB, P])
        self.s4_p = sb(s, "s4_p", [P, 2, P, 2, 2, NB])
        self.s4_v = sb(s, "s4_v", [P, 2, 2, S4_HP, P])
        self.s4_t = sb(s, "s4_t", [P, 2, S4_HP, 64])

    def memory_weights(self, s):
        sb = self.sb
        self.w_stage = sb(s, "w_stage", [P, 2, 3072])
        self.w_hi = sb(s, "w_hi", [P, 2, 3072], F32R)
        self.w_lo = sb(s, "w_lo", [P, 2, 3072], F32R)
        self.w_bias = sb(s, "w_bias", [P, 2, 6])
        self.r_w = sb(s, "r_w", [P, DT * E])
        self.r_hl = sb(s, "r_hl", [P, 2, DT * E], F32R)
        self.r_b = sb(s, "r_b", [P, E])

    def memory_attention(self, s):
        sb = self.sb
        self.xn = sb(s, "xn", [P, DT, COLS])
        self.ln_tmpA = sb(s, "ln_tmpA", [P, 2, DT, CH])
        self.ln_sqA = sb(s, "ln_sqA", [P, 2, DT, CH])
        self.ln_sdA = sb(s, "ln_sdA", [P, 2, 2, CH])
        self.a_w = sb(s, "a_w", [P, DT, 1280])
        self.a_wo = sb(s, "a_wo", [P, 4, D])
        self.a_b = sb(s, "a_b", [P, 6])
        self.a_bv = sb(s, "a_bv", [P, D])
        self.a_x = sb(s, "a_x", [P, DT, T])
        self.a_xc = sb(s, "a_xc", [P, DT, 16])
        self.a_rope = sb(s, "a_rope", [P, 2, 2, 256])
        self.a_q = sb(s, "a_q", [P, DT, T])
        self.a_qm = sb(s, "a_qm", [P, HEADS, 256])
        self.a_qc = sb(s, "a_qc", [P, DT, 16])
        self.a_k = sb(s, "a_k", [P, DT, T])
        self.a_v = sb(s, "a_v", [P, QT, HEADS * 32])
        self.a_vt = sb(s, "a_vt", [16, D])
        self.a_vc = sb(s, "a_vc", [P, HEADS * 32])
        self.a_p = sb(s, "a_p", [P, 2, QT, T])
        self.a_pt = sb(s, "a_pt", [P, 8, 512])
        self.a_nm = sb(s, "a_nm", [P, HEADS + 1, QT])
        self.a_sum = sb(s, "a_sum", [P, QT, HEADS])
        self.a_rs = sb(s, "a_rs", [P, QT, HEADS])
        self.a_rsc = sb(s, "a_rsc", [16, 2])
        self.a_pex = sb(s, "a_pex", [P, QT, HEADS])
        self.a_pc = sb(s, "a_pc", [16, T])
        self.a_pct = sb(s, "a_pct", [P, QT, 16])
        self.a_rst = sb(s, "a_rst", [P, T])
        self.a_pext = sb(s, "a_pext", [P, T])
        self.a_yc = sb(s, "a_yc", [P, 4, 16])
        self.a_y = sb(s, "a_y", [P, 4, T])
        self.a_yn = sb(s, "a_yn", [P, 4, T])
        self.a_maskb = sb(s, "a_maskb", [P, QT, 256], BF16)
        self.a_identb = sb(s, "a_identb", [P, P], BF16)

    def memory_ffn(self, s):
        sb = self.sb
        self.x_hl = sb(s, "x_hl", [P, 2, DT, COLS], F32R)
        self.gate = sb(s, "gate", [P, 2, COLS])
        self.f_act = sb(s, "f_act", [P, 2, CH])
        self.f_h = sb(s, "f_h", [P, 2, CH])
        self.f_hl = sb(s, "f_hl", [P, 2, 2, CH], F32R)
        self.f_t = sb(s, "f_t", [P, DT, CH])
        self.ln_tmpF = sb(s, "ln_tmpF", [P, 2, DT, CH])
        self.ln_sqF = sb(s, "ln_sqF", [P, 2, DT, CH])
        self.ln_sdF = sb(s, "ln_sdF", [P, 2, 2, CH])

    def memory_ln_out(self, s):
        sb = self.sb
        n = 17
        self.g_p = sb(s, "g_p", [P, n, E])
        self.g_cmp = sb(s, "g_cmp", [P, 2, n, E, E])
        self.g_m = sb(s, "g_m", [P, 4, n])
        self.g_sel = sb(s, "g_sel", [P, n, E])
        self.g_all = sb(s, "g_all", [P, n, E + 1])
        self.g_t = sb(s, "g_t", [E + 1, COLS])
        self.o_rows = sb(s, "o_rows", [P, 4, D])

    def program(self):
        stages = [self.load_constants, self.s4_tokens]
        for layer in range(2):
            stages += [lambda layer=layer: self.layernorm(f"a{layer}", True),
                       lambda layer=layer: self.attention(layer),
                       lambda layer=layer: self.layernorm(f"f{layer}", False),
                       lambda layer=layer: self.router(layer),
                       lambda layer=layer: self.experts(layer)]
        stages = stages[:self.stop]
        stages.append(self.write_out)
        parts = [s() for s in stages]
        nc = self.nc

        def run(eng, name):
            for n, part in enumerate(parts):
                if name in part:
                    part[name](eng)
                if n < len(parts) - 1:
                    eng.drain().then_inc(self.stage_done, 1)
                    eng.wait_ge(self.stage_done, 5 * (n + 1))

        with nc.Block() as block:
            @block.sync
            def _(sp):
                run(sp, "sp")

            @block.gpsimd
            def _(pool):
                run(pool, "pool")

            @block.scalar
            def _(act):
                run(act, "act")

            @block.vector
            def _(dve):
                run(dve, "dve")

            @block.tensor
            def _(pe):
                run(pe, "pe")

    def load_constants(self):
        A, xT = self.A, self.xT
        filled = self.sem("cls_loaded")
        padded = self.sem("padded")

        def sp(e):
            e.dma_start(self.cst[:], A["consts"]).then_inc(self.loaded, 16)
            e.dma_start(self.s4_small[:], A["s4_small"]).then_inc(self.loaded, 16)
            e.dma_start(self.s4_c[:], A["s4_c"]).then_inc(self.loaded, 16)
            e.dma_start(self.s4_tmp[:, 0, 0:DT], A["cls"]).then_inc(filled, 16)
            e.wait_ge(self.loaded, 48)

        def pool(e):
            e.memset(xT[:, :, TOK:COLS], 0.0).then_inc(padded, 1)
            e.wait_ge(filled, 16)
            for dt in range(DT):
                e.tensor_copy(xT[:, dt, 0:TOK].rearrange("p (b t) -> p b t", t=T)[:, :, 0:1],
                              self.s4_tmp[:, 0, dt:dt + 1].unsqueeze(1).to_broadcast([P, NB, 1])).then_inc(padded, 1)
            e.wait_ge(padded, 3)
        return {"sp": sp, "pool": pool}

    def s4_tokens(self):
        small, c, w, tmp, cb, prod = self.s4_small, self.s4_c, self.s4_w, self.s4_tmp, self.s4_cb, self.s4_prod
        pw, v, t, xT, psS = self.s4_p, self.s4_v, self.s4_t, self.xT, self.psS
        own_dve, own_pool = self.sem("s4_own_dve"), self.sem("s4_own_pool")
        w_ready, zeroed = self.sem("s4_w_ready"), self.sem("s4_zeroed")
        p_ready = self.sem("s4_p_ready")
        v_dve, v_pool = self.sem("s4_v_dve"), self.sem("s4_v_pool")
        k_ready, k_moved = self.sem("s4_k_ready"), self.sem("s4_k_moved")
        CREDIT = 2

        def act(e):
            for _ in range(CREDIT):
                e.nop().then_inc(k_moved, 1)
            with e.Fori(0, S4_NB // 2) as i:
                for s in range(2):
                    blk = i * 2 + s
                    e.wait_ge(k_ready, blk + 1 + CREDIT)
                    for a in range(2):
                        dst = xT[:, a, 0:TOK].rearrange("p (c t) -> p c t", t=T)[:, :, 1:T]
                        dst = dst.rearrange("p c (g h) -> p c g h", g=2)[:, :, :, bass.ds(blk * S4_HP, S4_HP)]
                        src = psS[:, s, :].rearrange("p (h g a c) -> p a c g h", g=2, a=2, c=NB)[:, a]
                        last = e.activation(dst, src, ACT.Copy)
                    last.then_inc(k_moved, 1)

        def powers(e, own, first, count, slot, blk):
            a, z = first, first + count

            def wk(k, ri, width):
                return w[:, k, ri, bass.ds(blk * S4_HP + first, count)].unsqueeze(2).to_broadcast([P, count, width])

            own.did(e.tensor_copy(v[:, slot, 0, a:z, 1:2], wk(0, 0, 1)))
            own.did(e.tensor_copy(v[:, slot, 1, a:z, 1:2], wk(0, 1, 1)))
            for k in range(1, 7):
                n = 1 << k
                own.wait()
                re, im = v[:, slot, 0, a:z, 0:n], v[:, slot, 1, a:z, 0:n]
                own.did(e.tensor_tensor(t[:, 0, a:z, 0:n], re, wk(k, 0, n), ALU.mult))
                own.did(e.tensor_tensor(t[:, 1, a:z, 0:n], im, wk(k, 1, n), ALU.mult))
                own.wait()
                own.did(e.tensor_tensor(v[:, slot, 0, a:z, n:2 * n], t[:, 0, a:z, 0:n], t[:, 1, a:z, 0:n], ALU.subtract))
                own.wait()
                own.did(e.tensor_tensor(t[:, 0, a:z, 0:n], re, wk(k, 1, n), ALU.mult))
                own.did(e.tensor_tensor(t[:, 1, a:z, 0:n], im, wk(k, 0, n), ALU.mult))
                own.wait()
                last = e.tensor_tensor(v[:, slot, 1, a:z, n:2 * n], t[:, 0, a:z, 0:n], t[:, 1, a:z, 0:n], ALU.add)
                if k < 6:
                    own.did(last)
            return last

        PER = 2 + 6 * 6 - 1

        def dve(e):
            own = Own(e, own_dve)

            def tt(out, a, b, op):
                own.did(e.tensor_tensor(out, a, b, op))

            def exponential():
                x = small[:, 2:5:2]
                k, r, q, two = (prod[:, 0, 2 * n:2 * n + 2] for n in range(4))
                ROUND = 1.5 * 2.0 ** 23
                LN2_HI, LN2_LO = 355.0 / 512.0, -2.12194440054690583e-4

                def step(ins):
                    own.did(ins)
                    own.wait()
                step(e.tensor_scalar(k, x, 1.0 / float(np.log(2.0)), ROUND, ALU.mult, ALU.add))
                step(e.tensor_scalar(k, k, -ROUND, -126.0, ALU.add, ALU.max))
                step(e.tensor_scalar(k, k, 127.0, None, ALU.min))
                step(e.scalar_tensor_tensor(r, k, -LN2_HI, x, ALU.mult, ALU.add))
                step(e.scalar_tensor_tensor(r, k, -LN2_LO, r, ALU.mult, ALU.add))
                fact = [1.0]
                for n in range(1, 9):
                    fact.append(fact[-1] * n)
                step(e.tensor_scalar(q, r, 1.0 / fact[8], None, ALU.mult))
                for n in range(7, 0, -1):
                    step(e.scalar_tensor_tensor(q, q, 1.0 / fact[n], r, ALU.add, ALU.mult))
                step(e.tensor_scalar(two.bitcast(mybir.dt.int32), k, 127.0, 2.0 ** 23, ALU.add, ALU.mult))
                step(e.scalar_tensor_tensor(x, q, 1.0, two, ALU.add, ALU.mult))

            exponential()
            bre, bim, ar, ai, dt = (small[:, n] for n in range(5))
            zr, zi, zr2, zi2, mag, num, omz, den = (tmp[:, n] for n in range(8))
            own.did(e.scalar_tensor_tensor(zr, ar, -0.5, dt, ALU.mult, ALU.mult))
            own.did(e.scalar_tensor_tensor(zi, ai, 0.5, dt, ALU.mult, ALU.mult))
            own.wait()
            tt(zr2, zr, zr, ALU.mult)
            tt(zi2, zi, zi, ALU.mult)
            own.did(e.tensor_scalar(omz, zr, -1.0, 1.0, ALU.mult, ALU.add))
            own.wait()
            tt(mag, zr2, zi2, ALU.add)
            tt(den, omz, omz, ALU.mult)
            own.wait()
            own.did(e.tensor_scalar(num, mag, -1.0, 1.0, ALU.mult, ALU.add))
            tt(den, den, zi2, ALU.add)
            own.wait()
            own.did(e.reciprocal(omz, den))
            own.wait()
            tt(w[:, 0, 0], num, omz, ALU.mult)
            own.did(e.scalar_tensor_tensor(w[:, 0, 1], zi, 2.0, omz, ALU.mult, ALU.mult))
            own.wait()
            for k in range(1, 8):
                r, i = w[:, k - 1, 0], w[:, k - 1, 1]
                tt(zr2, r, r, ALU.mult)
                tt(zi2, i, i, ALU.mult)
                own.did(e.scalar_tensor_tensor(w[:, k, 1], r, 2.0, i, ALU.mult, ALU.mult))
                own.wait()
                if k < 7:
                    tt(w[:, k, 0], zr2, zi2, ALU.subtract)
                    own.wait()
            e.tensor_tensor(w[:, 7, 0], zr2, zi2, ALU.subtract).then_inc(w_ready, 1)
            e.wait_ge(w_ready, 1)

            def cmul(out_re, out_im, xr, xi, yr, yi):
                for out, (a1, b1), (a2, b2), op in ((out_re, (xr, yr), (xi, yi), ALU.subtract),
                                                    (out_im, (xr, yi), (xi, yr), ALU.add)):
                    tt(prod[:, 0], a1, b1, ALU.mult)
                    tt(prod[:, 1], a2, b2, ALU.mult)
                    own.wait()
                    tt(out, prod[:, 0], prod[:, 1], op)
                    own.wait()

            def wide(x):
                return x.unsqueeze(1).to_broadcast([P, NB, P])
            cmul(cb[:, 0, 0], cb[:, 0, 1], c[:, 0], c[:, 1], wide(bre), wide(bim))
            cmul(cb[:, 1, 0], cb[:, 1, 1], cb[:, 0, 0], cb[:, 0, 1], wide(w[:, 7, 0]), wide(w[:, 7, 1]))
            e.wait_ge(zeroed, 4)
            for a in range(2):
                for ri, scale in ((0, 2.0), (1, -2.0)):
                    for h in range(2):
                        q = slice(64 * h, 64 * h + 64)
                        last = e.tensor_scalar(pw[q, ri, :, h, a, :].rearrange("p h c -> p c h"), cb[q, a, ri], scale, None, ALU.mult)
            last.then_inc(p_ready, 1)
            with e.Fori(0, S4_NB // 2) as i:
                own.enter(i, 2 * PER)
                for s in range(2):
                    blk = i * 2 + s
                    e.wait_ge(k_ready, blk - 1 + CREDIT)
                    powers(e, own, 0, S4_DVE, s, blk).then_inc(v_dve, 1)
                own.leave(S4_NB // 2)

        def pool(e):
            own = Own(e, own_pool, apart=self.paced)
            e.memset(pw[:, 0], 0.0).then_inc(zeroed, 1)
            e.memset(pw[:, 1], 0.0).then_inc(zeroed, 1)
            e.memset(v[:, :, 0, :, 0:1], 1.0).then_inc(zeroed, 1)
            e.memset(v[:, :, 1, :, 0:1], 0.0).then_inc(zeroed, 1)
            e.wait_ge(zeroed, 4)
            e.wait_ge(w_ready, 1)
            with e.Fori(0, S4_NB // 2) as i:
                own.enter(i, 2 * PER)
                for s in range(2):
                    e.wait_ge(k_ready, i * 2 + s - 1 + CREDIT)
                    e.nop().then_inc(self.paced, 1)
                    powers(e, own, S4_DVE, S4_HP - S4_DVE, s, i * 2 + s).then_inc(v_pool, 1)
                own.leave(S4_NB // 2)

        def pe(e):
            for _ in range(CREDIT):
                e.nop().then_inc(k_ready, 1)
            e.wait_ge(p_ready, 1)
            with e.Fori(0, S4_NB // 2) as i:
                for s in range(2):
                    blk = i * 2 + s
                    e.wait_ge(v_dve, blk + 1)
                    e.wait_ge(v_pool, blk + 1)
                    e.wait_ge(k_moved, blk - 1 + CREDIT)
                    for h in range(S4_HP):
                        for ri in range(2):
                            rhs = pw[:, ri, bass.ds(blk * S4_HP + h, 1)].rearrange("p h g a c -> p (h g a c)")
                            last = e.matmul(psS[:, s, 32 * h:32 * h + 32], v[:, s, ri, h, :], rhs,
                                            start=(ri == 0), stop=(ri == 1))
                    last.then_inc(k_ready, 1)
        return {"act": act, "dve": dve, "pool": pool, "pe": pe}

    def layernorm(self, tag, for_attention):
        xT, psS = self.xT, self.psS
        tmp, sq, sd = ((self.ln_tmpA, self.ln_sqA, self.ln_sdA) if for_attention
                       else (self.ln_tmpF, self.ln_sqF, self.ln_sdF))
        mean = self.const("mean")
        mean_ready, centred, squared, var_ready, rooted, normed, own_sem, hi_ready = (
            self.sem(f"ln{tag}_{n}") for n in ("mean", "centred", "squared", "var", "rooted", "normed", "own", "hi"))

        def cols(c):
            return slice(c * CH, (c + 1) * CH)

        def both(x):
            return x.unsqueeze(1).to_broadcast([P, DT, CH])

        def pe(e):
            def means(c):
                if c >= 2:
                    e.wait_ge(centred, c - 1)
                for dt in range(DT):
                    m = e.matmul(psS[:, c % 2, 0:CH], mean, xT[:, dt, cols(c)], start=dt == 0, stop=dt == DT - 1)
                m.then_inc(mean_ready, 1)
            means(0)
            for c in range(NCH):
                if c + 1 < NCH:
                    means(c + 1)
                e.wait_ge(squared, c + 1)
                if c >= 2:
                    e.wait_ge(rooted, c - 1)
                for dt in range(DT):
                    m = e.matmul(psS[:, 2 + c % 2, 0:CH], mean, sq[:, c % 2, dt], start=dt == 0, stop=dt == DT - 1)
                m.then_inc(var_ready, 1)

        def act(e):
            for c in range(NCH + 1):
                if c < NCH:
                    e.wait_ge(centred, c + 1)
                    if c >= 2:
                        e.wait_ge(var_ready, c - 1)
                    e.activation(sq[:, c % 2], tmp[:, c % 2], ACT.Square).then_inc(squared, 1)
                if c >= 1:
                    e.wait_ge(var_ready, c)
                    if c >= 3:
                        e.wait_ge(normed, c - 2)
                    e.activation(sd[:, (c - 1) % 2, 0], psS[:, 2 + (c - 1) % 2, 0:CH], ACT.Sqrt,
                                 bias=self.const("eps")).then_inc(rooted, 1)

        def dve(e):
            own = Own(e, own_sem)
            for c in range(NCH + 1):
                if c < NCH:
                    e.wait_ge(mean_ready, c + 1)
                    if c >= 2:
                        e.wait_ge(squared, c - 1)
                        e.wait_ge(normed, c - 1)
                    e.tensor_tensor(tmp[:, c % 2], xT[:, :, cols(c)], both(psS[:, c % 2, 0:CH]), ALU.subtract).then_inc(centred, 1)
                if c >= 1:
                    k = c - 1
                    e.wait_ge(rooted, c)
                    own.did(e.reciprocal(sd[:, k % 2, 1], sd[:, k % 2, 0]))
                    own.wait()
                    e.wait_ge(centred, c)
                    if for_attention:
                        e.tensor_tensor(self.xn[:, :, cols(k)], tmp[:, k % 2], both(sd[:, k % 2, 1]), ALU.mult).then_inc(normed, 1)
                    else:
                        own.did(e.tensor_tensor(tmp[:, k % 2], tmp[:, k % 2], both(sd[:, k % 2, 1]), ALU.mult))
                        own.wait()
                        own.did(e.tensor_copy(self.x_hl[:, 0, :, cols(k)], tmp[:, k % 2]))
                        own.wait()
                        e.tensor_tensor(self.x_hl[:, 1, :, cols(k)], tmp[:, k % 2],
                                        self.x_hl[:, 0, :, cols(k)].bitcast(F32), ALU.subtract).then_inc(normed, 1)
        return {"pe": pe, "act": act, "dve": dve}

    def attention(self, L):
        A, xT, psS, psT, psY = self.A, self.xT, self.psS, self.psT, self.psY
        full = L == 1
        NK = T if full else T - 1
        K0 = 0 if full else 1
        S = {}

        def sem(n):
            if n not in S:
                S[n] = self.sem(f"at{L}_{n}")
            return S[n]
        w, wo, bb, bv = self.a_w, self.a_wo, self.a_b, self.a_bv
        q, qm, qc, k, v, vc = self.a_q, self.a_qm, self.a_qc, self.a_k, self.a_v, self.a_vc
        prob, pt, nm = self.a_p, self.a_pt, self.a_nm
        NW = 768 if full else 1280
        w_ready, prep = sem("w_ready"), sem("prep")
        NPREP = 7 if full else 6
        BANKS = [psS[:, n, :] for n in range(4)] + [psT[:, n, :] for n in range(2)] + [psY[:, n, :] for n in range(2)]
        if full:
            units = [("q", t, 128 * t) for t in range(2)] + [("k", t, 256 + 128 * t) for t in range(2)]
            vcol = 512
        else:
            units = [(n, t, 256 * m + 128 * t) for t in range(2) for m, n in enumerate(("q", "qs"))]
            units += [(n, t, 512 + 256 * m + 128 * t) for t in range(2) for m, n in enumerate(("k", "ks"))]
            vcol = 1024
        units += [("v", t, vcol) for t in range(QT)] + ([("vc", 0, vcol)] if full else [])
        NU = len(units)
        NH = HEADS + (1 if full else 0)
        SUM_GUARD = 1e-20

        def sp(e):
            e.dma_start(w[:, :, 0:NW], A[f"w_qkv{L}"]).then_inc(w_ready, 16)
            e.dma_start(wo[:], A[f"w_o{L}"]).then_inc(w_ready, 16)
            if full:
                e.dma_start(bb[:], A["a_bias"]).then_inc(w_ready, 16)
                e.dma_start(bv[:], A["a_bv"]).then_inc(w_ready, 16)

        WR = 64 if full else 32

        def batch_end(e, b):
            e.drain().then_inc(sem("image_done"), 1)
            e.wait_ge(sem("image_done"), b * 4 + 4)

        def pool(e):
            own = Own(e, sem("own_pool"), apart=self.paced)
            e.wait_ge(w_ready, WR)
            for m in (v, vc, self.a_rst, self.a_pext):
                e.memset(m[:], 0.0).then_inc(prep, 1)
            with e.Fori(0, NB) as b:
                own.enter(b, 1)
                own.did(e.tensor_copy(self.a_x[:], self.xn[:, :, bass.ds(b * T, T)]))
                own.wait()
                e.tensor_copy(self.a_xc[:], self.a_x[:, :, 0:1].to_broadcast([P, DT, 16])).then_inc(sem("x_ready"), 1)
                if not full:
                    for n in range(4):
                        e.wait_ge(sem("moved"), b * NU + 2 * n + 2)
                        e.nop().then_inc(self.paced, 1)
                        dst = (q if n < 2 else k)[:, n % 2, 1:T]
                        e.tensor_tensor(dst, self.a_rope[:, n % 2, 0], self.a_rope[:, n % 2, 1], ALU.add).then_inc(sem("rope_add"), 1)
                else:
                    for u in range(HEADS):
                        e.wait_ge(sem("exp"), b * NH + u + 1)
                        e.nop().then_inc(self.paced, 1)
                        e.tensor_copy(self.a_pex[:, :, u:u + 1], prob[:, u % 2, :, 0:1]).then_inc(sem("pex"), 1)
                batch_end(e, b)
                own.leave(NB)

        def pe(e):
            e.wait_ge(w_ready, WR)
            e.wait_ge(prep, NPREP)
            ident = self.const("ident")
            with e.Fori(0, NB) as b:
                e.wait_ge(sem("x_ready"), b + 1)
                for n, (name, t, col) in enumerate(units):
                    if n >= 8:
                        e.wait_ge(sem("moved"), b * NU + n - 7)
                    for dt in range(DT):
                        st, sp_ = dt == 0, dt == DT - 1
                        if name == "v":
                            m = e.matmul(BANKS[n % 8][:, 0:D], self.a_x[:, dt, 1 + 128 * t:129 + 128 * t],
                                         w[:, dt, col:col + D], start=st, stop=sp_)
                        elif name == "vc":
                            m = e.matmul(BANKS[n % 8][0:16, 0:D], self.a_xc[:, dt], w[:, dt, col:col + D], start=st, stop=sp_)
                        else:
                            m = e.matmul(BANKS[n % 8][:, 0:NK], w[:, dt, col:col + P], self.a_x[:, dt, K0:T], start=st, stop=sp_)
                    m.then_inc(sem("proj"), 1)

                def scores(u):
                    s = u % 2
                    if u < HEADS:
                        e.wait_ge(sem("qm"), b * NH + u + 1)
                        if u < 2:
                            e.wait_ge(sem("moved"), b * NU + NU)
                            if not full:
                                e.wait_ge(sem("rope_add"), b * 4 + 4)
                        else:
                            e.wait_ge(sem("exp"), b * NH + u - 1)
                        for i in range(QT):
                            out = psS[:, 2 * s + i, 0:NK]
                            if not full:
                                e.matmul(out, self.a_identb[:], self.a_maskb[:, i], start=True, stop=False)
                            m = e.matmul(out, qm[:, u, 128 * i:128 * i + 128], k[:, u // 8, K0:T], start=full, stop=True)
                    else:
                        e.wait_ge(sem("qm"), b * NH + u + 1)
                        e.wait_ge(sem("exp"), b * NH + u - 1)
                        for t in range(2):
                            m = e.matmul(psS[0:16, 2 * s, 0:NK], qc[:, t], k[:, t, 0:T], start=t == 0, stop=t == 1)
                    m.then_inc(sem("scores"), 1)

                def turn(u):
                    s = u % 2
                    e.wait_ge(sem("exp"), b * NH + u + 1)
                    if u >= 2:
                        e.wait_ge(sem("pt"), b * NH + u - 1)
                    if u == HEADS:
                        e.nop().then_inc(self.paced, 1)
                    if u < HEADS:
                        for kt in range(2):
                            for i in range(QT):
                                at = kt * 256 + i * 128
                                m = e.transpose(psT[:, s, at:at + 128], prob[:, s, i, K0 * 0 + (NK - 256) + 128 * kt:(NK - 256) + 128 * kt + 128], ident)
                    else:
                        for kt in range(2):
                            m = e.transpose(psT[:, s, 16 * kt:16 * kt + 16], self.a_pc[:, 1 + 128 * kt:129 + 128 * kt], ident[0:16, 0:16])
                    m.then_inc(sem("turned"), 1)

                def values(g):
                    e.wait_ge(sem("pt"), b * NH + 4 * g + 4)
                    if g >= 2:
                        e.wait_ge(sem("y"), b * 4 + g - 1)
                    for kt in range(2):
                        for j in range(GRP):
                            h = GRP * g + j
                            m = e.matmul(psY[32 * j:32 * j + 32, g % 2, 0:256], v[:, kt, 32 * h:32 * h + 32],
                                         pt[:, h % 8, 256 * kt:256 * kt + 256], start=kt == 0, stop=kt == 1)
                    m.then_inc(sem("pv"), 1)

                for u in range(NH + 3):
                    if u < NH:
                        scores(u)
                    if 1 <= u <= NH:
                        turn(u - 1)
                    if u >= 5 and (u - 5) % 4 == 0 and (u - 5) // 4 < 4:
                        values((u - 5) // 4)
                e.wait_ge(sem("rs"), b + 1)
                e.wait_ge(sem("pt"), b * NH + NH)
                for i in range(QT):
                    m = e.transpose(psT[0:16, 0, 128 * i:128 * i + 128], self.a_rs[:, i, :], ident)
                if full:
                    e.wait_ge(sem("pex"), b * HEADS + HEADS)
                    for i in range(QT):
                        m = e.transpose(psT[0:16, 1, 128 * i:128 * i + 128], self.a_pex[:, i, :], ident)
                m.then_inc(sem("tailT"), 1)
                if full:
                    e.wait_ge(sem("y"), b * 4 + 4)
                    for g in range(4):
                        for kt in range(2):
                            m = e.matmul(psY[:, 0, 16 * g:16 * g + 16], v[:, kt, P * g:P * g + P], self.a_pct[:, kt], start=kt == 0, stop=kt == 1)
                    m.then_inc(sem("clsy"), 1)
                e.wait_ge(sem("tailC"), b + 1)
                e.wait_ge(sem("exp"), b * NH + NH)
                for g in range(4):
                    if g >= 2:
                        e.wait_ge(sem("yn"), b * 4 + g - 1)
                    m = e.matmul(psS[:, 2 + g % 2, 0:T], self.const("spread")[:, P * g:P * g + P], self.a_rst[:], start=True, stop=True)
                    if full:
                        m = e.matmul(psS[:, g % 2, 0:T], vc[:, P * g:P * g + P], self.a_pext[:], start=True, stop=True)
                    m.then_inc(sem("R"), 1)
                e.wait_ge(sem("yn"), b * 4 + 4)
                e.wait_ge(sem("y"), b * 4 + 4)
                for mt in range(DT):
                    for g in range(4):
                        m = e.matmul(psY[:, mt, 0:NK], wo[:, g, 128 * mt:128 * mt + 128], self.a_yn[:, g, K0:T], start=g == 0, stop=g == 3)
                m.then_inc(sem("out"), 1)
                batch_end(e, b)

        def act(e):
            with e.Fori(0, NB) as b:
                def y_out(g):
                    e.wait_ge(sem("pv"), b * 4 + g + 1)
                    e.activation(self.a_y[:, g, 1:T], psY[:, g % 2, 0:256], ACT.Copy).then_inc(sem("y"), 1)
                for u in range(NH):
                    s = u % 2
                    e.wait_ge(sem("max"), b * NH + u + 1)
                    if u >= 2:
                        e.wait_ge(sem("turned"), b * NH + u - 1)
                        if full:
                            e.wait_ge(sem("pex"), b * HEADS + min(u - 1, HEADS))
                    if u < HEADS:
                        for i in range(QT):
                            m = e.activation(prob[:, s, i, 0:NK], psS[:, 2 * s + i, 0:NK], ACT.Exp,
                                             bias=nm[:, u, i:i + 1], accum_out=self.a_sum[:, i, u:u + 1])
                    else:
                        m = e.activation(self.a_pc[:, 0:NK], psS[0:16, 2 * s, 0:NK], ACT.Exp,
                                         bias=nm[0:16, u, 0:1], accum_out=self.a_rsc[:, 0:1])
                    m.then_inc(sem("exp"), 1)
                    if u >= 6 and (u - 6) % 4 == 0 and u < 15:
                        y_out((u - 6) // 4)
                y_out(3) if True else None
                batch_end(e, b)

        def dve(e):
            own = Own(e, sem("own_dve"))
            e.tensor_copy(self.a_maskb[:], self.const("maskq").rearrange("p (i k) -> p i k", i=QT)).then_inc(prep, 1)
            e.tensor_copy(self.a_identb[:], self.const("ident")).then_inc(prep, 1)
            e.wait_ge(w_ready, WR)
            if full:
                e.tensor_scalar(bb[:, 0:2], bb[:, 0:2], 0.25, None, ALU.mult).then_inc(prep, 1)
            e.wait_ge(prep, NPREP)
            mask8 = self.const("headmask")
            with e.Fori(0, NB) as b:
                per = 7 if full else 3
                own.enter(b, per)

                def head_queries(t):
                    for j in range(8):
                        e.tensor_scalar(qm[:, 8 * t + j], q[:, t, 1:T], mask8[:, j:j + 1], None, ALU.mult).then_inc(sem("qm"), 1)

                for n, (name, t, _) in enumerate(units):
                    e.wait_ge(sem("proj"), b * NU + n + 1)
                    bank = BANKS[n % 8]
                    if name == "v":
                        dst = v[:, t].rearrange("p (h s) -> p h s", s=32)[:, :, 0:HD]
                        src = bank[:, 0:D].rearrange("p (h s) -> p h s", s=HD)
                        if full:
                            m = e.tensor_tensor(dst, src, bv[:].rearrange("p (h s) -> p h s", s=HD), ALU.add)
                        else:
                            m = e.tensor_copy(dst, src)
                    elif name == "vc":
                        own.did(e.tensor_tensor(self.a_vt[:], bank[0:16, 0:D], bv[0:16, :], ALU.add))
                        own.wait()
                        m = e.tensor_tensor(vc[0:16, :].rearrange("p (h s) -> p h s", s=32)[:, :, 0:HD],
                                            self.a_vt[:].rearrange("p (h s) -> p h s", s=HD),
                                            self.const("diag")[0:16, :].unsqueeze(2).to_broadcast([16, HEADS, HD]), ALU.mult)
                    elif full:
                        dst = (q if name == "q" else k)[:, t]
                        if name == "q":
                            m = e.tensor_scalar(dst, bank[:, 0:T], 0.25, bb[:, t:t + 1], ALU.mult, ALU.add)
                        else:
                            m = e.tensor_scalar(dst, bank[:, 0:T], bb[:, 2 + t:3 + t], None, ALU.add)
                    else:
                        r = 0 if name[0] == "q" else 2
                        if len(name) == 1 and r + t >= 2:
                            e.wait_ge(sem("rope_add"), b * 4 + r + t - 1)
                        tab = self.const(("c" if len(name) == 1 else "s") + name[0])
                        m = e.tensor_tensor(self.a_rope[:, t, len(name) - 1], bank[:, 0:256], tab, ALU.mult)
                    m.then_inc(sem("moved"), 1)
                    if full and name == "q":
                        e.wait_ge(sem("moved"), b * NU + n + 1)
                        head_queries(t)
                    if not full and name == "ks":
                        e.wait_ge(sem("rope_add"), b * 4 + t + 1)
                        head_queries(t)
                if not full:
                    e.wait_ge(sem("rope_add"), b * 4 + 4)
                if full:
                    e.tensor_tensor(qc[:], q[:, :, 0:1].to_broadcast([P, DT, 16]),
                                    self.const("clsheads").rearrange("p (t h) -> p t h", t=2), ALU.mult).then_inc(sem("qm"), 1)
                for u in range(NH + 1):
                    if u < NH:
                        s = u % 2
                        e.wait_ge(sem("scores"), b * NH + u + 1)
                        if u < HEADS:
                            e.tensor_reduce(nm[:, u, :], psS[:, 2 * s:2 * s + 2, 0:NK], AX, ALU.max, negate=True).then_inc(sem("max"), 1)
                        else:
                            e.tensor_reduce(nm[0:16, u, 0:1], psS[0:16, 2 * s, 0:NK], AX, ALU.max, negate=True).then_inc(sem("max"), 1)
                    if u >= 1:
                        h = u - 1
                        e.wait_ge(sem("turned"), b * NH + u)
                        if h < HEADS:
                            if h >= 8:
                                e.wait_ge(sem("pv"), b * 4 + (h - 8) // 4 + 1)
                            e.tensor_copy(pt[:, h % 8], psT[:, h % 2, :]).then_inc(sem("pt"), 1)
                        else:
                            e.tensor_copy(self.a_pct[:].rearrange("p k h -> p (k h)"), psT[:, h % 2, 0:32]).then_inc(sem("pt"), 1)
                e.wait_ge(sem("exp"), b * NH + NH)
                own.did(e.tensor_scalar(self.a_rs[:], self.a_sum[:], SUM_GUARD, None, ALU.max))
                own.wait()
                own.did(e.reciprocal(self.a_rs[:], self.a_rs[:]))
                own.wait()
                if full:
                    m = e.reciprocal(self.a_rsc[:, 1:2], self.a_rsc[:, 0:1])
                else:
                    m = e.tensor_tensor(self.a_rs[:], self.a_rs[:],
                                        self.const("valid").unsqueeze(2).to_broadcast([P, QT, HEADS]), ALU.mult)
                m.then_inc(sem("rs"), 1)
                e.wait_ge(sem("tailT"), b + 1)
                if full:
                    e.wait_ge(sem("rs"), b + 1)
                    e.tensor_copy(self.a_rst[0:16, 0:1], self.a_rsc[:, 1:2])
                    e.tensor_copy(self.a_pext[0:16, 1:T], psT[0:16, 1, 0:256])
                    e.tensor_copy(self.a_pext[0:16, 0:1], self.a_pc[:, 0:1])
                e.tensor_copy(self.a_rst[0:16, 1:T], psT[0:16, 0, 0:256]).then_inc(sem("tailC"), 1)
                if full:
                    e.wait_ge(sem("clsy"), b + 1)
                    own.did(e.tensor_tensor(self.a_yc[:], psY[:, 0, 0:64].rearrange("p (g h) -> p g h", h=16),
                                            self.const("clspick").rearrange("p (g h) -> p g h", h=16), ALU.mult))
                    own.wait()
                    own.did(e.tensor_reduce(self.a_y[:, :, 0:1], self.a_yc[:], AX, ALU.add))
                    own.wait()
                e.wait_ge(sem("y"), b * 4 + 4)
                for g in range(4):
                    e.wait_ge(sem("R"), b * 4 + g + 1)
                    if full:
                        if g >= 1:
                            pass
                        e.tensor_tensor(self.a_y[:, g], self.a_y[:, g], psS[:, g % 2, 0:T], ALU.add).then_inc(sem("yadd"), 1)
                        e.wait_ge(sem("yadd"), b * 4 + g + 1)
                        e.tensor_tensor(self.a_yn[:, g], self.a_y[:, g], psS[:, 2 + g % 2, 0:T], ALU.mult).then_inc(sem("yn"), 1)
                    else:
                        e.tensor_tensor(self.a_yn[:, g, 1:T], self.a_y[:, g, 1:T], psS[:, 2 + g % 2, 1:T], ALU.mult).then_inc(sem("yn"), 1)
                e.wait_ge(sem("out"), b + 1)
                for mt in range(DT):
                    dst = xT[:, mt, bass.ds(b * T + K0, NK)]
                    if full:
                        m = own.did(e.scalar_tensor_tensor(dst, psY[:, mt, 0:NK], bb[:, 4 + mt:5 + mt], dst, ALU.add, ALU.add))
                    else:
                        m = e.tensor_tensor(dst, psY[:, mt, 0:NK], dst, ALU.add)
                        if mt == 0:
                            own.did(m)
                batch_end(e, b)
                own.leave(NB)
        return {"sp": sp, "pool": pool, "pe": pe, "act": act, "dve": dve}

    def router(self, L):
        A, psT, psS = self.A, self.psT, self.psS
        N = 17
        starts = [128 * n for n in range(16)] + [COLS - 128]
        S = {n: self.sem(f"rt{L}_{n}") for n in ("w", "split", "logits", "own", "shift", "exp", "gates", "turned",
                                                   "moved", "stored")}

        def sp(e):
            e.dma_start(self.r_w[:], A[f"router{L}"]).then_inc(S["w"], 16)
            e.dma_start(self.r_b[:], A[f"router_b{L}"]).then_inc(S["w"], 16)
            e.wait_ge(S["moved"], 5)
            e.dma_start(self.gates_dram[L], self.g_t[:]).then_inc(S["stored"], 16)
            e.wait_ge(S["stored"], 16)

        def pe(e):
            e.wait_ge(S["split"], 2)
            for n, at in enumerate(starts):
                for c, (i, j) in enumerate([(x, y) for x in range(DT) for y in range(3)]):
                    xa, wa = ((0, 0), (0, 1), (1, 0))[j]
                    m = e.matmul(psT[:, 0, 8 * n:8 * n + 8], self.x_hl[:, xa, i, at:at + 128],
                                 self.r_hl[:, wa, E * i:E * i + E], start=c == 0, stop=c == 5)
            m.then_inc(S["logits"], 1)
            e.wait_ge(S["gates"], 1)
            for n in range(N):
                if n == 16:
                    e.wait_ge(S["moved"], 1)
                m = e.transpose(psS[0:E + 1, (n // 4) % 4, 128 * (n % 4):128 * (n % 4) + 128], self.g_all[:, n], self.const("ident"))
                if n % 4 == 3 or n == N - 1:
                    m.then_inc(S["turned"], 1)

        def act(e):
            e.wait_ge(S["shift"], 1)
            e.activation(self.g_p[:], self.g_p[:], ACT.Exp).then_inc(S["exp"], 1)

        def dve(e):
            own = Own(e, S["own"])
            p, sel, m4, cmp_ = self.g_p, self.g_sel, self.g_m, self.g_cmp
            e.wait_ge(S["w"], 32)
            e.tensor_copy(self.r_hl[:, 0], self.r_w[:]).then_inc(S["split"], 1)
            e.wait_ge(S["split"], 1)
            e.tensor_tensor(self.r_hl[:, 1], self.r_w[:], self.r_hl[:, 0].bitcast(F32), ALU.subtract).then_inc(S["split"], 1)
            e.wait_ge(S["logits"], 1)
            logits = psT[:, 0, 0:8 * N].rearrange("p (n e) -> p n e", e=E)
            own.did(e.tensor_tensor(p[:], logits, self.r_b[:].unsqueeze(1).to_broadcast([P, N, E]), ALU.add))
            own.wait()
            own.did(e.tensor_reduce(m4[:, 0], p[:], AX, ALU.max))
            own.wait()
            e.tensor_tensor(p[:], p[:], m4[:, 0].unsqueeze(2).to_broadcast([P, N, E]), ALU.subtract).then_inc(S["shift"], 1)
            e.wait_ge(S["exp"], 1)
            own.did(e.tensor_reduce(m4[:, 1], p[:], AX, ALU.add))
            own.wait()
            own.did(e.reciprocal(m4[:, 2], m4[:, 1]))
            own.wait()
            own.did(e.tensor_tensor(p[:], p[:], m4[:, 2].unsqueeze(2).to_broadcast([P, N, E]), ALU.mult))
            own.wait()
            shape = [P, N, E, E]
            mine = p[:].unsqueeze(3).to_broadcast(shape)
            other = p[:].unsqueeze(2).to_broadcast(shape)
            tri = self.const("tri").rearrange("p (a b) -> p a b", a=E)
            own.did(e.tensor_tensor(cmp_[:, 0], other, mine, ALU.is_gt))
            own.did(e.tensor_tensor(cmp_[:, 1], other, mine, ALU.is_equal))
            own.wait()
            own.did(e.tensor_tensor(cmp_[:, 1], cmp_[:, 1], tri.unsqueeze(1).to_broadcast(shape), ALU.mult))
            own.wait()
            own.did(e.tensor_tensor(cmp_[:, 0], cmp_[:, 0], cmp_[:, 1], ALU.add))
            own.wait()
            own.did(e.tensor_reduce(sel[:], cmp_[:, 0], AX, ALU.add))
            own.wait()
            own.did(e.tensor_scalar(sel[:], sel[:], 1.5, 0.5 if L == 0 else 1.0, ALU.is_lt, ALU.mult))
            own.did(e.memset(self.g_all[:, :, E:E + 1], 1.0 / 16 if L == 0 else 1.0))
            own.wait()
            e.tensor_tensor(self.g_all[:, :, 0:E], p[:], sel[:], ALU.mult).then_inc(S["gates"], 1)
            for c in range(5):
                e.wait_ge(S["turned"], c + 1)
                if c < 4:
                    e.tensor_copy(self.g_t[:, 512 * c:512 * c + 512], psS[0:E + 1, c, :]).then_inc(S["moved"], 1)
                else:
                    e.wait_ge(S["moved"], 4)
                    e.tensor_copy(self.g_t[:, COLS - 128:COLS], psS[0:E + 1, 0, 0:128]).then_inc(S["moved"], 1)
        return {"sp": sp, "pe": pe, "act": act, "dve": dve}

    def experts(self, L):
        A, xT, psS, psY = self.A, self.xT, self.psS, self.psY
        gated = L == 0
        NUN = 18 if gated else 9
        FT = 4
        W = 3072 if gated else 2048
        WL = W + (0 if gated else 6)
        O2 = 2048 if gated else 1024
        CREDIT = 3
        TERMS = ((0, 0), (0, 1), (1, 0))
        S = {n: self.sem(f"ex{L}_{n}") for n in ("w_loaded0", "w_loaded1", "w_hi", "w_lo", "g_loaded0", "g_loaded1", "unit_dve", "gu",
                                                   "act", "h", "hraw", "hhi", "w2", "t", "added", "bias")}
        src = A[f"ffn{L}"]

        def credit(e, *names):
            for name in names:
                for _ in range(CREDIT):
                    e.nop().then_inc(S[name], 1)


        def over_units(e, chunks, ahead=None):
            ahead = ahead or (lambda slot, i: None)
            ahead(0, 0)
            with e.Fori(0, (NUN - 1) // 2) as i:
                ahead(1, i)
                chunks(0, i)
                ahead(0, i + 1)
                chunks(1, i)
            last = (NUN - 1) // 2
            if NUN % 2 == 0:
                ahead(1, last)
                chunks(0, last)
                chunks(1, last)
            else:
                chunks(0, last)

        def sp(e):
            def load(slot, i):
                n = i * 2 + slot
                unit = src[n] if isinstance(n, int) else src[bass.ds(n, 1)].rearrange("o p w -> (o p) w")
                e.dma_start(self.w_stage[:, slot, 0:WL], unit).then_inc(S[f"w_loaded{slot}"], 16)

            def gates(slot, i):
                row = i if gated else i * 2 + slot
                g = self.gates_dram[L, row:row + 1] if isinstance(row, int) else self.gates_dram[L, bass.ds(row, 1)]
                e.dma_start(self.gate[:, slot], g.to_broadcast([P, COLS])).then_inc(S[f"g_loaded{slot}"], 16)

            def again(slot, i):
                n = i * 2 + slot
                e.wait_ge(S["w_lo"], n - 1)
                load(slot, i)
                e.wait_ge(S["unit_dve"], n - 1 + CREDIT)
                gates(slot, i)

            for slot in range(2):
                load(slot, 0)
                gates(slot, 0)
            with e.Fori(1, NUN // 2) as i:
                again(0, i)
                again(1, i)
            if NUN % 2:
                again(0, NUN // 2)

        def act(e):
            def split(slot, i):
                n = i * 2 + slot
                e.wait_ge(S[f"w_loaded{slot}"], i * 16 + 16)
                if not isinstance(n, int) or n >= 2:
                    e.wait_ge(S["w2"], (n - 1) * (NCH * FT) + CREDIT)
                if not gated:
                    e.wait_ge(S["unit_dve"], n - 1 + CREDIT)
                    e.activation(self.w_bias[:, slot], self.w_stage[:, slot, W:WL], ACT.Copy).then_inc(S["bias"], 1)
                e.activation(self.w_hi[:, slot, 0:W], self.w_stage[:, slot, 0:W], ACT.Copy).then_inc(S["w_hi"], 1)

            def chunks(slot, i):
                n = i * 2 + slot
                if not gated:
                    e.wait_ge(S["bias"], n + 1)
                    e.nop().then_inc(self.paced, 1)
                with e.Fori(0, NCH) as c:
                    k = n * (NCH * FT) + c * FT
                    for f in range(FT):
                        e.wait_ge(S["gu"], k + f + 1)
                        if gated:
                            e.wait_ge(S["hraw"], k + f - 1 + CREDIT)
                            e.activation(self.f_act[:, f % 2], psS[:, f % 2, 0:CH], ACT.Silu).then_inc(S["act"], 1)
                        else:
                            e.wait_ge(S["h"], k + f - 1 + CREDIT)
                            e.activation(self.f_h[:, f % 2], psS[:, f % 2, 0:CH], ACT.Gelu,
                                         bias=self.w_bias[:, slot, f:f + 1]).then_inc(S["act"], 1)
            over_units(e, chunks, split)

        def pool(e):
            credit(e, "added")

            def split(slot, i):
                n = i * 2 + slot
                e.wait_ge(S["w_hi"], n + 1)
                e.nop().then_inc(self.paced, 1)
                e.tensor_tensor(self.w_lo[:, slot, 0:W], self.w_stage[:, slot, 0:W], self.w_hi[:, slot, 0:W].bitcast(F32),
                                ALU.subtract).then_inc(S["w_lo"], 1)

            def chunks(slot, i):
                n = i * 2 + slot
                with e.Fori(0, NCH) as c:
                    e.wait_ge(S["t"], n * NCH + c + 1 + CREDIT)
                    e.nop().then_inc(self.paced, 1)
                    x = xT[:, :, bass.ds(c * CH, CH)]
                    e.tensor_tensor(x, x, self.f_t[:], ALU.add).then_inc(S["added"], 1)
            over_units(e, chunks, split)

        def dve(e):
            credit(e, "hraw", "h", "t", "unit_dve")

            def chunks(slot, i):
                n = i * 2 + slot
                e.wait_ge(S[f"g_loaded{slot}"], i * 16 + 16)
                e.nop().then_inc(self.paced, 1)
                if not gated:
                    e.wait_ge(S["bias"], n + 1)
                    e.nop().then_inc(self.paced, 1)
                with e.Fori(0, NCH) as c:
                    k = n * (NCH * FT) + c * FT
                    for f in range(FT):
                        e.wait_ge(S["act"], k + f + 1)
                        raw = self.f_h[:, f % 2]
                        if gated:
                            e.tensor_tensor(raw, self.f_act[:, f % 2], psS[:, 2 + f % 2, 0:CH], ALU.mult).then_inc(S["hraw"], 1)
                            e.wait_ge(S["hraw"], k + f + 1 + CREDIT)
                        e.wait_ge(S["w2"], k + f - 2 + CREDIT)
                        e.tensor_copy(self.f_hl[:, f % 2, 0], raw).then_inc(S["hhi"], 1)
                        e.wait_ge(S["hhi"], k + f + 1)
                        e.tensor_tensor(self.f_hl[:, f % 2, 1], raw, self.f_hl[:, f % 2, 0].bitcast(F32), ALU.subtract).then_inc(S["h"], 1)
                    e.wait_ge(S["w2"], k + FT + CREDIT)
                    e.wait_ge(S["added"], n * NCH + c + CREDIT)
                    for mt in range(DT):
                        bias = 0.0 if gated else self.w_bias[:, slot, 4 + mt:5 + mt]
                        m = e.scalar_tensor_tensor(self.f_t[:, mt], psY[:, mt, 0:CH], bias,
                                                   self.gate[:, slot, bass.ds(c * CH, CH)], ALU.add, ALU.mult)
                    m.then_inc(S["t"], 1)
                e.wait_ge(S["t"], n * NCH + NCH + CREDIT)
                e.nop().then_inc(S["unit_dve"], 1)

            over_units(e, chunks)

        def pe(e):
            wh, wl, hl, xhl = self.w_hi, self.w_lo, self.f_hl, self.x_hl
            w = (wh, wl)
            credit(e, "w2")

            def chunks(slot, i):
                n = i * 2 + slot
                e.wait_ge(S["w_lo"], n + 1)
                e.nop().then_inc(self.paced, 1)
                with e.Fori(0, NCH) as c:
                    k = n * (NCH * FT) + c * FT

                    def up(f):
                        e.wait_ge(S["h"], k + f - 1 + CREDIT)
                        for m_, base in ((0, 0), (2, 1024))[:2 if gated else 1]:
                            i = 0
                            for dt in range(DT):
                                for a, z in TERMS:
                                    at = base + 512 * dt + 128 * f
                                    m = e.matmul(psS[:, m_ + f % 2, 0:CH], w[a][:, slot, at:at + 128],
                                                 xhl[:, z, dt, bass.ds(c * CH, CH)], start=i == 0, stop=i == 2 * DT + 1)
                                    i += 1
                        m.then_inc(S["gu"], 1)

                    def down(f):
                        e.wait_ge(S["h"], k + f + 1 + CREDIT)
                        if f == 0:
                            e.wait_ge(S["t"], n * NCH + c + CREDIT)
                        for mt in range(DT):
                            for i, (a, z) in enumerate(TERMS):
                                at = O2 + 256 * f + 128 * mt
                                m = e.matmul(psY[:, mt, 0:CH], w[a][:, slot, at:at + 128], hl[:, f % 2, z],
                                             start=f == 0 and i == 0, stop=f == FT - 1 and i == 2)
                        m.then_inc(S["w2"], 1)
                    up(0)
                    for f in range(1, FT):
                        up(f)
                        down(f - 1)
                    down(FT - 1)
            over_units(e, chunks)
        return {"sp": sp, "act": act, "pool": pool, "dve": dve, "pe": pe}

    def write_out(self):
        xT, psS, rows = self.xT, self.psS, self.o_rows
        turned, moved = self.sem("o_turned"), self.sem("o_moved")
        stored = [self.sem(f"o_stored{n}") for n in range(4)]
        tiles = [(128 * n, 128) for n in range(16)] + [(2048, 8)]
        out = self.out.rearrange("b t d -> (b t) d")

        def pe(e):
            for n, (at, m) in enumerate(tiles):
                if n >= 4:
                    e.wait_ge(moved, n - 3)
                for dt in range(DT):
                    t = e.transpose(psS[0:m, n % 4, 128 * dt:128 * dt + 128], xT[:, dt, at:at + m], self.const("ident"))
                t.then_inc(turned, 1)

        def act(e):
            for n, (at, m) in enumerate(tiles):
                e.wait_ge(turned, n + 1)
                if n >= 4:
                    e.wait_ge(stored[n % 4], 16 * (n // 4))
                e.activation(rows[0:m, n % 4], psS[0:m, n % 4, 0:D], ACT.Copy).then_inc(moved, 1)

        def sp(e):
            for n, (at, m) in enumerate(tiles):
                e.wait_ge(moved, n + 1)
                e.dma_start(out[at:at + m, :], rows[0:m, n % 4]).then_inc(stored[n % 4], 16)
            for n in range(4):
                e.wait_ge(stored[n], 16 * ((len(tiles) - n + 3) // 4))
        return {"pe": pe, "act": act, "sp": sp}


def lay_out(x):
    f = lambda a: np.ascontiguousarray(a)
    n = {k: np.asarray(v) for k, v in x.items()}

    def by_pair(a):
        a = a.reshape(2, P, *a.shape[1:])
        return np.moveaxis(a, 1, -1)

    small = np.zeros((P, 5, P), np.float32)
    b = by_pair(n["L0_tok_B_ri"])
    small[:, 0:2] = b.reshape(P, 2, P)
    small[:, 2] = by_pair(n["L0_tok_inv_A_real"]).reshape(P, P)
    small[:, 3] = by_pair(n["L0_tok_A_imag"]).reshape(P, P)
    small[:, 4] = np.broadcast_to(n["L0_tok_log_dt"].reshape(2, 1, P), (2, 64, P)).reshape(P, P)
    c = n["x"].reshape(NB, 2, P, 64, 2).transpose(1, 3, 4, 0, 2).reshape(P, 2, NB, P)

    def down(w):
        return w.T.reshape(DT, P, w.shape[0]).transpose(1, 0, 2)

    def padded(w):
        r = np.zeros((4, GRP, 32, D), np.float32)
        r[:, :, 0:HD] = w.T.reshape(4, GRP, HD, D)
        return r.transpose(1, 2, 0, 3).reshape(P, 4, D)

    wa = n["L0_attn_w_attn"]
    wq, wk, wv = wa[0:D], wa[D:2 * D], wa[2 * D:]
    swap = np.arange(D).reshape(-1, 2)[:, ::-1].reshape(-1)
    a = {
        "consts": constants(), "s4_small": small, "s4_c": c,
        "cls": n["cls_tok"].reshape(DT, P).T,
        "w_qkv0": down(np.concatenate([wq, wq[swap], wk, wk[swap], wv])),
        "w_qkv1": down(np.concatenate([n["L1_attn_Wq"], n["L1_attn_Wk"], n["L1_attn_Wv"]])),
        "w_o0": padded(n["L0_attn_w_proj"]), "w_o1": padded(n["L1_attn_Wo"]),
        "a_bias": np.concatenate([n["L1_attn_" + k].reshape(DT, P).T for k in ("bq", "bk", "bo")], axis=1),
        "a_bv": np.broadcast_to(n["L1_attn_bv"][None, :], (P, D)),
        "router0": down(n["L0_ffn_gate_W"]).reshape(P, DT * E),
        "router1": n["L1_ffn_router_w"].reshape(DT, P, E).transpose(1, 0, 2).reshape(P, DT * E),
        "router_b0": np.zeros((P, E), np.float32),
        "router_b1": np.broadcast_to(n["L1_ffn_router_b"][None, :], (P, E)),
    }
    def up(e, s):
        w = np.concatenate([e, s.transpose(1, 0, 2).reshape(1, D, 1024)])
        return w.reshape(9, DT, P, 2, 512).transpose(0, 3, 2, 1, 4).reshape(18, P, 1024)
    w2 = np.concatenate([n["L0_ffn_w2_e"], n["L0_ffn_w2_s"].reshape(1, 1024, D)])
    w2 = w2.reshape(18, 4, P, D).transpose(0, 2, 1, 3).reshape(18, P, 1024)
    a["ffn0"] = np.concatenate([up(n["L0_ffn_w1_e"], n["L0_ffn_w1_s"]), up(n["L0_ffn_w3_e"], n["L0_ffn_w3_s"]), w2], axis=2)
    w1 = np.concatenate([n["L1_ffn_rw1"], n["L1_ffn_sw1"][None]]).reshape(9, DT, P, 512).transpose(0, 2, 1, 3).reshape(9, P, 1024)
    w2 = np.concatenate([n["L1_ffn_rw2"], n["L1_ffn_sw2"][None]]).reshape(9, 4, P, D).transpose(0, 2, 1, 3).reshape(9, P, 1024)
    b1 = np.concatenate([n["L1_ffn_rb1"], n["L1_ffn_sb1"][None]]).reshape(9, 4, P).transpose(0, 2, 1)
    b2 = np.concatenate([n["L1_ffn_rb2"], n["L1_ffn_sb2"][None]]).reshape(9, 2, P).transpose(0, 2, 1)
    a["ffn1"] = np.concatenate([w1, w2, b1, b2], axis=2)
    return {k: f(v) for k, v in a.items()}


def kernel(**inputs):
    import concourse.bacc as _bacc
    from concourse.bass_utils import run_bass_kernel_spmd as _run

    arrays = lay_out(inputs)
    nc = _bacc.Bacc("TRN2", target_bir_lowering=False, num_devices=1)
    args = {k: nc.dram_tensor("in_" + k, v.shape, F32, kind="ExternalInput").ap() for k, v in arrays.items()}
    out = nc.dram_tensor("out", (NB, T, D), F32, kind="ExternalOutput").ap()
    Tower(nc, args, out).build()
    r = _run(nc, [{"in_" + k: a for k, a in arrays.items()}], core_ids=[0])
    return r.results[0]["out"]
```

```python
from contextlib import ExitStack

import numpy as np
import concourse.bass as bass
from concourse import mybir

F32 = mybir.dt.float32
F32R = mybir.dt.float32r
BF16 = mybir.dt.bfloat16
ACT = mybir.ActivationFunctionType
ALU = mybir.AluOpType
AX = mybir.AxisListType.X

P = 128
NB, T, D = 8, 257, 256
DT = D // P
TOK = NB * T
NT = 17
COLS = NT * P
HEADS, HD = 16, 16
QT = 2
GRP = 4
BAND_REG, BAND_HALF = 16, 32
E = 8
TOP = 2
BL = 384
SUB = BL // P
ROUTED = (TOP * TOK + E * (BL - 1)) // BL
SHARED = -(-TOK // BL)
BLOCKS = ROUTED + SHARED
FIRST = 2
BACK = SUB * FIRST
SLOTS = ROUTED * BL
STEPS = -(-TOK // BL)
S4_HP = 16
S4_NB = P // S4_HP
S4_DVE = 11
EPS = 1e-5


ROPE_MASK = {"maskq": (0, 512), "cq": (512, 768), "sq": (768, 1024), "ck": (1024, 1280), "sk": (1280, 1536)}


def constant_layout():
    widths = [("ones", P), ("before", P), ("ident", P), ("headmask", 8), ("spread", 4 * P), ("diag", 16), ("clspick", 4 * 16),
              ("clsheads", 2 * 16), ("tri", 64), ("eps", 1), ("valid", QT),
              ("real", NT), ("steps", STEPS), ("blocks", ROUTED)]
    at, out = 0, {}
    for name, w in widths:
        out[name] = (at, at + w)
        at += w
    return out, at


def constants():
    where, width = constant_layout()
    c = np.zeros((P, width), np.float32)

    def put(name, value):
        a, b = where[name]
        c[:, a:b] = np.asarray(value, np.float32).reshape(P, b - a)

    table = {}
    p = np.arange(P)
    put("ones", np.ones((P, P)))
    put("before", p[:, None] < p[None, :])
    put("ident", np.eye(P))
    t = np.arange(1, 257)
    q = (p[:, None] + P * np.arange(QT)[None, :] + 1)[:, :, None]
    j = t[None, None, :]
    near = (q >= BAND_REG) & (j >= np.maximum(BAND_REG, q - BAND_HALF)) & (j <= q + BAND_HALF)
    table["maskq"] = (np.where((j < BAND_REG) | (q < BAND_REG) | near, -1e30, 0.0))
    theta = (np.float32(1.0) / np.float32(10000.0) ** (np.arange(0, HD, 2, dtype=np.float32) / np.float32(HD)))
    ang = (t.astype(np.float32)[None, :] * theta[(p % HD) // 2][:, None]).astype(np.float32)
    cos = np.cos(ang)
    sin = np.where((p % 2 == 0)[:, None], -np.sin(ang), np.sin(ang))
    table["ck"] = cos
    table["sk"] = sin
    table["cq"] = cos * np.float32(0.25)
    table["sq"] = sin * np.float32(0.25)
    put("headmask", p[:, None] // HD == np.arange(8)[None, :])
    g, m = np.arange(4)[None, :, None], np.arange(P)[None, None, :]
    put("spread", p[:, None, None] == GRP * g + m // 32)
    put("diag", p[:, None] == np.arange(16)[None, :])
    put("clspick", np.arange(16)[None, None, :] == GRP * np.arange(4)[None, :, None] + p[:, None, None] // 32)
    put("clsheads", np.arange(16)[None, None, :] == 8 * np.arange(2)[None, :, None] + p[:, None, None] // HD)
    put("tri", np.broadcast_to(np.arange(E)[None, :] < np.arange(E)[:, None], (P, E, E)))
    put("eps", np.full(P, EPS))
    put("valid", (q[:, :, 0] >= BAND_REG))
    put("real", (np.arange(NT)[None, :] < NT - 1) | (p[:, None] < NB))
    put("steps", np.broadcast_to(BL * np.arange(STEPS), (P, STEPS)))
    put("blocks", np.broadcast_to(np.arange(ROUTED), (P, ROUTED)))
    return c, np.concatenate([np.asarray(table[n], np.float32).reshape(P, -1) for n in ROPE_MASK], axis=1)


class Own:

    def __init__(self, eng, sem, apart=None):
        self.eng, self.sem, self.base, self.n, self.apart = eng, sem, 0, 0, apart

    def did(self, ins):
        ins.then_inc(self.sem, 1)
        self.n += 1
        return ins

    def wait(self):
        self.eng.wait_ge(self.sem, self.base + self.n)
        if self.apart:
            self.eng.nop().then_inc(self.apart, 1)

    def enter(self, i, per):
        self.outer, self.per, self.start = self.base, per, self.n
        self.base, self.n = self.outer + self.start + i * per, 0

    def leave(self, passes):
        assert self.n == self.per, (self.sem, self.n, self.per)
        self.base, self.n = self.outer, self.start + passes * self.per


class Tower:
    def __init__(self, nc, A, out, stop=99):
        self.nc, self.A, self.out, self.stop = nc, A, out, stop
        self.engines = {}

    def sem(self, name, again=True):
        if not again:
            return self.top.enter_context(self.nc.semaphore(name))
        s = self.free.pop(0) if self.free else self.top.enter_context(self.nc.semaphore(name))
        self.used.append(s)
        return s

    def sb(self, scope, name, shape, dt=F32):
        return scope.enter_context(self.nc.sbuf_tensor(name, shape, dt))

    def const(self, name, *dims):
        a, b = constant_layout()[0][name]
        return self.cst[:, a:b]

    def table(self, name):
        a, b = ROPE_MASK[name]
        return self.a_table[:, a:b]

    def build(self):
        nc = self.nc
        with ExitStack() as self.top:
            sb, top = self.sb, self.top
            self.X = sb(top, "X", [P, NT, D])
            self.cst = sb(top, "cst", [P, constant_layout()[1]])
            self.psS = top.enter_context(nc.psum_tensor("psS", [P, 4, 512], F32))
            self.psT = top.enter_context(nc.psum_tensor("psT", [P, 2, 512], F32))
            self.psY = top.enter_context(nc.psum_tensor("psY", [P, 2, 512], F32))
            self.rows_in = nc.dram_tensor("rows_in", [SLOTS, D], F32, kind="Internal").ap()
            self.rows_out = nc.dram_tensor("rows_out", [SLOTS, D], F32, kind="Internal").ap()
            with ExitStack() as s4:
                self.memory_s4(s4)
            self.where = sb(top, "where", [P, TOP, NT], mybir.dt.int32)
            self.gates = sb(top, "gates", [P, TOP, NT])
            self.expert_of = sb(top, "expert_of", [P, BLOCKS], mybir.dt.int32)
            with ExitStack() as a:
                self.memory_norm(a)
                with ExitStack() as b:
                    self.memory_attention(b)
                with ExitStack() as b:
                    self.memory_router(b)
                with ExitStack() as b:
                    self.memory_experts(b)
            self.free, self.used = [], []
            self.stage_done = self.sem("stage_done")
            self.loaded = self.sem("loaded")
            self.rows_cleared = self.sem("rows_cleared")
            self.scattered = self.sem("scattered", again=False)
            self.gathered = [self.sem(f"gathered{s}", again=False) for s in range(BACK)]
            self.paced = self.sem("paced")
            self.program()

    def memory_s4(self, s):
        sb = self.sb
        self.s4_small = sb(s, "s4_small", [P, 5, P])
        self.s4_c = sb(s, "s4_c", [P, 2, NB, P])
        self.s4_w = sb(s, "s4_w", [P, 8, 2, P])
        self.s4_tmp = sb(s, "s4_tmp", [P, 8, P])
        self.s4_cb = sb(s, "s4_cb", [P, 2, 2, NB, P])
        self.s4_prod = sb(s, "s4_prod", [P, 2, NB, P])
        self.s4_p = sb(s, "s4_p", [P, 2, P, 2, 2, NB])
        self.s4_v = sb(s, "s4_v", [P, 2, 2, S4_HP, P])
        self.s4_t = sb(s, "s4_t", [P, 2, S4_HP, 64])
        self.s4_k = sb(s, "s4_k", [P, DT, NB * 256])
        self.s4_zero = sb(s, "s4_zero", [P, D])

    def memory_norm(self, s):
        sb = self.sb
        self.n_stat = sb(s, "n_stat", [P, NT, 6])
        self.n_mv = sb(s, "n_mv", [P, NT, 2])
        self.n_sd = sb(s, "n_sd", [P, NT, 2])
        self.n_rows = sb(s, "n_rows", [P, NT, D])

    def memory_attention(self, s):
        sb = self.sb
        self.xn = sb(s, "xn", [P, DT, COLS])
        self.a_w = sb(s, "a_w", [P, DT, 1280])
        self.a_wo = sb(s, "a_wo", [P, 4, D])
        self.a_b = sb(s, "a_b", [P, 4])
        self.a_bo = sb(s, "a_bo", [P, D])
        self.a_table = sb(s, "a_table", [P, 1536])
        self.a_ycls = sb(s, "a_ycls", [P, 4, NB])
        self.a_bv = sb(s, "a_bv", [P, D])
        self.a_x = sb(s, "a_x", [P, DT, T])
        self.a_xc = sb(s, "a_xc", [P, DT, 16])
        self.a_rope = sb(s, "a_rope", [P, 2, 2, 256])
        self.a_q = sb(s, "a_q", [P, DT, T])
        self.a_qm = sb(s, "a_qm", [P, HEADS, 256])
        self.a_qc = sb(s, "a_qc", [P, DT, 16])
        self.a_k = sb(s, "a_k", [P, DT, T])
        self.a_v = sb(s, "a_v", [P, QT, HEADS * 32])
        self.a_vt = sb(s, "a_vt", [16, D])
        self.a_vc = sb(s, "a_vc", [P, HEADS * 32])
        self.a_p = sb(s, "a_p", [P, 2, QT, T])
        self.a_pt = sb(s, "a_pt", [P, 8, 512])
        self.a_nm = sb(s, "a_nm", [P, HEADS + 1, QT])
        self.a_sum = sb(s, "a_sum", [P, QT, HEADS])
        self.a_rs = sb(s, "a_rs", [P, QT, HEADS])
        self.a_rsc = sb(s, "a_rsc", [16, 2])
        self.a_pex = sb(s, "a_pex", [P, QT, HEADS])
        self.a_pc = sb(s, "a_pc", [16, T])
        self.a_pct = sb(s, "a_pct", [P, QT, 16])
        self.a_rst = sb(s, "a_rst", [P, T])
        self.a_pext = sb(s, "a_pext", [P, T])
        self.a_yc = sb(s, "a_yc", [P, 4, 16])
        self.a_y = sb(s, "a_y", [P, 4, T])
        self.a_yn = sb(s, "a_yn", [P, 4, T])
        self.a_maskb = sb(s, "a_maskb", [P, QT, 256], BF16)
        self.a_identb = sb(s, "a_identb", [P, P], BF16)

    def memory_router(self, s):
        sb = self.sb
        self.x_hl = sb(s, "x_hl", [P, 2, DT, COLS], F32R)
        self.r_w = sb(s, "r_w", [P, DT * E])
        self.r_hl = sb(s, "r_hl", [P, 2, DT * E], F32R)
        self.r_b = sb(s, "r_b", [P, E])
        self.g_p = sb(s, "g_p", [P, NT, E])
        self.g_cmp = sb(s, "g_cmp", [P, 2, NT, E, E])
        self.g_m = sb(s, "g_m", [P, 4, NT])
        self.g_sel = sb(s, "g_sel", [P, NT, E])
        self.g_pick = sb(s, "g_pick", [P, TOP, NT, E])
        self.g_tmp = sb(s, "g_tmp", [P, NT, E])
        self.g_carry = sb(s, "g_carry", [P, NT + 1, E])
        self.g_tot = sb(s, "g_tot", [P, NT, E])
        self.g_pos = sb(s, "g_pos", [P, TOP, NT])
        self.g_cnt = sb(s, "g_cnt", [P, 2, E])
        self.g_big = sb(s, "g_big", [P, ROUTED, E])

    def memory_experts(self, s):
        sb = self.sb
        self.w_b1 = sb(s, "w_b1", [P, 2, 4])
        self.w_b2 = sb(s, "w_b2", [P, 2, D])
        self.e_rows = sb(s, "e_rows", [P, SUB, D])
        self.e_x = sb(s, "e_x", [P, 2, 2, DT, BL], F32R)
        self.e_act = sb(s, "e_act", [P, 2, BL])
        self.e_h = sb(s, "e_h", [P, 2, BL])
        self.e_hl = sb(s, "e_hl", [P, 2, 8, BL], F32R)
        self.e_y = sb(s, "e_y", [P, 2, SUB, D])
        self.w_stage = sb(s, "w_stage", [P, 2, 2048])
        self.w_hi = sb(s, "w_hi", [P, 2, 3 * 2048], F32R)
        self.w_lo = sb(s, "w_lo", [P, 2, 3 * 2048], F32R)

    def program(self):
        stages = [self.load_constants, self.s4_tokens, self.tokens_to_rows]
        for layer in range(2):
            stages += [lambda layer=layer: self.layernorm(f"a{layer}", True),
                       lambda layer=layer: self.attention(layer),
                       lambda layer=layer: self.layernorm(f"f{layer}", False),
                       lambda layer=layer: self.router(layer),
                       lambda layer=layer: self.experts(layer)]
        stages = stages[:self.stop]
        stages.append(self.write_out)
        nc = self.nc
        parts, spent, self.free = [], [], []
        for s in stages:
            self.used = []
            parts.append(s())
            self.free += spent[-2] if len(spent) > 1 else []
            spent.append(self.used)

        def run(eng, name):
            for n, part in enumerate(parts):
                if name == "sp" and 0 < n < len(parts) - 1:
                    for s in spent[n - 1]:
                        eng.sem_clear(s)
                if name in part:
                    part[name](eng)
                if n < len(parts) - 1:
                    eng.drain().then_inc(self.stage_done, 1)
                    eng.wait_ge(self.stage_done, 5 * (n + 1))

        with nc.Block() as block:
            @block.sync
            def _(sp):
                run(sp, "sp")

            @block.gpsimd
            def _(pool):
                run(pool, "pool")

            @block.scalar
            def _(act):
                run(act, "act")

            @block.vector
            def _(dve):
                run(dve, "dve")

            @block.tensor
            def _(pe):
                run(pe, "pe")

    def load_constants(self):
        A, X = self.A, self.X
        cls_loaded, cleared = self.sem("cls_loaded"), self.sem("cleared")

        def sp(e):
            e.dma_start(self.s4_small[:], A["s4_small"]).then_inc(self.loaded, 16)
            e.dma_start(self.s4_c[:], A["s4_c"]).then_inc(self.loaded, 16)
            e.dma_start(self.cst[:], A["consts"]).then_inc(self.loaded, 16)
            e.wait_ge(cleared, 2)
            e.dma_start(X[0:NB, NT - 1, :], A["cls"].to_broadcast([NB, D])).then_inc(cls_loaded, 16)
            zero = self.s4_zero[:].unsqueeze(1)
            e.dma_start(self.rows_in.rearrange("(n p) d -> p n d", p=P),
                        zero.to_broadcast([P, SLOTS // P, D])).then_inc(self.rows_cleared, 16)
            e.wait_ge(self.loaded, 48)
            e.wait_ge(cls_loaded, 16)

        def pool(e):
            e.memset(X[:, NT - 1], 0.0).then_inc(cleared, 1)
            e.memset(self.s4_zero[:], 0.0).then_inc(cleared, 1)
        return {"sp": sp, "pool": pool}

    def s4_tokens(self):
        small, c, w, tmp, cb, prod = self.s4_small, self.s4_c, self.s4_w, self.s4_tmp, self.s4_cb, self.s4_prod
        pw, v, t, kern, psS = self.s4_p, self.s4_v, self.s4_t, self.s4_k, self.psS
        own_dve, own_pool = self.sem("s4_own_dve"), self.sem("s4_own_pool")
        w_ready, zeroed = self.sem("s4_w_ready"), self.sem("s4_zeroed")
        p_ready = self.sem("s4_p_ready")
        v_dve, v_pool = self.sem("s4_v_dve"), self.sem("s4_v_pool")
        k_ready, k_moved = self.sem("s4_k_ready"), self.sem("s4_k_moved")
        CREDIT = 2

        def act(e):
            for _ in range(CREDIT):
                e.nop().then_inc(k_moved, 1)
            with e.Fori(0, S4_NB // 2) as i:
                for s in range(2):
                    blk = i * 2 + s
                    e.wait_ge(k_ready, blk + 1 + CREDIT)
                    for a in range(2):
                        dst = kern[:, a].rearrange("p (c g h) -> p c g h", c=NB, g=2)[:, :, :, bass.ds(blk * S4_HP, S4_HP)]
                        src = psS[:, s, :].rearrange("p (h g a c) -> p a c g h", g=2, a=2, c=NB)[:, a]
                        last = e.activation(dst, src, ACT.Copy)
                    last.then_inc(k_moved, 1)

        def powers(e, own, first, count, slot, blk):
            a, z = first, first + count

            def wk(k, ri, width):
                return w[:, k, ri, bass.ds(blk * S4_HP + first, count)].unsqueeze(2).to_broadcast([P, count, width])

            own.did(e.tensor_copy(v[:, slot, 0, a:z, 1:2], wk(0, 0, 1)))
            own.did(e.tensor_copy(v[:, slot, 1, a:z, 1:2], wk(0, 1, 1)))
            for k in range(1, 7):
                n = 1 << k
                own.wait()
                re, im = v[:, slot, 0, a:z, 0:n], v[:, slot, 1, a:z, 0:n]
                own.did(e.tensor_tensor(t[:, 0, a:z, 0:n], re, wk(k, 0, n), ALU.mult))
                own.did(e.tensor_tensor(t[:, 1, a:z, 0:n], im, wk(k, 1, n), ALU.mult))
                own.wait()
                own.did(e.tensor_tensor(v[:, slot, 0, a:z, n:2 * n], t[:, 0, a:z, 0:n], t[:, 1, a:z, 0:n], ALU.subtract))
                own.wait()
                own.did(e.tensor_tensor(t[:, 0, a:z, 0:n], re, wk(k, 1, n), ALU.mult))
                own.did(e.tensor_tensor(t[:, 1, a:z, 0:n], im, wk(k, 0, n), ALU.mult))
                own.wait()
                last = e.tensor_tensor(v[:, slot, 1, a:z, n:2 * n], t[:, 0, a:z, 0:n], t[:, 1, a:z, 0:n], ALU.add)
                if k < 6:
                    own.did(last)
            return last

        PER = 2 + 6 * 6 - 1

        def dve(e):
            own = Own(e, own_dve)

            def tt(out, a, b, op):
                own.did(e.tensor_tensor(out, a, b, op))

            def exponential():
                x = small[:, 2:5:2]
                k, r, q, two = (prod[:, 0, 2 * n:2 * n + 2] for n in range(4))
                ROUND = 1.5 * 2.0 ** 23
                LN2_HI, LN2_LO = 355.0 / 512.0, -2.12194440054690583e-4

                def step(ins):
                    own.did(ins)
                    own.wait()
                step(e.tensor_scalar(k, x, 1.0 / float(np.log(2.0)), ROUND, ALU.mult, ALU.add))
                step(e.tensor_scalar(k, k, -ROUND, -126.0, ALU.add, ALU.max))
                step(e.tensor_scalar(k, k, 127.0, None, ALU.min))
                step(e.scalar_tensor_tensor(r, k, -LN2_HI, x, ALU.mult, ALU.add))
                step(e.scalar_tensor_tensor(r, k, -LN2_LO, r, ALU.mult, ALU.add))
                fact = [1.0]
                for n in range(1, 9):
                    fact.append(fact[-1] * n)
                step(e.tensor_scalar(q, r, 1.0 / fact[8], None, ALU.mult))
                for n in range(7, 0, -1):
                    step(e.scalar_tensor_tensor(q, q, 1.0 / fact[n], r, ALU.add, ALU.mult))
                step(e.tensor_scalar(two.bitcast(mybir.dt.int32), k, 127.0, 2.0 ** 23, ALU.add, ALU.mult))
                step(e.scalar_tensor_tensor(x, q, 1.0, two, ALU.add, ALU.mult))

            exponential()
            bre, bim, ar, ai, dt = (small[:, n] for n in range(5))
            zr, zi, zr2, zi2, mag, num, omz, den = (tmp[:, n] for n in range(8))
            own.did(e.scalar_tensor_tensor(zr, ar, -0.5, dt, ALU.mult, ALU.mult))
            own.did(e.scalar_tensor_tensor(zi, ai, 0.5, dt, ALU.mult, ALU.mult))
            own.wait()
            tt(zr2, zr, zr, ALU.mult)
            tt(zi2, zi, zi, ALU.mult)
            own.did(e.tensor_scalar(omz, zr, -1.0, 1.0, ALU.mult, ALU.add))
            own.wait()
            tt(mag, zr2, zi2, ALU.add)
            tt(den, omz, omz, ALU.mult)
            own.wait()
            own.did(e.tensor_scalar(num, mag, -1.0, 1.0, ALU.mult, ALU.add))
            tt(den, den, zi2, ALU.add)
            own.wait()
            own.did(e.reciprocal(omz, den))
            own.wait()
            tt(w[:, 0, 0], num, omz, ALU.mult)
            own.did(e.scalar_tensor_tensor(w[:, 0, 1], zi, 2.0, omz, ALU.mult, ALU.mult))
            own.wait()
            for k in range(1, 8):
                r, i = w[:, k - 1, 0], w[:, k - 1, 1]
                tt(zr2, r, r, ALU.mult)
                tt(zi2, i, i, ALU.mult)
                own.did(e.scalar_tensor_tensor(w[:, k, 1], r, 2.0, i, ALU.mult, ALU.mult))
                own.wait()
                if k < 7:
                    tt(w[:, k, 0], zr2, zi2, ALU.subtract)
                    own.wait()
            e.tensor_tensor(w[:, 7, 0], zr2, zi2, ALU.subtract).then_inc(w_ready, 1)
            e.wait_ge(w_ready, 1)

            def cmul(out_re, out_im, xr, xi, yr, yi):
                for out, (a1, b1), (a2, b2), op in ((out_re, (xr, yr), (xi, yi), ALU.subtract),
                                                    (out_im, (xr, yi), (xi, yr), ALU.add)):
                    tt(prod[:, 0], a1, b1, ALU.mult)
                    tt(prod[:, 1], a2, b2, ALU.mult)
                    own.wait()
                    tt(out, prod[:, 0], prod[:, 1], op)
                    own.wait()

            def wide(x):
                return x.unsqueeze(1).to_broadcast([P, NB, P])
            cmul(cb[:, 0, 0], cb[:, 0, 1], c[:, 0], c[:, 1], wide(bre), wide(bim))
            cmul(cb[:, 1, 0], cb[:, 1, 1], cb[:, 0, 0], cb[:, 0, 1], wide(w[:, 7, 0]), wide(w[:, 7, 1]))
            e.wait_ge(zeroed, 4)
            for a in range(2):
                for ri, scale in ((0, 2.0), (1, -2.0)):
                    for h in range(2):
                        q = slice(64 * h, 64 * h + 64)
                        last = e.tensor_scalar(pw[q, ri, :, h, a, :].rearrange("p h c -> p c h"), cb[q, a, ri], scale, None, ALU.mult)
            last.then_inc(p_ready, 1)
            with e.Fori(0, S4_NB // 2) as i:
                own.enter(i, 2 * PER)
                for s in range(2):
                    blk = i * 2 + s
                    e.wait_ge(k_ready, blk - 1 + CREDIT)
                    powers(e, own, 0, S4_DVE, s, blk).then_inc(v_dve, 1)
                own.leave(S4_NB // 2)

        def pool(e):
            own = Own(e, own_pool, apart=self.paced)
            e.memset(pw[:, 0], 0.0).then_inc(zeroed, 1)
            e.memset(pw[:, 1], 0.0).then_inc(zeroed, 1)
            e.memset(v[:, :, 0, :, 0:1], 1.0).then_inc(zeroed, 1)
            e.memset(v[:, :, 1, :, 0:1], 0.0).then_inc(zeroed, 1)
            e.wait_ge(zeroed, 4)
            e.wait_ge(w_ready, 1)
            with e.Fori(0, S4_NB // 2) as i:
                own.enter(i, 2 * PER)
                for s in range(2):
                    e.wait_ge(k_ready, i * 2 + s - 1 + CREDIT)
                    e.nop().then_inc(self.paced, 1)
                    powers(e, own, S4_DVE, S4_HP - S4_DVE, s, i * 2 + s).then_inc(v_pool, 1)
                own.leave(S4_NB // 2)

        def pe(e):
            for _ in range(CREDIT):
                e.nop().then_inc(k_ready, 1)
            e.wait_ge(p_ready, 1)
            with e.Fori(0, S4_NB // 2) as i:
                for s in range(2):
                    blk = i * 2 + s
                    e.wait_ge(v_dve, blk + 1)
                    e.wait_ge(v_pool, blk + 1)
                    e.wait_ge(k_moved, blk - 1 + CREDIT)
                    for h in range(S4_HP):
                        for ri in range(2):
                            rhs = pw[:, ri, bass.ds(blk * S4_HP + h, 1)].rearrange("p h g a c -> p (h g a c)")
                            last = e.matmul(psS[:, s, 32 * h:32 * h + 32], v[:, s, ri, h, :], rhs,
                                            start=(ri == 0), stop=(ri == 1))
                    last.then_inc(k_ready, 1)
        return {"act": act, "dve": dve, "pool": pool, "pe": pe}

    def tokens_to_rows(self):
        turned, moved = self.sem("tr_turned"), [self.sem("tr_moved_act"), self.sem("tr_moved_dve")]

        def pe(e):
            for n in range(NT - 1):
                if n >= 4:
                    e.wait_ge(moved[n % 2], (n - 4) // 2 + 1)
                for dt in range(DT):
                    m = e.transpose(self.psS[:, n % 4, P * dt:P * dt + P], self.s4_k[:, dt, P * n:P * n + P], self.const("ident"))
                m.then_inc(turned, 1)

        def mover(which):
            def run(e):
                for n in range(which, NT - 1, 2):
                    e.wait_ge(turned, n + 1)
                    src = self.psS[:, n % 4, 0:D]
                    m = e.activation(self.X[:, n], src, ACT.Copy) if which == 0 else e.tensor_copy(self.X[:, n], src)
                    m.then_inc(moved[which], 1)
            return run

        def sp(e):
            e.wait_ge(self.rows_cleared, 16)
        return {"pe": pe, "act": mover(0), "dve": mover(1), "sp": sp}

    def layernorm(self, tag, for_attention):
        X, psS, psT = self.X, self.psS, self.psT
        stat, mv, sd, rows = self.n_stat, self.n_mv, self.n_sd, self.n_rows
        stats, moments, rooted, own_sem, normed, turned, moved_act, moved_dve = (
            self.sem(f"ln{tag}_{n}") for n in ("stats", "moments", "rooted", "own", "normed", "turned", "moved_act",
                                               "moved_dve"))
        NG = (NT + 1) // 2
        BK = [psS[:, n, :] for n in range(4)] + [psT[:, n, :] for n in range(2)]

        def tiles(g):
            return range(2 * g, min(2 * g + 2, NT))

        def group(buf, g):
            w = len(tiles(g))
            return buf[:, :, 2 * P * g:2 * P * g + P * w].rearrange("p a (n t) -> p n a t", t=P)

        def bank(g):
            w = len(tiles(g))
            return BK[g % 6][:, 0:2 * P * w].rearrange("p (n a t) -> p n a t", a=DT, t=P)

        def pe(e):
            for g in range(NG):
                if g >= 6:
                    for m in ((moved_act, moved_dve)[(g - 6) % 2],) if for_attention else (moved_dve,):
                        e.wait_ge(m, (g - 6) // 2 + 1 if for_attention else g - 5)
                for n in tiles(g):
                    e.wait_ge(normed, n + 1)
                    for dt in range(DT):
                        at = 2 * P * (n % 2) + P * dt
                        m = e.transpose(BK[g % 6][:, at:at + P], rows[:, n, P * dt:P * dt + P], self.const("ident"))
                m.then_inc(turned, 1)

        def act(e):
            e.wait_ge(moments, NT)
            e.activation(sd[:, :, 0:1], mv[:, :, 1:2], ACT.Sqrt, bias=self.const("eps")).then_inc(rooted, 1)
            for g in range(0, NG, 2 if for_attention else 1):
                e.wait_ge(turned, g + 1)
                dst = group(self.xn, g) if for_attention else group(self.x_hl[:, 0], g)
                e.activation(dst, bank(g), ACT.Copy).then_inc(moved_act, 1)

        def dve(e):
            own = Own(e, own_sem)
            for n in range(NT):
                e.bn_stats(stat[:, n], X[:, n]).then_inc(stats, 1)
            for n in range(NT):
                e.wait_ge(stats, n + 1)
                e.bn_aggr(mv[:, n], stat[:, n]).then_inc(moments, 1)
            e.wait_ge(rooted, 1)
            own.did(e.reciprocal(sd[:, :, 1:2], sd[:, :, 0:1]))
            own.wait()
            for n in range(NT):
                e.tensor_scalar(rows[:, n], X[:, n], mv[:, n, 0:1], sd[:, n, 1:2], ALU.subtract, ALU.mult).then_inc(normed, 1)
            for g in range(1 if for_attention else 0, NG, 2 if for_attention else 1):
                if for_attention:
                    e.wait_ge(turned, g + 1)
                    e.tensor_copy(group(self.xn, g), bank(g)).then_inc(moved_dve, 1)
                else:
                    e.wait_ge(moved_act, g + 1)
                    e.tensor_tensor(group(self.x_hl[:, 1], g), bank(g), group(self.x_hl[:, 0], g).bitcast(F32),
                                    ALU.subtract).then_inc(moved_dve, 1)

        return {"pe": pe, "act": act, "dve": dve}

    def attention(self, L):
        A, X, psS, psT, psY = self.A, self.X, self.psS, self.psT, self.psY
        full = L == 1
        NK = T if full else T - 1
        K0 = 0 if full else 1
        S = {n: self.sem(f"at{L}_{n}") for n in (
            "R", "clsy", "exp", "image_done", "max", "moved", "out", "own_dve", "own_pool",
            "pex", "prep", "proj", "pt", "pv", "qm", "rope_add", "rs", "scores",
            "tailC", "tailT", "turned", "w_ready", "x_ready", "y", "yadd", "yn")}

        def sem(n):
            return S[n]
        w, wo, bb, bv = self.a_w, self.a_wo, self.a_b, self.a_bv
        q, qm, qc, k, v, vc = self.a_q, self.a_qm, self.a_qc, self.a_k, self.a_v, self.a_vc
        prob, pt, nm = self.a_p, self.a_pt, self.a_nm
        NW = 768 if full else 1280
        w_ready, prep = sem("w_ready"), sem("prep")
        NPREP = 5 if full else 6
        BANKS = [psS[:, n, :] for n in range(4)] + [psT[:, n, :] for n in range(2)] + [psY[:, n, :] for n in range(2)]
        if full:
            units = [("q", t, 128 * t) for t in range(2)] + [("k", t, 256 + 128 * t) for t in range(2)]
            vcol = 512
        else:
            units = [(n, t, 256 * m + 128 * t) for t in range(2) for m, n in enumerate(("q", "qs"))]
            units += [(n, t, 512 + 256 * m + 128 * t) for t in range(2) for m, n in enumerate(("k", "ks"))]
            vcol = 1024
        units += [("v", t, vcol) for t in range(QT)] + ([("vc", 0, vcol)] if full else [])
        NU = len(units)
        NH = HEADS + (1 if full else 0)
        SUM_GUARD = 1e-20

        def sp(e):
            e.dma_start(w[:, :, 0:NW], A[f"w_qkv{L}"]).then_inc(w_ready, 16)
            e.dma_start(wo[:], A[f"w_o{L}"]).then_inc(w_ready, 16)
            if not full:
                e.dma_start(self.a_table[:], A["rope_mask"]).then_inc(w_ready, 16)
            if full:
                e.dma_start(bb[:], A["a_bias"]).then_inc(w_ready, 16)
                e.dma_start(bv[:], A["a_bv"].to_broadcast([P, D])).then_inc(w_ready, 16)
                e.dma_start(self.a_bo[:], A["a_bo"].to_broadcast([P, D])).then_inc(w_ready, 16)

        WR = 80 if full else 48

        def batch_end(e, b):
            e.drain().then_inc(sem("image_done"), 1)
            e.wait_ge(sem("image_done"), b * 4 + 4)

        def pool(e):
            own = Own(e, sem("own_pool"), apart=self.paced)
            e.wait_ge(w_ready, WR)
            for m in (v, vc, self.a_rst, self.a_pext):
                e.memset(m[:], 0.0).then_inc(prep, 1)
            with e.Fori(0, NB) as b:
                own.enter(b, 2)
                own.did(e.tensor_copy(self.a_x[:, :, 1:T], self.xn[:, :, bass.ds(b * 256, 256)]))
                own.did(e.tensor_copy(self.a_x[:, :, 0:1], self.xn[:, :, bass.ds(b + 2048, 1)]))
                own.wait()
                e.tensor_copy(self.a_xc[:], self.a_x[:, :, 0:1].to_broadcast([P, DT, 16])).then_inc(sem("x_ready"), 1)
                if not full:
                    for n in range(4):
                        e.wait_ge(sem("moved"), b * NU + 2 * n + 2)
                        e.nop().then_inc(self.paced, 1)
                        dst = (q if n < 2 else k)[:, n % 2, 1:T]
                        e.tensor_tensor(dst, self.a_rope[:, n % 2, 0], self.a_rope[:, n % 2, 1], ALU.add).then_inc(sem("rope_add"), 1)
                else:
                    for u in range(HEADS):
                        e.wait_ge(sem("exp"), b * NH + u + 1)
                        e.nop().then_inc(self.paced, 1)
                        e.tensor_copy(self.a_pex[:, :, u:u + 1], prob[:, u % 2, :, 0:1]).then_inc(sem("pex"), 1)
                batch_end(e, b)
                own.leave(NB)

        def pe(e):
            e.wait_ge(w_ready, WR)
            e.wait_ge(prep, NPREP)
            ident = self.const("ident")
            with e.Fori(0, NB) as b:
                e.wait_ge(sem("x_ready"), b + 1)
                for n, (name, t, col) in enumerate(units):
                    if n >= 8:
                        e.wait_ge(sem("moved"), b * NU + n - 7)
                    for dt in range(DT):
                        st, sp_ = dt == 0, dt == DT - 1
                        if name == "v":
                            m = e.matmul(BANKS[n % 8][:, 0:D], self.a_x[:, dt, 1 + 128 * t:129 + 128 * t],
                                         w[:, dt, col:col + D], start=st, stop=sp_)
                        elif name == "vc":
                            m = e.matmul(BANKS[n % 8][0:16, 0:D], self.a_xc[:, dt], w[:, dt, col:col + D], start=st, stop=sp_)
                        else:
                            m = e.matmul(BANKS[n % 8][:, 0:NK], w[:, dt, col:col + P], self.a_x[:, dt, K0:T], start=st, stop=sp_)
                    m.then_inc(sem("proj"), 1)

                def scores(u):
                    s = u % 2
                    if u < HEADS:
                        e.wait_ge(sem("qm"), b * NH + u + 1)
                        if u < 2:
                            e.wait_ge(sem("moved"), b * NU + NU)
                            if not full:
                                e.wait_ge(sem("rope_add"), b * 4 + 4)
                        else:
                            e.wait_ge(sem("exp"), b * NH + u - 1)
                        for i in range(QT):
                            out = psS[:, 2 * s + i, 0:NK]
                            if not full:
                                e.matmul(out, self.a_identb[:], self.a_maskb[:, i], start=True, stop=False)
                            m = e.matmul(out, qm[:, u, 128 * i:128 * i + 128], k[:, u // 8, K0:T], start=full, stop=True)
                    else:
                        e.wait_ge(sem("qm"), b * NH + u + 1)
                        e.wait_ge(sem("exp"), b * NH + u - 1)
                        for t in range(2):
                            m = e.matmul(psS[0:16, 2 * s, 0:NK], qc[:, t], k[:, t, 0:T], start=t == 0, stop=t == 1)
                    m.then_inc(sem("scores"), 1)

                def turn(u):
                    s = u % 2
                    e.wait_ge(sem("exp"), b * NH + u + 1)
                    if u >= 2:
                        e.wait_ge(sem("pt"), b * NH + u - 1)
                    if u == HEADS:
                        e.nop().then_inc(self.paced, 1)
                    if u < HEADS:
                        for kt in range(2):
                            for i in range(QT):
                                at = kt * 256 + i * 128
                                m = e.transpose(psT[:, s, at:at + 128], prob[:, s, i, K0 * 0 + (NK - 256) + 128 * kt:(NK - 256) + 128 * kt + 128], ident)
                    else:
                        for kt in range(2):
                            m = e.transpose(psT[:, s, 16 * kt:16 * kt + 16], self.a_pc[:, 1 + 128 * kt:129 + 128 * kt], ident[0:16, 0:16])
                    m.then_inc(sem("turned"), 1)

                def values(g):
                    e.wait_ge(sem("pt"), b * NH + 4 * g + 4)
                    if g >= 2:
                        e.wait_ge(sem("y"), b * 4 + g - 1)
                    for kt in range(2):
                        for j in range(GRP):
                            h = GRP * g + j
                            m = e.matmul(psY[32 * j:32 * j + 32, g % 2, 0:256], v[:, kt, 32 * h:32 * h + 32],
                                         pt[:, h % 8, 256 * kt:256 * kt + 256], start=kt == 0, stop=kt == 1)
                    m.then_inc(sem("pv"), 1)

                for u in range(NH + 3):
                    if u < NH:
                        scores(u)
                    if 1 <= u <= NH:
                        turn(u - 1)
                    if u >= 5 and (u - 5) % 4 == 0 and (u - 5) // 4 < 4:
                        values((u - 5) // 4)
                e.wait_ge(sem("rs"), b + 1)
                e.wait_ge(sem("pt"), b * NH + NH)
                for i in range(QT):
                    m = e.transpose(psT[0:16, 0, 128 * i:128 * i + 128], self.a_rs[:, i, :], ident)
                if full:
                    e.wait_ge(sem("pex"), b * HEADS + HEADS)
                    for i in range(QT):
                        m = e.transpose(psT[0:16, 1, 128 * i:128 * i + 128], self.a_pex[:, i, :], ident)
                m.then_inc(sem("tailT"), 1)
                if full:
                    e.wait_ge(sem("y"), b * 4 + 4)
                    for g in range(4):
                        for kt in range(2):
                            m = e.matmul(psY[:, 0, 16 * g:16 * g + 16], v[:, kt, P * g:P * g + P], self.a_pct[:, kt], start=kt == 0, stop=kt == 1)
                    m.then_inc(sem("clsy"), 1)
                e.wait_ge(sem("tailC"), b + 1)
                e.wait_ge(sem("exp"), b * NH + NH)
                for g in range(4):
                    if g >= 2:
                        e.wait_ge(sem("yn"), b * 4 + g - 1)
                    m = e.matmul(psS[:, 2 + g % 2, 0:T], self.const("spread")[:, P * g:P * g + P], self.a_rst[:], start=True, stop=True)
                    if full:
                        m = e.matmul(psS[:, g % 2, 0:T], vc[:, P * g:P * g + P], self.a_pext[:], start=True, stop=True)
                    m.then_inc(sem("R"), 1)
                e.wait_ge(sem("yn"), b * 4 + 4)
                e.wait_ge(sem("y"), b * 4 + 4)
                for i in range(QT):
                    for g in range(4):
                        m = e.matmul(psY[:, i, 0:D], self.a_yn[:, g, 1 + P * i:1 + P * i + P], wo[:, g], start=g == 0, stop=g == 3)
                m.then_inc(sem("out"), 1)
                batch_end(e, b)
            if full:
                for g in range(4):
                    m = e.matmul(psY[0:NB, 0, 0:D], self.a_ycls[:, g], wo[:, g], start=g == 0, stop=g == 3)
                m.then_inc(sem("out"), 1)

        def act(e):
            with e.Fori(0, NB) as b:
                def y_out(g):
                    e.wait_ge(sem("pv"), b * 4 + g + 1)
                    e.activation(self.a_y[:, g, 1:T], psY[:, g % 2, 0:256], ACT.Copy).then_inc(sem("y"), 1)
                for u in range(NH):
                    s = u % 2
                    e.wait_ge(sem("max"), b * NH + u + 1)
                    if u >= 2:
                        e.wait_ge(sem("turned"), b * NH + u - 1)
                        if full:
                            e.wait_ge(sem("pex"), b * HEADS + min(u - 1, HEADS))
                    if u < HEADS:
                        for i in range(QT):
                            m = e.activation(prob[:, s, i, 0:NK], psS[:, 2 * s + i, 0:NK], ACT.Exp,
                                             bias=nm[:, u, i:i + 1], accum_out=self.a_sum[:, i, u:u + 1])
                    else:
                        m = e.activation(self.a_pc[:, 0:NK], psS[0:16, 2 * s, 0:NK], ACT.Exp,
                                         bias=nm[0:16, u, 0:1], accum_out=self.a_rsc[:, 0:1])
                    m.then_inc(sem("exp"), 1)
                    if u >= 6 and (u - 6) % 4 == 0 and u < 15:
                        y_out((u - 6) // 4)
                y_out(3) if True else None
                batch_end(e, b)

        def dve(e):
            own = Own(e, sem("own_dve"))
            e.wait_ge(w_ready, WR)
            if not full:
                e.tensor_copy(self.a_maskb[:], self.table("maskq").rearrange("p (i k) -> p i k", i=QT)).then_inc(prep, 1)
                e.tensor_copy(self.a_identb[:], self.const("ident")).then_inc(prep, 1)
            if full:
                e.tensor_scalar(bb[:, 0:2], bb[:, 0:2], 0.25, None, ALU.mult).then_inc(prep, 1)
            e.wait_ge(prep, NPREP)
            mask8 = self.const("headmask")
            with e.Fori(0, NB) as b:
                per = 9 if full else 4
                own.enter(b, per)

                def head_queries(t):
                    for j in range(8):
                        e.tensor_scalar(qm[:, 8 * t + j], q[:, t, 1:T], mask8[:, j:j + 1], None, ALU.mult).then_inc(sem("qm"), 1)

                for n, (name, t, _) in enumerate(units):
                    e.wait_ge(sem("proj"), b * NU + n + 1)
                    bank = BANKS[n % 8]
                    if name == "v":
                        dst = v[:, t].rearrange("p (h s) -> p h s", s=32)[:, :, 0:HD]
                        src = bank[:, 0:D].rearrange("p (h s) -> p h s", s=HD)
                        if full:
                            m = e.tensor_tensor(dst, src, bv[:].rearrange("p (h s) -> p h s", s=HD), ALU.add)
                        else:
                            m = e.tensor_copy(dst, src)
                    elif name == "vc":
                        own.did(e.tensor_tensor(self.a_vt[:], bank[0:16, 0:D], bv[0:16, :], ALU.add))
                        own.wait()
                        m = e.tensor_tensor(vc[0:16, :].rearrange("p (h s) -> p h s", s=32)[:, :, 0:HD],
                                            self.a_vt[:].rearrange("p (h s) -> p h s", s=HD),
                                            self.const("diag")[0:16, :].unsqueeze(2).to_broadcast([16, HEADS, HD]), ALU.mult)
                    elif full:
                        dst = (q if name == "q" else k)[:, t]
                        if name == "q":
                            m = e.tensor_scalar(dst, bank[:, 0:T], 0.25, bb[:, t:t + 1], ALU.mult, ALU.add)
                        else:
                            m = e.tensor_scalar(dst, bank[:, 0:T], bb[:, 2 + t:3 + t], None, ALU.add)
                    else:
                        r = 0 if name[0] == "q" else 2
                        if len(name) == 1 and r + t >= 2:
                            e.wait_ge(sem("rope_add"), b * 4 + r + t - 1)
                        tab = self.table(("c" if len(name) == 1 else "s") + name[0])
                        m = e.tensor_tensor(self.a_rope[:, t, len(name) - 1], bank[:, 0:256], tab, ALU.mult)
                    m.then_inc(sem("moved"), 1)
                    if full and name == "q":
                        e.wait_ge(sem("moved"), b * NU + n + 1)
                        head_queries(t)
                    if not full and name == "ks":
                        e.wait_ge(sem("rope_add"), b * 4 + t + 1)
                        head_queries(t)
                if not full:
                    e.wait_ge(sem("rope_add"), b * 4 + 4)
                if full:
                    e.tensor_tensor(qc[:], q[:, :, 0:1].to_broadcast([P, DT, 16]),
                                    self.const("clsheads").rearrange("p (t h) -> p t h", t=2), ALU.mult).then_inc(sem("qm"), 1)
                for u in range(NH + 1):
                    if u < NH:
                        s = u % 2
                        e.wait_ge(sem("scores"), b * NH + u + 1)
                        if u < HEADS:
                            e.tensor_reduce(nm[:, u, :], psS[:, 2 * s:2 * s + 2, 0:NK], AX, ALU.max, negate=True).then_inc(sem("max"), 1)
                        else:
                            e.tensor_reduce(nm[0:16, u, 0:1], psS[0:16, 2 * s, 0:NK], AX, ALU.max, negate=True).then_inc(sem("max"), 1)
                    if u >= 1:
                        h = u - 1
                        e.wait_ge(sem("turned"), b * NH + u)
                        if h < HEADS:
                            if h >= 8:
                                e.wait_ge(sem("pv"), b * 4 + (h - 8) // 4 + 1)
                            e.tensor_copy(pt[:, h % 8], psT[:, h % 2, :]).then_inc(sem("pt"), 1)
                        else:
                            e.tensor_copy(self.a_pct[:].rearrange("p k h -> p (k h)"), psT[:, h % 2, 0:32]).then_inc(sem("pt"), 1)
                e.wait_ge(sem("exp"), b * NH + NH)
                own.did(e.tensor_scalar(self.a_rs[:], self.a_sum[:], SUM_GUARD, None, ALU.max))
                own.wait()
                own.did(e.reciprocal(self.a_rs[:], self.a_rs[:]))
                own.wait()
                if full:
                    m = e.reciprocal(self.a_rsc[:, 1:2], self.a_rsc[:, 0:1])
                else:
                    m = e.tensor_tensor(self.a_rs[:], self.a_rs[:],
                                        self.const("valid").unsqueeze(2).to_broadcast([P, QT, HEADS]), ALU.mult)
                m.then_inc(sem("rs"), 1)
                e.wait_ge(sem("tailT"), b + 1)
                if full:
                    e.wait_ge(sem("rs"), b + 1)
                    e.tensor_copy(self.a_rst[0:16, 0:1], self.a_rsc[:, 1:2])
                    e.tensor_copy(self.a_pext[0:16, 1:T], psT[0:16, 1, 0:256])
                    e.tensor_copy(self.a_pext[0:16, 0:1], self.a_pc[:, 0:1])
                e.tensor_copy(self.a_rst[0:16, 1:T], psT[0:16, 0, 0:256]).then_inc(sem("tailC"), 1)
                if full:
                    e.wait_ge(sem("clsy"), b + 1)
                    own.did(e.tensor_tensor(self.a_yc[:], psY[:, 0, 0:64].rearrange("p (g h) -> p g h", h=16),
                                            self.const("clspick").rearrange("p (g h) -> p g h", h=16), ALU.mult))
                    own.wait()
                    own.did(e.tensor_reduce(self.a_y[:, :, 0:1], self.a_yc[:], AX, ALU.add))
                    own.wait()
                e.wait_ge(sem("y"), b * 4 + 4)
                for g in range(4):
                    e.wait_ge(sem("R"), b * 4 + g + 1)
                    if full:
                        if g >= 1:
                            pass
                        e.tensor_tensor(self.a_y[:, g], self.a_y[:, g], psS[:, g % 2, 0:T], ALU.add).then_inc(sem("yadd"), 1)
                        e.wait_ge(sem("yadd"), b * 4 + g + 1)
                        e.tensor_tensor(self.a_yn[:, g], self.a_y[:, g], psS[:, 2 + g % 2, 0:T], ALU.mult).then_inc(sem("yn"), 1)
                    else:
                        e.tensor_tensor(self.a_yn[:, g, 1:T], self.a_y[:, g, 1:T], psS[:, 2 + g % 2, 1:T], ALU.mult).then_inc(sem("yn"), 1)
                if full:
                    e.wait_ge(sem("yn"), b * 4 + 4)
                    e.tensor_copy(self.a_ycls[:, :, bass.ds(b, 1)], self.a_yn[:, :, 0:1])
                e.wait_ge(sem("out"), b + 1)
                for i in range(QT):
                    dst = X[:, bass.ds(b * 2 + i, 1)].rearrange("p o d -> p (o d)")
                    m = own.did(e.tensor_tensor(dst, psY[:, i, 0:D], dst, ALU.add))
                if full:
                    own.wait()
                    for i in range(QT):
                        dst = X[:, bass.ds(b * 2 + i, 1)].rearrange("p o d -> p (o d)")
                        own.did(e.tensor_tensor(dst, dst, self.a_bo[:], ALU.add))
                batch_end(e, b)
                own.leave(NB)
            if full:
                e.wait_ge(sem("out"), NB + 1)
                dst = X[0:NB, NT - 1]
                own.did(e.tensor_tensor(dst, psY[0:NB, 0, 0:D], dst, ALU.add))
                own.wait()
                own.did(e.tensor_tensor(dst, dst, self.a_bo[0:NB], ALU.add))
        return {"sp": sp, "pool": pool, "pe": pe, "act": act, "dve": dve}

    def router(self, L):
        A, psT, psS = self.A, self.psT, self.psS
        S = {n: self.sem(f"rt{L}_{n}") for n in ("w", "split", "logits", "own", "shift", "exp", "picked", "counted",
                                                   "placed")}

        weights_sp, weights_act, weights_pool = self.first_weights(L)

        def sp(e):
            e.dma_start(self.r_w[:], A[f"router{L}"]).then_inc(S["w"], 16)
            e.dma_start(self.r_b[:], A[f"router_b{L}"]).then_inc(S["w"], 16)
            weights_sp(e)

        def pe(e):
            e.wait_ge(S["split"], 2)
            for n in range(NT):
                for c, (i, j) in enumerate([(x, y) for x in range(DT) for y in range(3)]):
                    xa, wa = ((0, 0), (0, 1), (1, 0))[j]
                    m = e.matmul(psT[:, 0, E * n:E * n + E], self.x_hl[:, xa, i, P * n:P * n + P],
                                 self.r_hl[:, wa, E * i:E * i + E], start=c == 0, stop=c == 5)
            m.then_inc(S["logits"], 1)
            e.wait_ge(S["picked"], 1)
            sel = self.g_sel[:].rearrange("p n e -> p (n e)")
            e.matmul(psS[:, 0, 0:NT * E], self.const("before"), sel, start=True, stop=True)
            e.matmul(psS[:, 1, 0:NT * E], self.const("ones"), sel, start=True, stop=True).then_inc(S["counted"], 1)

        def act(e):
            e.wait_ge(S["shift"], 1)
            e.activation(self.g_p[:], self.g_p[:], ACT.Exp).then_inc(S["exp"], 1)
            weights_act(e)

        def dve(e):
            own = Own(e, S["own"])
            p, sel, m4, cmp_, tmp = self.g_p, self.g_sel, self.g_m, self.g_cmp, self.g_tmp

            def step(ins):
                own.did(ins)
                own.wait()

            def over_e(x, shape=(P, NT, E)):
                return x.unsqueeze(2).to_broadcast(list(shape))
            e.wait_ge(S["w"], 32)
            e.tensor_copy(self.r_hl[:, 0], self.r_w[:]).then_inc(S["split"], 1)
            e.wait_ge(S["split"], 1)
            e.tensor_tensor(self.r_hl[:, 1], self.r_w[:], self.r_hl[:, 0].bitcast(F32), ALU.subtract).then_inc(S["split"], 1)
            e.wait_ge(S["logits"], 1)
            logits = psT[:, 0, 0:E * NT].rearrange("p (n e) -> p n e", e=E)
            step(e.tensor_tensor(p[:], logits, self.r_b[:].unsqueeze(1).to_broadcast([P, NT, E]), ALU.add))
            step(e.tensor_reduce(m4[:, 0], p[:], AX, ALU.max))
            e.tensor_tensor(p[:], p[:], over_e(m4[:, 0]), ALU.subtract).then_inc(S["shift"], 1)
            e.wait_ge(S["exp"], 1)
            step(e.tensor_reduce(m4[:, 1], p[:], AX, ALU.add))
            step(e.reciprocal(m4[:, 2], m4[:, 1]))
            step(e.tensor_tensor(p[:], p[:], over_e(m4[:, 2]), ALU.mult))
            shape = [P, NT, E, E]
            mine = p[:].unsqueeze(3).to_broadcast(shape)
            other = p[:].unsqueeze(2).to_broadcast(shape)
            tri = self.const("tri").rearrange("p (a b) -> p a b", a=E)
            own.did(e.tensor_tensor(cmp_[:, 0], other, mine, ALU.is_gt))
            step(e.tensor_tensor(cmp_[:, 1], other, mine, ALU.is_equal))
            step(e.tensor_tensor(cmp_[:, 1], cmp_[:, 1], tri.unsqueeze(1).to_broadcast(shape), ALU.mult))
            step(e.tensor_tensor(cmp_[:, 0], cmp_[:, 0], cmp_[:, 1], ALU.add))
            step(e.tensor_reduce(tmp[:], cmp_[:, 0], AX, ALU.add))
            real = over_e(self.const("real"))
            for j in range(TOP):
                step(e.tensor_scalar(self.g_pick[:, j], tmp[:], float(j), None, ALU.is_equal))
                step(e.tensor_tensor(self.g_pick[:, j], self.g_pick[:, j], real, ALU.mult))
            e.tensor_tensor(sel[:], self.g_pick[:, 0], self.g_pick[:, 1], ALU.add).then_inc(S["picked"], 1)
            for j in range(TOP):
                step(e.tensor_tensor(tmp[:], p[:], self.g_pick[:, j], ALU.mult))
                step(e.tensor_reduce(self.gates[:, j], tmp[:], AX, ALU.add))
            if L == 0:
                own.did(e.tensor_scalar(self.gates[:, 0:TOP], self.gates[:, 0:TOP], 0.5, None, ALU.mult))
            e.wait_ge(S["counted"], 1)
            step(e.tensor_copy(self.g_tot[:].rearrange("p n e -> p (n e)"), psS[:, 1, 0:NT * E]))
            step(e.memset(self.g_carry[:, 0], 0.0))
            for n in range(NT):
                step(e.tensor_tensor(self.g_carry[:, n + 1], self.g_carry[:, n], self.g_tot[:, n], ALU.add))
            total = self.g_carry[:, NT]
            need, start = self.g_cnt[:, 0], self.g_cnt[:, 1]
            steps = cmp_[:, 0, 0, :, 0:STEPS]
            step(e.tensor_tensor(steps, total.unsqueeze(2).to_broadcast([P, E, STEPS]),
                                 self.const("steps").unsqueeze(1).to_broadcast([P, E, STEPS]), ALU.is_gt))
            step(e.tensor_reduce(need, steps, AX, ALU.add))
            lower = cmp_[:, 1, 0]
            step(e.tensor_tensor(lower, tri, need.unsqueeze(1).to_broadcast([P, E, E]), ALU.mult))
            step(e.tensor_reduce(start, lower, AX, ALU.add))
            step(e.tensor_tensor(self.g_big[:], start.unsqueeze(1).to_broadcast([P, ROUTED, E]),
                                 self.const("blocks").unsqueeze(2).to_broadcast([P, ROUTED, E]), ALU.is_le))
            started = tmp[:].rearrange("p n e -> p (n e)")[:, 0:ROUTED]
            step(e.tensor_reduce(started, self.g_big[:], AX, ALU.add))
            own.did(e.tensor_scalar(self.expert_of[:, FIRST:FIRST + ROUTED], started, -1.0, None, ALU.add))
            own.did(e.memset(self.expert_of[:, 0:FIRST], E))
            own.did(e.memset(self.expert_of[:, FIRST + ROUTED:BLOCKS], E))
            step(e.tensor_scalar(start, start, float(BL), None, ALU.mult))
            step(e.tensor_tensor(self.g_tot[:], self.g_carry[:, 0:NT], start.unsqueeze(1).to_broadcast([P, NT, E]), ALU.add))
            step(e.tensor_tensor(self.g_tot[:], self.g_tot[:], psS[:, 0, 0:NT * E].rearrange("p (n e) -> p n e", e=E), ALU.add))
            for j in range(TOP):
                step(e.tensor_tensor(tmp[:], self.g_tot[:], self.g_pick[:, j], ALU.mult))
                step(e.tensor_reduce(self.g_pos[:, j], tmp[:], AX, ALU.add))
            e.tensor_copy(self.where[:], self.g_pos[:]).then_inc(S["placed"], 1)
        return {"sp": sp, "pe": pe, "act": act, "dve": dve, "pool": weights_pool}

    def expert_shape(self, L):
        return (8, 2048, 3) if L == 0 else (4, 1024, 2)

    def first_weights(self, L):
        _, PW, NP = self.expert_shape(L)
        came = [self.sem(f"fw{L}_came{j}") for j in range(NP)]
        high, low = self.sem(f"fw{L}_high"), self.sem(f"fw{L}_low")

        def sp(e):
            for j in range(NP):
                if j >= 2:
                    e.wait_ge(low, j - 1)
                e.dma_start(self.w_stage[:, j % 2, 0:PW], self.A[f"ffn{L}"][E, j]).then_inc(came[j], 16)

        def act(e):
            for j in range(NP):
                e.wait_ge(came[j], 16)
                e.activation(self.w_hi[:, 1, PW * j:PW * j + PW], self.w_stage[:, j % 2, 0:PW], ACT.Copy).then_inc(high, 1)

        def pool(e):
            for j in range(NP):
                e.wait_ge(high, j + 1)
                at = slice(PW * j, PW * j + PW)
                e.tensor_tensor(self.w_lo[:, 1, at], self.w_stage[:, j % 2, 0:PW], self.w_hi[:, 1, at].bitcast(F32),
                                ALU.subtract).then_inc(low, 1)
        return sp, act, pool

    def experts(self, L):
        A, X, psS, psT, psY = self.A, self.X, self.psS, self.psT, self.psY
        gated = L == 0
        FT, PW, NP = self.expert_shape(L)
        O2 = (NP - 1) * PW
        SHARED_GATE = 1.0 / 16 if L == 0 else 1.0
        CREDIT = 3
        TERMS = ((0, 0), (0, 1), (1, 0))
        names = ["xt", "x_in", "x_hi", "x_lo", "gu", "act", "hraw", "hhi", "h", "y", "y_moved", "biased", "added"]
        names += [f"{a}{j}" for a in ("w_in", "w_hi", "w_lo") for j in range(NP)]
        names += [f"{a}{s}" for a in ("b_in", "y_out") for s in range(2)]
        S = {n: self.sem(f"ex{L}_{n}") for n in names}
        w = (self.w_hi, self.w_lo)
        TAIL = FIRST + ROUTED
        I0, I1 = FIRST // 2, TAIL // 2
        LASTB = BLOCKS - 1

        def is_shared(t):
            return isinstance(t, int) and not FIRST <= t < TAIL

        def tiles(t):
            n = SUB * (t if t < FIRST else t - ROUTED)
            return range(n, min(n + SUB, NT))

        def columns(t):
            return P * len(tiles(t)) if is_shared(t) else BL

        def weights_slot(slot, t):
            return slot if not is_shared(t) else (1 if t < FIRST else 0)

        def sets(t):
            return TAIL - FIRST + 1 if isinstance(t, int) and t >= TAIL else t - FIRST + 1

        def stage_slot(j, slot):
            return (NP * slot + j) % 2

        def credit(e, *names):
            for name in names:
                for _ in range(CREDIT):
                    e.nop().then_inc(S[name], 1)

        def over_blocks(block, ahead):
            def run(e):
                ahead(0, 0)
                for i in range(I0):
                    block(0, i, lambda: ahead(1, i))
                    block(1, i, lambda: ahead(0, i + 1))
                with e.Fori(I0, I1 - 1) as i:
                    block(0, i, lambda: ahead(1, i))
                    block(1, i, lambda: ahead(0, i + 1))
                for i in range(I1 - 1, BLOCKS // 2):
                    block(0, i, lambda: ahead(1, i))
                    block(1, i, (lambda: ahead(0, i + 1)) if 2 * i + 1 < LASTB else lambda: None)
            return run

        def sp(e):
            for s in range(2):
                e.nop().then_inc(S[f"y_out{s}"], 16)

            def expert(t):
                return e.value_load(self.expert_of[0:1, bass.ds(t, 1) if not isinstance(t, int) else slice(t, t + 1)],
                                    min_val=0, max_val=E)

            def weights(slot, t, ex):
                for j in range(NP):
                    if j >= 2:
                        e.wait_ge(S[f"w_lo{j - 2}"], sets(t))
                    elif not isinstance(t, int) or t > FIRST:
                        e.wait_ge(S[f"w_lo{j - 2 + NP}"], sets(t) - 1)
                    e.dma_start(self.w_stage[:, stage_slot(j, slot), 0:PW],
                                A[f"ffn{L}"][bass.ds(ex, 1), j].rearrange("o p w -> (o p) w")).then_inc(S[f"w_in{j}"], 16)

            def rows_of(dram, t):
                at = t * BL - FIRST * BL
                return dram[slice(at, at + BL) if isinstance(t, int) else bass.ds(at, BL)].rearrange("(s p) d -> p s d", p=P)

            def rows(t):
                e.wait_ge(S["xt"], t)
                e.dma_start(self.e_rows[:], rows_of(self.rows_in, t)).then_inc(S["x_in"], 16)

            def biases(slot, t, ex):
                if gated:
                    return
                if not (isinstance(t, int) and t < 2):
                    e.wait_ge(S["y_moved"], (t - 1) * 2 + CREDIT)
                e.dma_start(self.w_b1[:, slot], A["ffn_b1"][bass.ds(ex, 1)].rearrange("o p w -> (o p) w")).then_inc(S[f"b_in{slot}"], 16)
                e.dma_start(self.w_b2[:, slot], A["ffn_b2"][bass.ds(ex, 1)].to_broadcast([P, D])).then_inc(S[f"b_in{slot}"], 16)

            def store(slot, t):
                e.wait_ge(S["y_moved"], (t + 1) * 2 + CREDIT)
                e.dma_start(rows_of(self.rows_out, t), self.e_y[:, slot]).then_inc(S[f"y_out{slot}"], 16)

            for t in range(FIRST):
                biases(t % 2, t, expert(t))
            for t in range(FIRST, FIRST + 2):
                ex = expert(t)
                weights(t % 2, t, ex)
                if t == FIRST:
                    e.wait_ge(self.scattered, 16 * NT * TOP * (L + 1))
                rows(t)
                biases(t % 2, t, ex)
            with e.Fori(I0, I1 - 1) as i:
                for slot in range(2):
                    t = i * 2 + slot
                    ex = expert(t + 2)
                    weights(slot, t + 2, ex)
                    rows(t + 2)
                    store(slot, t)
                    biases(slot, t + 2, ex)
            weights(0, TAIL, expert(TAIL))
            for slot in range(2):
                store(slot, TAIL - 2 + slot)
            for t in range(TAIL, BLOCKS):
                biases(t % 2, t, expert(t))

        def pe(e):
            credit(e, "y")

            def turn(slot, i):
                t = i * 2 + slot
                if is_shared(t):
                    rows = [self.n_rows[:, n] for n in tiles(t)]
                else:
                    e.wait_ge(S["x_in"], (t - FIRST) * 16 + 16)
                    rows = [self.e_rows[:, sub] for sub in range(SUB)]
                e.wait_ge(S["x_lo"], t + CREDIT)
                for sub, row in enumerate(rows):
                    for dt in range(DT):
                        m = e.transpose(psT[:, dt, P * sub:P * sub + P], row[:, P * dt:P * dt + P], self.const("ident"))
                m.then_inc(S["xt"], 1)

            def block(slot, i, ahead):
                t = i * 2 + slot
                ws, cols = weights_slot(slot, t), columns(t)
                e.wait_ge(S["x_lo"], t + 1 + CREDIT)
                first = isinstance(t, int) and t < FIRST
                if not first:
                    for j in range(NP - 1):
                        e.wait_ge(S[f"w_lo{j}"], sets(t))
                for f in range(FT):
                    if gated:
                        e.wait_ge(S["hraw"], t * FT + f - 1 + CREDIT)
                    else:
                        e.wait_ge(S["act"], t * FT + f - 1 + CREDIT)
                    for j in range(NP - 1):
                        n = 0
                        for dt in range(DT):
                            for a, z in TERMS:
                                at = PW * j + (PW // DT) * dt + P * f
                                m = e.matmul(psS[:, 2 * j + f % 2, 0:cols], w[a][:, ws, at:at + P], self.e_x[:, slot, z, dt, 0:cols],
                                             start=n == 0, stop=n == 2 * DT + 1)
                                n += 1
                    m.then_inc(S["gu"], 1)
                ahead()
                if not first:
                    e.wait_ge(S[f"w_lo{NP - 1}"], sets(t))
                for sub in range(cols // P):
                    if sub % 2 == 0:
                        e.wait_ge(S["y_moved"], (t - 1) * 2 + sub // 2 + 1 + CREDIT)
                    for f in range(FT):
                        if sub == 0:
                            e.wait_ge(S["h"], t * FT + f + 1 + CREDIT)
                        for n, (a, z) in enumerate(TERMS):
                            at = O2 + D * f
                            m = e.matmul(psY[:, sub // 2, D * (sub % 2):D * (sub % 2) + D], self.e_hl[:, z, f, P * sub:P * sub + P],
                                         w[a][:, ws, at:at + D], start=f == 0 and n == 0, stop=f == FT - 1 and n == 2)
                    if sub % 2 == 1 or sub == SUB - 1:
                        m.then_inc(S["y"], 1)
            over_blocks(block, turn)(e)

        WHEN = {0: (0, 0), 1: (0, 1), 2: (1, 0), 3: (1, 1)}
        if NP == 3:
            WHEN.update({FT - 2: (2, 0), FT - 1: (2, 1)})

        def act(e):
            credit(e, "act")

            def split(j, half, slot, i):
                t = i * 2 + slot
                if half == 0:
                    e.wait_ge(S[f"w_in{j}"], sets(t) * 16)
                    e.wait_ge(S["y"], (t - 1) * 2 + CREDIT)
                at = half * (PW // 2)
                e.activation(self.w_hi[:, slot, PW * j + at:PW * j + at + PW // 2],
                             self.w_stage[:, stage_slot(j, slot), at:at + PW // 2], ACT.Copy).then_inc(S[f"w_hi{j}"], 1)

            def x_hi(slot, i):
                t = i * 2 + slot
                e.wait_ge(S["xt"], t + 1)
                cols = columns(t)
                e.activation(self.e_x[:, slot, 0, :, 0:cols], psT[:, :, 0:cols], ACT.Copy).then_inc(S["x_hi"], 1)

            def block(slot, i, ahead):
                t = i * 2 + slot
                cols = columns(t)
                new = not isinstance(t, int) or FIRST <= t + 1 <= TAIL
                nxt = (1, i) if slot == 0 else (0, i + 1)
                if not gated:
                    e.wait_ge(S[f"b_in{slot}"], i * 32 + 32)
                for f in range(FT):
                    e.wait_ge(S["gu"], t * FT + f + 1)
                    if gated:
                        e.wait_ge(S["hraw"], t * FT + f - 1 + CREDIT)
                        e.activation(self.e_act[:, f % 2, 0:cols], psS[:, f % 2, 0:cols], ACT.Silu).then_inc(S["act"], 1)
                    else:
                        e.wait_ge(S["h"], t * FT + f - 1 + CREDIT)
                        e.activation(self.e_h[:, f % 2, 0:cols], psS[:, f % 2, 0:cols], ACT.Gelu,
                                     bias=self.w_b1[:, slot, f:f + 1]).then_inc(S["act"], 1)
                    if new and f in WHEN:
                        split(*WHEN[f], *nxt)
                ahead()
            over_blocks(block, x_hi)(e)

        def pool(e):
            for n in range(NT):
                m = P if n < NT - 1 else NB
                for j in range(TOP):
                    e.indirect_dma_start(self.rows_in, bass.IndirectOffsetOnAxis(ap=self.where[0:m, j, n:n + 1], axis=0),
                                         self.n_rows[0:m, n, :], None).then_inc(self.scattered, 16)

            def split(slot, i):
                t = i * 2 + slot
                for j in range(NP):
                    for half in range(2):
                        e.wait_ge(S[f"w_hi{j}"], (sets(t) - 1) * 2 + half + 1)
                        e.nop().then_inc(self.paced, 1)
                        at = half * (PW // 2)
                        to = slice(PW * j + at, PW * j + at + PW // 2)
                        m = e.tensor_tensor(self.w_lo[:, slot, to], self.w_stage[:, stage_slot(j, slot), at:at + PW // 2],
                                            self.w_hi[:, slot, to].bitcast(F32), ALU.subtract)
                    m.then_inc(S[f"w_lo{j}"], 1)
            split(0, I0)
            with e.Fori(I0, I1 - 1) as i:
                split(1, i)
                split(0, i + 1)
            split(1, I1 - 1)
            split(0, I1)
            e.wait_ge(self.scattered, 16 * NT * TOP * (L + 1))
            for s in range(2):
                e.wait_ge(S[f"y_out{s}"], 16 * (ROUTED // 2) + 16)
            for k in range(TOP * NT):
                j, n = divmod(k, NT)
                m = P if n < NT - 1 else NB
                if k >= BACK:
                    e.wait_ge(S["added"], k - BACK + 1)
                e.indirect_dma_start(self.n_rows[0:m, k % BACK, :], None, self.rows_out,
                                     bass.IndirectOffsetOnAxis(ap=self.where[0:m, j, n:n + 1], axis=0)).then_inc(self.gathered[k % BACK], 16)

        def dve(e):
            credit(e, "hraw", "h", "x_lo", "y_moved")
            biased, added = Own(e, S["biased"]), Own(e, S["added"])

            def x_lo(slot, i):
                t = i * 2 + slot
                e.wait_ge(S["x_hi"], t + 1)
                cols = columns(t)
                e.tensor_tensor(self.e_x[:, slot, 1, :, 0:cols], psT[:, :, 0:cols], self.e_x[:, slot, 0, :, 0:cols].bitcast(F32),
                                ALU.subtract).then_inc(S["x_lo"], 1)

            def add_routed(last):
                for k in range(added.n, min(last, TOP * NT)):
                    j, n = divmod(k, NT)
                    m = P if n < NT - 1 else NB
                    a = -(-(TOP * NT - k % BACK) // BACK)
                    e.wait_ge(self.gathered[k % BACK], 16 * (L * a + k // BACK + 1))
                    added.wait()
                    added.did(e.scalar_tensor_tensor(X[0:m, n], self.n_rows[0:m, k % BACK], self.gates[0:m, j, n:n + 1], X[0:m, n],
                                                     ALU.mult, ALU.add))

            def block(slot, i, ahead):
                t = i * 2 + slot
                cols = columns(t)
                for f in range(FT):
                    k = t * FT + f
                    e.wait_ge(S["act"], k + 1 + CREDIT)
                    raw = self.e_h[:, f % 2, 0:cols]
                    if gated:
                        e.wait_ge(S["h"], k - 1 + CREDIT)
                        e.tensor_tensor(raw, self.e_act[:, f % 2, 0:cols], psS[:, 2 + f % 2, 0:cols], ALU.mult).then_inc(S["hraw"], 1)
                        e.wait_ge(S["hraw"], k + 1 + CREDIT)
                    if f == 0:
                        e.wait_ge(S["y"], t * 2 + CREDIT)
                    e.tensor_copy(self.e_hl[:, 0, f, 0:cols], raw).then_inc(S["hhi"], 1)
                    e.wait_ge(S["hhi"], k + 1)
                    e.tensor_tensor(self.e_hl[:, 1, f, 0:cols], raw, self.e_hl[:, 0, f, 0:cols].bitcast(F32),
                                    ALU.subtract).then_inc(S["h"], 1)
                    if isinstance(t, int) and t >= TAIL:
                        add_routed(2 * ((t - TAIL) * FT + f - 3))
                ahead()
                if not is_shared(t):
                    e.wait_ge(S[f"y_out{slot}"], (i - I0) * 16 + 16)
                    for bank in range(2):
                        e.wait_ge(S["y"], t * 2 + bank + 1 + CREDIT)
                        n = min(2, SUB - 2 * bank)
                        src = psY[:, bank, 0:n * D].rearrange("p (n d) -> p n d", d=D)
                        dst = self.e_y[:, slot, 2 * bank:2 * bank + n]
                        if gated:
                            m = e.tensor_copy(dst, src)
                        else:
                            m = e.tensor_tensor(dst, src, self.w_b2[:, slot].unsqueeze(1).to_broadcast([P, n, D]), ALU.add)
                        m.then_inc(S["y_moved"], 1)
                    return
                for bank, n0 in enumerate(range(tiles(t)[0], tiles(t)[-1] + 1, 2)):
                    n = min(2, tiles(t)[-1] + 1 - n0)
                    dst = X[:, n0:n0 + n]
                    added.wait()
                    if not gated:
                        biased.did(e.tensor_tensor(dst, dst, self.w_b2[:, slot].unsqueeze(1).to_broadcast([P, n, D]), ALU.add))
                        biased.wait()
                    e.wait_ge(S["y"], t * 2 + bank + 1 + CREDIT)
                    e.scalar_tensor_tensor(dst, psY[:, bank, 0:n * D].rearrange("p (n d) -> p n d", d=D), SHARED_GATE, dst,
                                           ALU.mult, ALU.add).then_inc(S["y_moved"], 1)
                    done = t * 2 + bank + 1 + CREDIT
                if t >= TAIL:
                    e.wait_ge(S["y_moved"], done)
            over_blocks(block, x_lo)(e)
            add_routed(TOP * NT)
        return {"sp": sp, "act": act, "pool": pool, "dve": dve, "pe": pe}

    def write_out(self):
        stored = self.sem("o_stored")

        def sp(e):
            for i in range(QT):
                e.dma_start(self.out[:, 1 + P * i:1 + P * i + P, :].rearrange("b p d -> p b d"),
                            self.X[:, i:NT - 1:QT]).then_inc(stored, 16)
            e.dma_start(self.out[:, 0, :], self.X[0:NB, NT - 1]).then_inc(stored, 16)
            e.wait_ge(stored, 48)
        return {"sp": sp}


def lay_out(x):
    f = lambda a: np.ascontiguousarray(a)
    n = {k: np.asarray(v) for k, v in x.items()}

    def by_pair(a):
        a = a.reshape(2, P, *a.shape[1:])
        return np.moveaxis(a, 1, -1)

    small = np.zeros((P, 5, P), np.float32)
    b = by_pair(n["L0_tok_B_ri"])
    small[:, 0:2] = b.reshape(P, 2, P)
    small[:, 2] = by_pair(n["L0_tok_inv_A_real"]).reshape(P, P)
    small[:, 3] = by_pair(n["L0_tok_A_imag"]).reshape(P, P)
    small[:, 4] = np.broadcast_to(n["L0_tok_log_dt"].reshape(2, 1, P), (2, 64, P)).reshape(P, P)
    c = n["x"].reshape(NB, 2, P, 64, 2).transpose(1, 3, 4, 0, 2).reshape(P, 2, NB, P)

    def down(w):
        return w.T.reshape(DT, P, w.shape[0]).transpose(1, 0, 2)

    def padded(w):
        r = np.zeros((4, GRP, 32, D), np.float32)
        r[:, :, 0:HD] = w.T.reshape(4, GRP, HD, D)
        return r.transpose(1, 2, 0, 3).reshape(P, 4, D)

    wa = n["L0_attn_w_attn"]
    wq, wk, wv = wa[0:D], wa[D:2 * D], wa[2 * D:]
    swap = np.arange(D).reshape(-1, 2)[:, ::-1].reshape(-1)
    a = {
        "consts": constants()[0], "rope_mask": constants()[1], "s4_small": small, "s4_c": c,
        "cls": n["cls_tok"].reshape(1, D),
        "w_qkv0": down(np.concatenate([wq, wq[swap], wk, wk[swap], wv])),
        "w_qkv1": down(np.concatenate([n["L1_attn_Wq"], n["L1_attn_Wk"], n["L1_attn_Wv"]])),
        "w_o0": padded(n["L0_attn_w_proj"]), "w_o1": padded(n["L1_attn_Wo"]),
        "a_bias": np.concatenate([n["L1_attn_" + k].reshape(DT, P).T for k in ("bq", "bk")], axis=1),
        "a_bv": n["L1_attn_bv"][None, :], "a_bo": n["L1_attn_bo"][None, :],
        "router0": down(n["L0_ffn_gate_W"]).reshape(P, DT * E),
        "router1": n["L1_ffn_router_w"].reshape(DT, P, E).transpose(1, 0, 2).reshape(P, DT * E),
        "router_b0": np.zeros((P, E), np.float32),
        "router_b1": np.broadcast_to(n["L1_ffn_router_b"][None, :], (P, E)),
    }
    def up(e, s):
        w = np.concatenate([e, s[None]])
        return w.reshape(9, DT, P, -1).transpose(0, 2, 1, 3).reshape(9, 1, P, -1)

    def back(e, s):
        w = np.concatenate([e, s[None]])
        return w.reshape(9, -1, P, D).transpose(0, 2, 1, 3).reshape(9, 1, P, -1)
    a["ffn0"] = np.concatenate([up(n["L0_ffn_w1_e"], n["L0_ffn_w1_s"].transpose(1, 0, 2).reshape(D, 1024)),
                                up(n["L0_ffn_w3_e"], n["L0_ffn_w3_s"].transpose(1, 0, 2).reshape(D, 1024)),
                                back(n["L0_ffn_w2_e"], n["L0_ffn_w2_s"].reshape(1024, D))], axis=1)
    a["ffn1"] = np.concatenate([up(n["L1_ffn_rw1"], n["L1_ffn_sw1"]), back(n["L1_ffn_rw2"], n["L1_ffn_sw2"])], axis=1)
    a["ffn_b1"] = np.concatenate([n["L1_ffn_rb1"], n["L1_ffn_sb1"][None]]).reshape(9, 4, P).transpose(0, 2, 1)
    a["ffn_b2"] = np.concatenate([n["L1_ffn_rb2"], n["L1_ffn_sb2"][None]])
    return {k: f(v) for k, v in a.items()}


def kernel(**inputs):
    import concourse.bacc as _bacc
    from concourse.bass_utils import run_bass_kernel_spmd as _run

    arrays = lay_out(inputs)
    nc = _bacc.Bacc("TRN2", target_bir_lowering=False, num_devices=1)
    args = {k: nc.dram_tensor("in_" + k, v.shape, F32, kind="ExternalInput").ap() for k, v in arrays.items()}
    out = nc.dram_tensor("out", (NB, T, D), F32, kind="ExternalOutput").ap()
    Tower(nc, args, out).build()
    r = _run(nc, [{"in_" + k: a for k, a in arrays.items()}], core_ids=[0])
    return r.results[0]["out"]
```

```python
from contextlib import ExitStack

import numpy as np
import concourse.bass as bass
from concourse import mybir

F32 = mybir.dt.float32
F32R = mybir.dt.float32r
BF16 = mybir.dt.bfloat16
ACT = mybir.ActivationFunctionType
ALU = mybir.AluOpType
AX = mybir.AxisListType.X

P = 128
NB, T, D = 8, 257, 256
DT = D // P
TOK = NB * T
NT = 17
COLS = NT * P
HEADS, HD = 16, 16
QT = 2
GRP = 4
BAND_REG, BAND_HALF = 16, 32
E = 8
TOP = 2
BL = 384
SUB = BL // P
ROUTED = (TOP * TOK + E * (BL - 1)) // BL
SHARED = -(-TOK // BL)
BLOCKS = ROUTED + SHARED
FIRST = 2
BACK = SUB * FIRST
SLOTS = ROUTED * BL
STEPS = -(-TOK // BL)
S4_HP = 16
S4_NB = P // S4_HP
S4_DVE = 11
EPS = 1e-5


ROPE_MASK = {"maskq": (0, 512), "cq": (512, 768), "sq": (768, 1024), "ck": (1024, 1280), "sk": (1280, 1536)}


def constant_layout():
    widths = [("ones", P), ("before", P), ("ident", P), ("headmask", 8), ("spread", 4 * P), ("diag", 16), ("clspick", 4 * 16),
              ("clsheads", 2 * 16), ("tri", 64), ("eps", 1), ("valid", QT),
              ("real", NT), ("steps", STEPS), ("blocks", ROUTED)]
    at, out = 0, {}
    for name, w in widths:
        out[name] = (at, at + w)
        at += w
    return out, at


def constants():
    where, width = constant_layout()
    c = np.zeros((P, width), np.float32)

    def put(name, value):
        a, b = where[name]
        c[:, a:b] = np.asarray(value, np.float32).reshape(P, b - a)

    table = {}
    p = np.arange(P)
    put("ones", np.ones((P, P)))
    put("before", p[:, None] < p[None, :])
    put("ident", np.eye(P))
    t = np.arange(1, 257)
    q = (p[:, None] + P * np.arange(QT)[None, :] + 1)[:, :, None]
    j = t[None, None, :]
    near = (q >= BAND_REG) & (j >= np.maximum(BAND_REG, q - BAND_HALF)) & (j <= q + BAND_HALF)
    table["maskq"] = (np.where((j < BAND_REG) | (q < BAND_REG) | near, -1e30, 0.0))
    theta = (np.float32(1.0) / np.float32(10000.0) ** (np.arange(0, HD, 2, dtype=np.float32) / np.float32(HD)))
    ang = (t.astype(np.float32)[None, :] * theta[(p % HD) // 2][:, None]).astype(np.float32)
    cos = np.cos(ang)
    sin = np.where((p % 2 == 0)[:, None], -np.sin(ang), np.sin(ang))
    table["ck"] = cos
    table["sk"] = sin
    table["cq"] = cos * np.float32(0.25)
    table["sq"] = sin * np.float32(0.25)
    put("headmask", p[:, None] // HD == np.arange(8)[None, :])
    g, m = np.arange(4)[None, :, None], np.arange(P)[None, None, :]
    put("spread", p[:, None, None] == GRP * g + m // 32)
    put("diag", p[:, None] == np.arange(16)[None, :])
    put("clspick", np.arange(16)[None, None, :] == GRP * np.arange(4)[None, :, None] + p[:, None, None] // 32)
    put("clsheads", np.arange(16)[None, None, :] == 8 * np.arange(2)[None, :, None] + p[:, None, None] // HD)
    put("tri", np.broadcast_to(np.arange(E)[None, :] < np.arange(E)[:, None], (P, E, E)))
    put("eps", np.full(P, EPS))
    put("valid", (q[:, :, 0] >= BAND_REG))
    put("real", (np.arange(NT)[None, :] < NT - 1) | (p[:, None] < NB))
    put("steps", np.broadcast_to(BL * np.arange(STEPS), (P, STEPS)))
    put("blocks", np.broadcast_to(np.arange(ROUTED), (P, ROUTED)))
    return c, np.concatenate([np.asarray(table[n], np.float32).reshape(P, -1) for n in ROPE_MASK], axis=1)


def span(at, count):
    return slice(at, at + count) if isinstance(at, int) else bass.ds(at, count)


class Own:

    def __init__(self, eng, sem, apart=None):
        self.eng, self.sem, self.base, self.n, self.apart = eng, sem, 0, 0, apart

    def did(self, ins):
        ins.then_inc(self.sem, 1)
        self.n += 1
        return ins

    def wait(self):
        self.eng.wait_ge(self.sem, self.base + self.n)
        if self.apart:
            self.eng.nop().then_inc(self.apart, 1)

    def enter(self, i, per):
        self.outer, self.per, self.start = self.base, per, self.n
        self.base, self.n = self.outer + self.start + i * per, 0

    def leave(self, passes):
        assert self.n == self.per, (self.sem, self.n, self.per)
        self.base, self.n = self.outer, self.start + passes * self.per


class Tower:
    def __init__(self, nc, A, out, stop=99):
        self.nc, self.A, self.out, self.stop = nc, A, out, stop
        self.engines = {}

    def sem(self, name, again=True):
        if not again:
            return self.top.enter_context(self.nc.semaphore(name))
        s = self.free.pop(0) if self.free else self.top.enter_context(self.nc.semaphore(name))
        self.used.append(s)
        return s

    def sb(self, scope, name, shape, dt=F32):
        return scope.enter_context(self.nc.sbuf_tensor(name, shape, dt))

    def const(self, name, *dims):
        a, b = constant_layout()[0][name]
        return self.cst[:, a:b]

    def table(self, name):
        a, b = ROPE_MASK[name]
        return self.a_table[:, a:b]

    def build(self):
        nc = self.nc
        with ExitStack() as self.top:
            sb, top = self.sb, self.top
            self.X = sb(top, "X", [P, NT, D])
            self.cst = sb(top, "cst", [P, constant_layout()[1]])
            self.psS = top.enter_context(nc.psum_tensor("psS", [P, 4, 512], F32))
            self.psT = top.enter_context(nc.psum_tensor("psT", [P, 2, 512], F32))
            self.psY = top.enter_context(nc.psum_tensor("psY", [P, 2, 512], F32))
            self.rows_in = nc.dram_tensor("rows_in", [SLOTS, D], F32, kind="Internal").ap()
            self.rows_out = nc.dram_tensor("rows_out", [SLOTS, D], F32, kind="Internal").ap()
            with ExitStack() as s4:
                self.memory_s4(s4)
            self.where = sb(top, "where", [P, TOP, NT], mybir.dt.int32)
            self.gates = sb(top, "gates", [P, TOP, NT])
            self.expert_of = sb(top, "expert_of", [P, BLOCKS], mybir.dt.int32)
            self.memory_norm(top)
            with ExitStack() as a:
                self.xa_hl = sb(a, "xa_hl", [P, 2, DT, COLS], F32R)
                self.rows_a = sb(a, "rows_a", [P, NT, D])
            with ExitStack() as a:
                self.memory_attention(a)
            with ExitStack() as a:
                self.n_rows = sb(a, "n_rows", [P, NT, D])
                with ExitStack() as b:
                    self.memory_router(b)
                with ExitStack() as b:
                    self.memory_experts(b)
            self.free, self.used = [], []
            self.stage_done = self.sem("stage_done")
            self.loaded = self.sem("loaded")
            self.rows_cleared = self.sem("rows_cleared")
            self.attention_loaded = self.sem("attention_loaded")
            self.scattered = self.sem("scattered", again=False)
            self.gathered = [self.sem(f"gathered{s}", again=False) for s in range(BACK)]
            self.paced = self.sem("paced")
            self.program()

    def memory_s4(self, s):
        sb = self.sb
        self.s4_small = sb(s, "s4_small", [P, 5, P])
        self.s4_c = sb(s, "s4_c", [P, 2, NB, P])
        self.s4_w = sb(s, "s4_w", [P, 8, 2, P])
        self.s4_tmp = sb(s, "s4_tmp", [P, 8, P])
        self.s4_cb = sb(s, "s4_cb", [P, 2, 2, NB, P])
        self.s4_prod = sb(s, "s4_prod", [P, 2, NB, P])
        self.s4_p = sb(s, "s4_p", [P, 2, P, 2, 2, NB])
        self.s4_v = sb(s, "s4_v", [P, 2, 2, S4_HP, P])
        self.s4_t = sb(s, "s4_t", [P, 2, S4_HP, 64])
        self.s4_k = sb(s, "s4_k", [P, DT, NB * 256])
        self.s4_zero = sb(s, "s4_zero", [P, D])

    def memory_norm(self, s):
        sb = self.sb
        self.n_stat = sb(s, "n_stat", [P, NT, 6])
        self.n_mv = sb(s, "n_mv", [P, NT, 2])
        self.n_sd = sb(s, "n_sd", [P, NT, 2])

    def memory_attention(self, s):
        sb = self.sb
        self.a_qm = sb(s, "a_qm", [P, 2, HEADS, 256])
        self.a_v = sb(s, "a_v", [P, 2, QT, HEADS * 32])
        self.a_pt = sb(s, "a_pt", [P, 8, 512])
        self.a_w = sb(s, "a_w", [P, DT * 1280])
        self.a_whl = sb(s, "a_whl", [P, 2, DT * 1280], F32R)
        self.a_wo = sb(s, "a_wo", [P, 4, D])
        self.a_table = sb(s, "a_table", [P, 1536])
        self.a_b = sb(s, "a_b", [P, 4])
        self.a_bo = sb(s, "a_bo", [P, D])
        self.a_bv = sb(s, "a_bv", [P, D])
        self.a_maskb = sb(s, "a_maskb", [P, QT, 256], BF16)
        self.a_identb = sb(s, "a_identb", [P, P], BF16)
        self.a_qk = sb(s, "a_qk", [P, 4, NB * T])
        self.a_v_all = sb(s, "a_v_all", [P, NB, QT, D])
        self.a_vt = sb(s, "a_vt", [16, NB, D])
        self.a_rs_all = sb(s, "a_rs_all", [P, NB, QT, HEADS])
        self.a_pex_all = sb(s, "a_pex_all", [P, NB, QT, HEADS])
        self.a_yc_all = sb(s, "a_yc_all", [P, NB, 64])
        self.a_rsc_all = sb(s, "a_rsc_all", [16, NB])
        self.a_pc0_all = sb(s, "a_pc0_all", [16, NB])
        self.a_ycls = sb(s, "a_ycls", [P, 4, NB])
        self.a_xc = sb(s, "a_xc", [P, 2, 2, DT, 16], F32R)
        self.a_qc = sb(s, "a_qc", [P, 2, DT, 16])
        self.a_vc = sb(s, "a_vc", [P, 2, HEADS * 32])
        self.a_pct = sb(s, "a_pct", [P, 2, QT, 16])
        self.a_sum = sb(s, "a_sum", [P, 2, QT, HEADS])
        self.a_rs = sb(s, "a_rs", [P, 2, QT, HEADS])
        self.a_pexs = sb(s, "a_pexs", [P, 2, QT, HEADS])
        self.a_rst = sb(s, "a_rst", [P, 2, T])
        self.a_pext = sb(s, "a_pext", [P, 2, T])
        with ExitStack() as first:
            self.a_x = sb(first, "a_x", [P, 2, 2, DT, 256], F32R)
            self.a_rope = sb(first, "a_rope", [P, 2, 2, 256])
        self.a_yn = sb(s, "a_yn", [P, 2, 4, T])
        self.a_yc = sb(s, "a_yc", [P, 2, 4, 16])
        self.a_rsc = sb(s, "a_rsc", [16, 2])
        self.a_p = sb(s, "a_p", [P, 2, QT, T])
        self.a_nm = sb(s, "a_nm", [P, HEADS + 1, QT])
        self.a_st = sb(s, "a_st", [P, QT, HEADS])
        self.a_pex = sb(s, "a_pex", [P, QT, HEADS])
        self.a_pc = sb(s, "a_pc", [16, T])

    def memory_router(self, s):
        sb = self.sb
        self.x_hl = sb(s, "x_hl", [P, 2, DT, COLS], F32R)
        self.r_w = sb(s, "r_w", [P, DT * E])
        self.r_hl = sb(s, "r_hl", [P, 2, DT * E], F32R)
        self.r_b = sb(s, "r_b", [P, E])
        self.g_p = sb(s, "g_p", [P, NT, E])
        self.g_cmp = sb(s, "g_cmp", [P, 2, NT, E, E])
        self.g_lt = sb(s, "g_lt", [E, COLS])
        self.g_m = sb(s, "g_m", [P, 4, NT])
        self.g_sel = sb(s, "g_sel", [P, NT, E])
        self.g_pick = sb(s, "g_pick", [P, TOP, NT, E])
        self.g_tmp = sb(s, "g_tmp", [P, NT, E])
        self.g_carry = sb(s, "g_carry", [P, NT + 1, E])
        self.g_tot = sb(s, "g_tot", [P, NT, E])
        self.g_pos = sb(s, "g_pos", [P, TOP, NT])
        self.g_cnt = sb(s, "g_cnt", [P, 2, E])
        self.g_big = sb(s, "g_big", [P, ROUTED, E])

    def memory_experts(self, s):
        sb = self.sb
        self.w_b1 = sb(s, "w_b1", [P, 2, 4])
        self.w_b2 = sb(s, "w_b2", [P, 2, D])
        self.e_rows = sb(s, "e_rows", [P, SUB, D])
        self.e_x = sb(s, "e_x", [P, 2, 2, DT, BL], F32R)
        self.e_act = sb(s, "e_act", [P, 2, BL])
        self.e_h = sb(s, "e_h", [P, 2, BL])
        self.e_hl = sb(s, "e_hl", [P, 2, 8, BL], F32R)
        self.e_y = sb(s, "e_y", [P, 2, SUB, D])
        self.w_stage = sb(s, "w_stage", [P, 2, 2048])
        self.w_hi = sb(s, "w_hi", [P, 2, 3 * 2048], F32R)
        self.w_lo = sb(s, "w_lo", [P, 2, 3 * 2048], F32R)

    def program(self):
        stages = [self.load_constants, self.s4_tokens, self.tokens_to_rows]
        for layer in range(2):
            stages += [lambda layer=layer: self.layernorm(f"a{layer}", layer, True),
                       lambda layer=layer: self.attention(layer),
                       lambda layer=layer: self.layernorm(f"f{layer}", layer, False),
                       lambda layer=layer: self.router(layer),
                       lambda layer=layer: self.experts(layer)]
        stages = stages[:self.stop]
        stages.append(self.write_out)
        nc = self.nc
        parts, spent, self.free = [], [], []
        for s in stages:
            self.used = []
            parts.append(s())
            self.free += spent[-2] if len(spent) > 1 else []
            spent.append(self.used)

        def run(eng, name):
            for n, part in enumerate(parts):
                if name == "sp" and 0 < n < len(parts) - 1:
                    for s in spent[n - 1]:
                        eng.sem_clear(s)
                if name in part:
                    part[name](eng)
                if n < len(parts) - 1:
                    eng.drain().then_inc(self.stage_done, 1)
                    eng.wait_ge(self.stage_done, 5 * (n + 1))

        with nc.Block() as block:
            @block.sync
            def _(sp):
                run(sp, "sp")

            @block.gpsimd
            def _(pool):
                run(pool, "pool")

            @block.scalar
            def _(act):
                run(act, "act")

            @block.vector
            def _(dve):
                run(dve, "dve")

            @block.tensor
            def _(pe):
                run(pe, "pe")

    def load_constants(self):
        A, X = self.A, self.X
        cls_loaded, cleared = self.sem("cls_loaded"), self.sem("cleared")

        def sp(e):
            e.dma_start(self.s4_small[:], A["s4_small"]).then_inc(self.loaded, 16)
            e.dma_start(self.s4_c[:], A["s4_c"]).then_inc(self.loaded, 16)
            e.dma_start(self.cst[:], A["consts"]).then_inc(self.loaded, 16)
            e.wait_ge(cleared, 2)
            e.dma_start(X[0:NB, NT - 1, :], A["cls"].to_broadcast([NB, D])).then_inc(cls_loaded, 16)
            zero = self.s4_zero[:].unsqueeze(1)
            e.dma_start(self.rows_in.rearrange("(n p) d -> p n d", p=P),
                        zero.to_broadcast([P, SLOTS // P, D])).then_inc(self.rows_cleared, 16)
            e.wait_ge(self.loaded, 48)
            e.wait_ge(cls_loaded, 16)

        def pool(e):
            e.memset(X[:, NT - 1], 0.0).then_inc(cleared, 1)
            e.memset(self.s4_zero[:], 0.0).then_inc(cleared, 1)
        return {"sp": sp, "pool": pool}

    def s4_tokens(self):
        small, c, w, tmp, cb, prod = self.s4_small, self.s4_c, self.s4_w, self.s4_tmp, self.s4_cb, self.s4_prod
        pw, v, t, kern, psS = self.s4_p, self.s4_v, self.s4_t, self.s4_k, self.psS
        own_dve, own_pool = self.sem("s4_own_dve"), self.sem("s4_own_pool")
        w_ready, zeroed = self.sem("s4_w_ready"), self.sem("s4_zeroed")
        p_ready = self.sem("s4_p_ready")
        v_dve, v_pool = self.sem("s4_v_dve"), self.sem("s4_v_pool")
        k_ready, k_moved = self.sem("s4_k_ready"), self.sem("s4_k_moved")
        CREDIT = 2

        def act(e):
            for _ in range(CREDIT):
                e.nop().then_inc(k_moved, 1)
            with e.Fori(0, S4_NB // 2) as i:
                for s in range(2):
                    blk = i * 2 + s
                    e.wait_ge(k_ready, blk + 1 + CREDIT)
                    for a in range(2):
                        dst = kern[:, a].rearrange("p (c g h) -> p c g h", c=NB, g=2)[:, :, :, bass.ds(blk * S4_HP, S4_HP)]
                        src = psS[:, s, :].rearrange("p (h g a c) -> p a c g h", g=2, a=2, c=NB)[:, a]
                        last = e.activation(dst, src, ACT.Copy)
                    last.then_inc(k_moved, 1)

        def powers(e, own, first, count, slot, blk):
            a, z = first, first + count

            def wk(k, ri, width):
                return w[:, k, ri, bass.ds(blk * S4_HP + first, count)].unsqueeze(2).to_broadcast([P, count, width])

            own.did(e.tensor_copy(v[:, slot, 0, a:z, 1:2], wk(0, 0, 1)))
            own.did(e.tensor_copy(v[:, slot, 1, a:z, 1:2], wk(0, 1, 1)))
            for k in range(1, 7):
                n = 1 << k
                own.wait()
                re, im = v[:, slot, 0, a:z, 0:n], v[:, slot, 1, a:z, 0:n]
                own.did(e.tensor_tensor(t[:, 0, a:z, 0:n], re, wk(k, 0, n), ALU.mult))
                own.did(e.tensor_tensor(t[:, 1, a:z, 0:n], im, wk(k, 1, n), ALU.mult))
                own.wait()
                own.did(e.tensor_tensor(v[:, slot, 0, a:z, n:2 * n], t[:, 0, a:z, 0:n], t[:, 1, a:z, 0:n], ALU.subtract))
                own.wait()
                own.did(e.tensor_tensor(t[:, 0, a:z, 0:n], re, wk(k, 1, n), ALU.mult))
                own.did(e.tensor_tensor(t[:, 1, a:z, 0:n], im, wk(k, 0, n), ALU.mult))
                own.wait()
                last = e.tensor_tensor(v[:, slot, 1, a:z, n:2 * n], t[:, 0, a:z, 0:n], t[:, 1, a:z, 0:n], ALU.add)
                if k < 6:
                    own.did(last)
            return last

        PER = 2 + 6 * 6 - 1

        def dve(e):
            own = Own(e, own_dve)

            def tt(out, a, b, op):
                own.did(e.tensor_tensor(out, a, b, op))

            def exponential():
                x = small[:, 2:5:2]
                k, r, q, two = (prod[:, 0, 2 * n:2 * n + 2] for n in range(4))
                ROUND = 1.5 * 2.0 ** 23
                LN2_HI, LN2_LO = 355.0 / 512.0, -2.12194440054690583e-4

                def step(ins):
                    own.did(ins)
                    own.wait()
                step(e.tensor_scalar(k, x, 1.0 / float(np.log(2.0)), ROUND, ALU.mult, ALU.add))
                step(e.tensor_scalar(k, k, -ROUND, -126.0, ALU.add, ALU.max))
                step(e.tensor_scalar(k, k, 127.0, None, ALU.min))
                step(e.scalar_tensor_tensor(r, k, -LN2_HI, x, ALU.mult, ALU.add))
                step(e.scalar_tensor_tensor(r, k, -LN2_LO, r, ALU.mult, ALU.add))
                fact = [1.0]
                for n in range(1, 9):
                    fact.append(fact[-1] * n)
                step(e.tensor_scalar(q, r, 1.0 / fact[8], None, ALU.mult))
                for n in range(7, 0, -1):
                    step(e.scalar_tensor_tensor(q, q, 1.0 / fact[n], r, ALU.add, ALU.mult))
                step(e.tensor_scalar(two.bitcast(mybir.dt.int32), k, 127.0, 2.0 ** 23, ALU.add, ALU.mult))
                step(e.scalar_tensor_tensor(x, q, 1.0, two, ALU.add, ALU.mult))

            exponential()
            bre, bim, ar, ai, dt = (small[:, n] for n in range(5))
            zr, zi, zr2, zi2, mag, num, omz, den = (tmp[:, n] for n in range(8))
            own.did(e.scalar_tensor_tensor(zr, ar, -0.5, dt, ALU.mult, ALU.mult))
            own.did(e.scalar_tensor_tensor(zi, ai, 0.5, dt, ALU.mult, ALU.mult))
            own.wait()
            tt(zr2, zr, zr, ALU.mult)
            tt(zi2, zi, zi, ALU.mult)
            own.did(e.tensor_scalar(omz, zr, -1.0, 1.0, ALU.mult, ALU.add))
            own.wait()
            tt(mag, zr2, zi2, ALU.add)
            tt(den, omz, omz, ALU.mult)
            own.wait()
            own.did(e.tensor_scalar(num, mag, -1.0, 1.0, ALU.mult, ALU.add))
            tt(den, den, zi2, ALU.add)
            own.wait()
            own.did(e.reciprocal(omz, den))
            own.wait()
            tt(w[:, 0, 0], num, omz, ALU.mult)
            own.did(e.scalar_tensor_tensor(w[:, 0, 1], zi, 2.0, omz, ALU.mult, ALU.mult))
            own.wait()
            for k in range(1, 8):
                r, i = w[:, k - 1, 0], w[:, k - 1, 1]
                tt(zr2, r, r, ALU.mult)
                tt(zi2, i, i, ALU.mult)
                own.did(e.scalar_tensor_tensor(w[:, k, 1], r, 2.0, i, ALU.mult, ALU.mult))
                own.wait()
                if k < 7:
                    tt(w[:, k, 0], zr2, zi2, ALU.subtract)
                    own.wait()
            e.tensor_tensor(w[:, 7, 0], zr2, zi2, ALU.subtract).then_inc(w_ready, 1)
            e.wait_ge(w_ready, 1)

            def cmul(out_re, out_im, xr, xi, yr, yi):
                for out, (a1, b1), (a2, b2), op in ((out_re, (xr, yr), (xi, yi), ALU.subtract),
                                                    (out_im, (xr, yi), (xi, yr), ALU.add)):
                    tt(prod[:, 0], a1, b1, ALU.mult)
                    tt(prod[:, 1], a2, b2, ALU.mult)
                    own.wait()
                    tt(out, prod[:, 0], prod[:, 1], op)
                    own.wait()

            def wide(x):
                return x.unsqueeze(1).to_broadcast([P, NB, P])
            cmul(cb[:, 0, 0], cb[:, 0, 1], c[:, 0], c[:, 1], wide(bre), wide(bim))
            cmul(cb[:, 1, 0], cb[:, 1, 1], cb[:, 0, 0], cb[:, 0, 1], wide(w[:, 7, 0]), wide(w[:, 7, 1]))
            e.wait_ge(zeroed, 4)
            for a in range(2):
                for ri, scale in ((0, 2.0), (1, -2.0)):
                    for h in range(2):
                        q = slice(64 * h, 64 * h + 64)
                        last = e.tensor_scalar(pw[q, ri, :, h, a, :].rearrange("p h c -> p c h"), cb[q, a, ri], scale, None, ALU.mult)
            last.then_inc(p_ready, 1)
            with e.Fori(0, S4_NB // 2) as i:
                own.enter(i, 2 * PER)
                for s in range(2):
                    blk = i * 2 + s
                    e.wait_ge(k_ready, blk - 1 + CREDIT)
                    powers(e, own, 0, S4_DVE, s, blk).then_inc(v_dve, 1)
                own.leave(S4_NB // 2)

        def pool(e):
            own = Own(e, own_pool, apart=self.paced)
            e.memset(pw[:, 0], 0.0).then_inc(zeroed, 1)
            e.memset(pw[:, 1], 0.0).then_inc(zeroed, 1)
            e.memset(v[:, :, 0, :, 0:1], 1.0).then_inc(zeroed, 1)
            e.memset(v[:, :, 1, :, 0:1], 0.0).then_inc(zeroed, 1)
            e.wait_ge(zeroed, 4)
            e.wait_ge(w_ready, 1)
            with e.Fori(0, S4_NB // 2) as i:
                own.enter(i, 2 * PER)
                for s in range(2):
                    e.wait_ge(k_ready, i * 2 + s - 1 + CREDIT)
                    e.nop().then_inc(self.paced, 1)
                    powers(e, own, S4_DVE, S4_HP - S4_DVE, s, i * 2 + s).then_inc(v_pool, 1)
                own.leave(S4_NB // 2)

        def pe(e):
            for _ in range(CREDIT):
                e.nop().then_inc(k_ready, 1)
            e.wait_ge(p_ready, 1)
            with e.Fori(0, S4_NB // 2) as i:
                for s in range(2):
                    blk = i * 2 + s
                    e.wait_ge(v_dve, blk + 1)
                    e.wait_ge(v_pool, blk + 1)
                    e.wait_ge(k_moved, blk - 1 + CREDIT)
                    for h in range(S4_HP):
                        for ri in range(2):
                            rhs = pw[:, ri, bass.ds(blk * S4_HP + h, 1)].rearrange("p h g a c -> p (h g a c)")
                            last = e.matmul(psS[:, s, 32 * h:32 * h + 32], v[:, s, ri, h, :], rhs,
                                            start=(ri == 0), stop=(ri == 1))
                    last.then_inc(k_ready, 1)
        return {"act": act, "dve": dve, "pool": pool, "pe": pe}

    def tokens_to_rows(self):
        turned, moved = self.sem("tr_turned"), [self.sem("tr_moved_act"), self.sem("tr_moved_dve")]

        def pe(e):
            for n in range(NT - 1):
                if n >= 4:
                    e.wait_ge(moved[n % 2], (n - 4) // 2 + 1)
                for dt in range(DT):
                    m = e.transpose(self.psS[:, n % 4, P * dt:P * dt + P], self.s4_k[:, dt, P * n:P * n + P], self.const("ident"))
                m.then_inc(turned, 1)

        def mover(which):
            def run(e):
                for n in range(which, NT - 1, 2):
                    e.wait_ge(turned, n + 1)
                    src = self.psS[:, n % 4, 0:D]
                    m = e.activation(self.X[:, n], src, ACT.Copy) if which == 0 else e.tensor_copy(self.X[:, n], src)
                    m.then_inc(moved[which], 1)
            return run

        def sp(e):
            e.wait_ge(self.rows_cleared, 16)
        return {"pe": pe, "act": mover(0), "dve": mover(1), "sp": sp}

    def layernorm(self, tag, L, for_attention):
        X, psS, psT = self.X, self.psS, self.psT
        stat, mv, sd = self.n_stat, self.n_mv, self.n_sd
        rows, x_hl = (self.rows_a, self.xa_hl) if for_attention else (self.n_rows, self.x_hl)
        stats, moments, rooted, own_sem, normed, turned, high, low = (
            self.sem(f"ln{tag}_{n}") for n in ("stats", "moments", "rooted", "own", "normed", "turned", "high", "low"))
        if not for_attention:
            came, wsplit, logits, kept = (self.sem(f"ln{tag}_{n}") for n in ("came", "wsplit", "logits", "kept"))
            weights_sp, weights_act, weights_pool = self.first_weights(L)
            r_w, r_hl = self.r_w, self.r_hl
        NC = -(-COLS // 512)
        NG = (NT + 1) // 2
        BK = [psS[:, n, :] for n in range(4)] + [psT[:, n, :] for n in range(2)]

        def tiles(g):
            return range(2 * g, min(2 * g + 2, NT))

        def group(z, g):
            w = len(tiles(g))
            return x_hl[:, z, :, 2 * P * g:2 * P * g + P * w].rearrange("p a (n t) -> p n a t", t=P)

        def bank(g):
            w = len(tiles(g))
            return BK[g % 6][:, 0:2 * P * w].rearrange("p (n a t) -> p n a t", a=DT, t=P)

        def pe(e):
            for g in range(NG):
                if g >= 6:
                    e.wait_ge(low, g - 5)
                for n in tiles(g):
                    e.wait_ge(normed, n + 1)
                    for dt in range(DT):
                        at = 2 * P * (n % 2) + P * dt
                        m = e.transpose(BK[g % 6][:, at:at + P], rows[:, n, P * dt:P * dt + P], self.const("ident"))
                m.then_inc(turned, 1)
                if not for_attention and g >= 4 and g % 2 == 0:
                    router_logits(e, g // 2 - 2)
            if not for_attention:
                for c in range((NG - 1) // 2 - 1, NC):
                    router_logits(e, c)

        def router_logits(e, c):
            at = slice(512 * c, min(512 * c + 512, COLS))
            e.wait_ge(wsplit, 2)
            e.wait_ge(low, min(2 * c + 2, NG))
            if c >= 2:
                e.wait_ge(kept, c - 1)
            terms = [(dt, a, z) for dt in range(DT) for a, z in ((0, 0), (0, 1), (1, 0))]
            for n, (dt, a, z) in enumerate(terms):
                m = e.matmul(self.psY[0:E, c % 2, 0:at.stop - at.start], r_hl[:, a, E * dt:E * dt + E], x_hl[:, z, dt, at],
                             start=n == 0, stop=n == len(terms) - 1)
            m.then_inc(logits, 1)

        def act(e):
            def keep_logits(c):
                at = slice(512 * c, min(512 * c + 512, COLS))
                e.wait_ge(logits, c + 1)
                e.activation(self.g_lt[:, at], self.psY[0:E, c % 2, 0:at.stop - at.start], ACT.Copy).then_inc(kept, 1)
            if not for_attention:
                weights_act(e, 0)
            e.wait_ge(moments, NT)
            e.activation(sd[:, :, 0:1], mv[:, :, 1:2], ACT.Sqrt, bias=self.const("eps")).then_inc(rooted, 1)
            for g in range(NG):
                e.wait_ge(turned, g + 1)
                e.activation(group(0, g), bank(g), ACT.Copy).then_inc(high, 1)
                if not for_attention:
                    if g == 1:
                        weights_act(e, 1)
                    if g >= 5 and g % 2 == 1:
                        keep_logits((g - 5) // 2)
            if not for_attention:
                for c in range((NG - 5) // 2, NC):
                    keep_logits(c)
                weights_act(e, 2)

        def dve(e):
            own = Own(e, own_sem)
            for n in range(NT):
                e.bn_stats(stat[:, n], X[:, n]).then_inc(stats, 1)
            if not for_attention:
                e.wait_ge(came, 32)
                e.tensor_copy(r_hl[:, 0], r_w[:]).then_inc(wsplit, 1)
                e.wait_ge(wsplit, 1)
                e.tensor_tensor(r_hl[:, 1], r_w[:], r_hl[:, 0].bitcast(F32), ALU.subtract).then_inc(wsplit, 1)
            for n in range(NT):
                e.wait_ge(stats, n + 1)
                e.bn_aggr(mv[:, n], stat[:, n]).then_inc(moments, 1)
            e.wait_ge(rooted, 1)
            own.did(e.reciprocal(sd[:, :, 1:2], sd[:, :, 0:1]))
            own.wait()

            def split(g):
                e.wait_ge(high, g + 1)
                e.tensor_tensor(group(1, g), bank(g), group(0, g).bitcast(F32), ALU.subtract).then_inc(low, 1)
            LAG = 4
            for n in range(NT):
                e.tensor_scalar(rows[:, n], X[:, n], mv[:, n, 0:1], sd[:, n, 1:2], ALU.subtract, ALU.mult).then_inc(normed, 1)
                if n >= LAG and (n - LAG) % 2 == 1:
                    split((n - LAG) // 2)
            for g in range((NT - LAG) // 2, NG):
                split(g)
        stage = {"pe": pe, "act": act, "dve": dve}
        def sp(e):
            if for_attention:
                self.attention_loads(L, e)
                return
            e.dma_start(r_w[:], self.A[f"router{L}"]).then_inc(came, 16)
            e.dma_start(self.r_b[:], self.A[f"router_b{L}"]).then_inc(came, 16)
            weights_sp(e)
        stage["sp"] = sp
        if not for_attention:
            stage["pool"] = weights_pool
        return stage

    def attention_loads(self, L, e):
        A, ready = self.A, self.attention_loaded
        e.dma_start(self.a_w[:, 0:DT * (1280 if L == 0 else 768)], A[f"w_qkv{L}"]).then_inc(ready, 16)
        e.dma_start(self.a_wo[:], A[f"w_o{L}"]).then_inc(ready, 16)
        if L == 0:
            e.dma_start(self.a_table[:], A["rope_mask"]).then_inc(ready, 16)
        else:
            e.dma_start(self.a_b[:], A["a_bias"]).then_inc(ready, 16)
            e.dma_start(self.a_bv[:], A["a_bv"].to_broadcast([P, D])).then_inc(ready, 16)
            e.dma_start(self.a_bo[:], A["a_bo"].to_broadcast([P, D])).then_inc(ready, 16)

    def attention(self, L):
        A, X, psS, psT, psY = self.A, self.X, self.psS, self.psT, self.psY
        full = L == 1
        NK = T if full else T - 1
        K0 = 0 if full else 1
        S = {n: self.sem(f"at{L}_{n}") for n in (
            "w_high", "w_low", "prep", "x_ready", "proj", "moved", "rope_add", "ycls", "yc", "qm", "qc", "qm_first", "scores", "max", "exp", "turned",
            "pt", "pex", "pv", "y", "rs", "own", "collected", "tail_turned", "tail_moved", "spread", "yadd", "yn",
            "out", "onto_x", "vpad")}
        CREDIT = 8
        w, whl, wo, bb, bv = self.a_w, self.a_whl, self.a_wo, self.a_b, self.a_bv
        TERMS = ((0, 0), (0, 1), (1, 0))
        qk, v_all, ident = self.a_qk, self.a_v_all, self.const("ident")
        prob, pt, nm = self.a_p, self.a_pt, self.a_nm
        SUM_GUARD = 1e-20
        if full:
            units = [("q", t, 128 * t) for t in range(2)] + [("k", t, 256 + 128 * t) for t in range(2)]
            vcol = 512
        else:
            units = [(n, t, 256 * m + 128 * t) for t in range(2) for m, n in enumerate(("q", "qs"))]
            units += [(n, t, 512 + 256 * m + 128 * t) for t in range(2) for m, n in enumerate(("k", "ks"))]
            vcol = 1024
        CLS_UNITS = units if full else []
        units = units + [("v", t, vcol) for t in range(QT)] + ([("vc", 0, vcol)] if full else [])
        NU = len(units)
        ALL_UNITS = NB * NU + len(CLS_UNITS)
        BANKS = [psS[:, n, :] for n in range(4)] + [psT[:, n, :] for n in range(2)] + [psY[:, n, :] for n in range(2)]
        NBK = 7 if full else 5
        assert 2 * NU % NBK == 0 and NBK <= CREDIT
        NH = HEADS + (1 if full else 0)
        NG = 4 + (1 if full else 0)
        VALUES = {5: 0, 9: 1, (15 if full else 13): 2}

        def credit(e, *names):
            for name in names:
                e.nop().then_inc(S[name], CREDIT)

        def over_images(image):
            def run(e, own=None, per=0):
                with e.Fori(0, NB // 2 - 1) as i:
                    if own:
                        own.enter(i, 2 * per)
                    for s in range(2):
                        image(s, i * 2 + s, True)
                    if own:
                        own.leave(NB // 2 - 1)
                image(0, NB - 2, True)
                image(1, NB - 1, False)
            return run

        def unit_slot(s, u):
            return (s * NH + u) % 2

        def group_slot(s, g):
            return (s * NG + g) % 2

        AHEAD = 2

        def ahead_of(s, b, u):
            return (s, b, u + AHEAD) if u + AHEAD < NH else (1 - s, b + 1, u + AHEAD - NH)

        def cols(b, first, count):
            return span(b * T + first, count)

        LOADED = 48 + 80 * L
        NW = 768 if full else 1280

        NPREP = 4 if full else 4 + 2

        def pool(e):
            credit(e, "rope_add", "qm")

            def wait(name, value):
                if isinstance(value, int) and value <= CREDIT:
                    return
                e.wait_ge(S[name], value)
                e.nop().then_inc(self.paced, 1)

            def load(s, b):
                wait("proj", (b - 1) * NU + CREDIT)
                e.tensor_copy(self.a_x[:, s], self.xa_hl[:, :, :, span(b * 256, 256)]).then_inc(S["x_ready"], 1)
                if full:
                    for z in range(2):
                        e.tensor_copy(self.a_xc[:, s, z], self.xa_hl[:, z, :, span(b + NB * 256, 1)].to_broadcast([P, DT, 16])).then_inc(S["x_ready"], 1)

            def image_rope(s, b, more):
                if more:
                    load(1 - s, b + 1)
                if not full:
                    for n in range(4):
                        wait("moved", b * NU + 2 * n + 2 + CREDIT)
                        e.tensor_tensor(qk[:, n, cols(b, 1, 256)], self.a_rope[:, n % 2, 0], self.a_rope[:, n % 2, 1],
                                        ALU.add).then_inc(S["rope_add"], 1)
            load(0, 0)
            over_images(image_rope)(e)
            e.wait_ge(S["moved"], ALL_UNITS + CREDIT)
            for m in (self.a_v, self.a_vc, self.a_rst, self.a_pext):
                e.memset(m[:], 0.0).then_inc(S["prep"], 1)

            def operands(s, b):
                wait("scores", b * NH - NH + CREDIT)
                mask = self.const("headmask").unsqueeze(2).to_broadcast([P, 8, 256])
                first = isinstance(b, int) and b == 0
                for t in range(0 if first else 2):
                    q = qk[:, t, cols(b, 1, 256)].unsqueeze(1).to_broadcast([P, 8, 256])
                    e.tensor_tensor(self.a_qm[:, s, 8 * t:8 * t + 8], q, mask, ALU.mult).then_inc(S["qm"], 1)
                if full:
                    e.tensor_tensor(self.a_qc[:, s], qk[:, 0:2, cols(b, 0, 1)].to_broadcast([P, DT, 16]),
                                    self.const("clsheads").rearrange("p (t h) -> p t h", t=2), ALU.mult).then_inc(S["qc"], 1)
                wait("pv", b * NG - NG + CREDIT)
                for t in range(QT):
                    src = v_all[:, span(b, 1), t]
                    e.tensor_copy(self.a_v[:, s, t].rearrange("p (h s) -> p h s", s=32)[:, :, 0:HD],
                                  src.rearrange("p o (h s) -> p (o h) s", s=HD)).then_inc(S["vpad"], 1)
            e.wait_ge(S["moved"], ALL_UNITS + CREDIT)
            if not full:
                e.wait_ge(S["rope_add"], NB * 4 + CREDIT)
            e.wait_ge(S["prep"], NPREP)
            operands(0, 0)
            over_images(lambda s, b, more: operands(1 - s, b + 1) if more else None)(e)

            def collect(s, b):
                at = span(b, 1)
                wait("tail_turned", b - 1 + CREDIT)
                wait("spread", (b - 1) * 4 + CREDIT)
                e.tensor_copy(self.a_rs[:, s], self.a_rs_all[:, at].rearrange("p o i h -> p (o i) h")).then_inc(S["collected"], 1)
                if full:
                    e.tensor_copy(self.a_pexs[:, s], self.a_pex_all[:, at].rearrange("p o i h -> p (o i) h")).then_inc(S["collected"], 1)
                    e.tensor_tensor(self.a_vc[0:16, s].rearrange("p (h s) -> p h s", s=32)[:, :, 0:HD],
                                    self.a_vt[:, at].rearrange("p o (h s) -> p (o h) s", s=HD),
                                    self.const("diag")[0:16, :].unsqueeze(2).to_broadcast([16, HEADS, HD]), ALU.mult).then_inc(S["collected"], 1)

            e.wait_ge(S["rs"], NB + CREDIT)
            collect(0, 0)
            over_images(lambda s, b, more: collect(1 - s, b + 1) if more else None)(e)


        def pe(e):
            credit(e, "proj", "scores", "turned", "pv", "tail_turned", "spread", "out")
            e.wait_ge(self.attention_loaded, LOADED)

            e.wait_ge(S["w_low"], 1)

            def project(name, col, x, out, count):
                terms = [(dt, a, z) for dt in range(DT) for a, z in TERMS]
                for n, (dt, a, z) in enumerate(terms):
                    st, sp_ = n == 0, n == len(terms) - 1
                    at = NW * dt + col
                    if name in ("v", "vc"):
                        m = e.matmul(out[0:count, 0:D], x(z, dt), whl[:, a, at:at + D], start=st, stop=sp_)
                    else:
                        m = e.matmul(out[:, 0:count], whl[:, a, at:at + P], x(z, dt), start=st, stop=sp_)
                m.then_inc(S["proj"], 1)

            def image_units(s, b, more):
                e.wait_ge(S["x_ready"], (b + 1) * (3 if full else 1))
                for n, (name, t, col) in enumerate(units):
                    e.wait_ge(S["moved"], b * NU + n - NBK + 1 + CREDIT)
                    bank = BANKS[(s * NU + n) % NBK]
                    if name == "v":
                        project(name, col, lambda z, dt: self.a_x[:, s, z, dt, 128 * t:128 * t + 128], bank, P)
                    elif name == "vc":
                        project(name, col, lambda z, dt: self.a_xc[:, s, z, dt], bank, 16)
                    else:
                        project(name, col, lambda z, dt: self.a_x[:, s, z, dt], bank, 256)
            over_images(image_units)(e)
            for n, (name, t, col) in enumerate(CLS_UNITS):
                e.wait_ge(S["moved"], NB * NU + n - NBK + 1 + CREDIT)
                project(name, col, lambda z, dt: self.xa_hl[:, z, dt, NB * 256:NB * 256 + NB], BANKS[n % NBK], NB)
            e.wait_ge(S["moved"], ALL_UNITS + CREDIT)
            if not full:
                e.wait_ge(S["rope_add"], NB * 4 + CREDIT)
            e.wait_ge(S["prep"], NPREP)

            def scores(s, b, u):
                k, slot = b * NH + u, unit_slot(s, u)
                if u % 8 == 0 and u < HEADS:
                    e.wait_ge(S["qm"], (b - 1) * 2 + u // 8 + 1 + CREDIT)
                if u == HEADS:
                    e.wait_ge(S["qc"], b + 1)
                e.wait_ge(S["exp"], k - 1 + CREDIT)
                if u < HEADS:
                    for i in range(QT):
                        out = psS[:, 2 * slot + i, 0:NK]
                        if not full:
                            e.matmul(out, self.a_identb[:], self.a_maskb[:, i], start=True, stop=False)
                        m = e.matmul(out, self.a_qm[:, s, u, 128 * i:128 * i + 128], qk[:, 2 + u // 8, cols(b, K0, NK)],
                                     start=full, stop=True)
                else:
                    e.nop().then_inc(self.paced, 1)
                    for t in range(2):
                        m = e.matmul(psS[0:16, 2 * slot, 0:NK], self.a_qc[:, s, t], qk[:, 2 + t, cols(b, 0, NK)], start=t == 0, stop=t == 1)
                m.then_inc(S["scores"], 1)

            def turn(s, b, u):
                k, slot = b * NH + u, unit_slot(s, u)
                e.wait_ge(S["exp"], k + 1 + CREDIT)
                e.wait_ge(S["pt"], k - 1 + CREDIT)
                if u == HEADS:
                    e.nop().then_inc(self.paced, 1)
                    for kt in range(2):
                        m = e.transpose(psT[:, slot, 16 * kt:16 * kt + 16], self.a_pc[:, 1 + 128 * kt:129 + 128 * kt], ident[0:16, 0:16])
                else:
                    for kt in range(2):
                        for i in range(QT):
                            at, key = kt * 256 + i * 128, NK - 256 + 128 * kt
                            m = e.transpose(psT[:, slot, at:at + 128], prob[:, slot, i, key:key + 128], ident)
                m.then_inc(S["turned"], 1)

            def values(s, b, g):
                c, slot = b * NG + g, group_slot(s, g)
                e.wait_ge(S["pt"], b * NH + min(4 * g + 4, NH) + CREDIT)
                e.wait_ge(S["y"], c - 1 + CREDIT)
                if g == 0:
                    e.wait_ge(S["vpad"], b * QT + QT)
                if g == 4:
                    for gg in range(4):
                        for kt in range(2):
                            m = e.matmul(psY[:, slot, 16 * gg:16 * gg + 16], self.a_v[:, s, kt, P * gg:P * gg + P], self.a_pct[:, s, kt],
                                         start=kt == 0, stop=kt == 1)
                    m.then_inc(S["pv"], 1)
                    return
                for kt in range(2):
                    for j in range(GRP):
                        h = GRP * g + j
                        m = e.matmul(psY[32 * j:32 * j + 32, slot, 0:256], self.a_v[:, s, kt, 32 * h:32 * h + 32],
                                     pt[:, h % 8, 256 * kt:256 * kt + 256], start=kt == 0, stop=kt == 1)
                m.then_inc(S["pv"], 1)

            def image_heads(s, b, more):
                for u in range(NH):
                    if u + AHEAD < NH or more:
                        scores(*ahead_of(s, b, u))
                    turn(s, b, u)
                    if u in VALUES:
                        values(s, b, VALUES[u])
                for g in range(3, NG):
                    values(s, b, g)
            e.wait_ge(S["qm_first"], HEADS)
            for u in range(AHEAD):
                scores(0, 0, u)
            over_images(image_heads)(e)

            def tail_turn(s, b):
                e.wait_ge(S["collected"], (b + 1) * COLLECTED)
                e.wait_ge(S["tail_moved"], (b - 1) * TAIL_MOVED + CREDIT)
                for i in range(QT):
                    m = e.transpose(psT[0:16, s, 128 * i:128 * i + 128], self.a_rs[:, s, i, :], ident)
                if full:
                    for i in range(QT):
                        m = e.transpose(psT[0:16, s, 256 + 128 * i:384 + 128 * i], self.a_pexs[:, s, i, :], ident)
                m.then_inc(S["tail_turned"], 1)

            def spread(s, b):
                e.wait_ge(S["tail_moved"], (b + 1) * TAIL_MOVED + CREDIT)
                for g in range(4):
                    if full:
                        e.wait_ge(S["yn"], b * 4 + g - 1 + CREDIT)
                        m = e.matmul(psS[:, 2 + g % 2, 0:T], self.const("spread")[:, P * g:P * g + P], self.a_rst[:, s], start=True, stop=True)
                        m = e.matmul(psS[:, g % 2, 0:T], self.a_vc[:, s, P * g:P * g + P], self.a_pext[:, s], start=True, stop=True)
                    else:
                        e.wait_ge(S["yn"], (b - 1) * 4 + g + 1 + CREDIT)
                        m = e.matmul(psS[:, g, 0:256], self.const("spread")[:, P * g:P * g + P], self.a_rst[:, s, 1:T], start=True, stop=True)
                    m.then_inc(S["spread"], 1)

            def out_projection(s, b):
                e.wait_ge(S["yn"], b * 4 + 4 + CREDIT)
                e.wait_ge(S["onto_x"], b * 2 + CREDIT)
                for i in range(QT):
                    for g in range(4):
                        m = e.matmul(psY[:, i, 0:D], self.a_yn[:, s, g, 1 + P * i:1 + P * i + P], wo[:, g], start=g == 0, stop=g == 3)
                m.then_inc(S["out"], 1)

            def image_tail(s, b, more):
                if more:
                    tail_turn(1 - s, b + 1)
                out_projection(s, b)
                if more:
                    spread(1 - s, b + 1)
            e.wait_ge(S["pt"], NB * NH + CREDIT)
            e.wait_ge(S["y"], NB * NG + CREDIT)
            tail_turn(0, 0)
            spread(0, 0)
            over_images(image_tail)(e)
            if full:
                e.wait_ge(S["onto_x"], NB * 2 + CREDIT)
                e.wait_ge(S["ycls"], NB + CREDIT)
                for g in range(4):
                    m = e.matmul(psY[0:NB, 0, 0:D], self.a_ycls[:, g], wo[:, g], start=g == 0, stop=g == 3)
                m.then_inc(S["out"], 1)

        def act(e):
            credit(e, "exp", "y", "tail_moved")
            e.wait_ge(self.attention_loaded, LOADED)
            e.activation(whl[:, 0, 0:DT * NW], w[:, 0:DT * NW], ACT.Copy).then_inc(S["w_high"], 1)

            def exp(s, b, u):
                k, slot = b * NH + u, unit_slot(s, u)
                e.wait_ge(S["max"], k + 1)
                e.wait_ge(S["turned"], k - 1 + CREDIT)
                if u == 0:
                    e.wait_ge(S["rs"], b - 1 + CREDIT)
                if full and u < HEADS:
                    e.wait_ge(S["pex"], b * HEADS + max(u - 1, 0) + CREDIT)
                if u < HEADS:
                    for i in range(QT):
                        m = e.activation(prob[:, slot, i, 0:NK], psS[:, 2 * slot + i, 0:NK], ACT.Exp,
                                         bias=nm[:, u, i:i + 1], accum_out=self.a_sum[:, s, i, u:u + 1])
                else:
                    e.wait_ge(S["rs"], b + CREDIT)
                    m = e.activation(self.a_pc[:, 0:NK], psS[0:16, 2 * slot, 0:NK], ACT.Exp,
                                     bias=nm[0:16, u, 0:1], accum_out=self.a_rsc[:, s:s + 1])
                m.then_inc(S["exp"], 1)

            def y_out(s, b, g):
                slot = group_slot(s, g)
                e.wait_ge(S["pv"], b * NG + g + 1 + CREDIT)
                if g == 4:
                    m = e.activation(self.a_yc_all[:, span(b, 1)].rearrange("p o c -> p (o c)"),
                                     psY[:, slot, 0:64], ACT.Copy)
                else:
                    m = e.activation(qk[:, g, cols(b, 1, 256)], psY[:, slot, 0:256], ACT.Copy)
                m.then_inc(S["y"], 1)

            def image_heads(s, b, more):
                for u in range(NH):
                    if u + AHEAD < NH or more:
                        exp(*ahead_of(s, b, u))
                    if u in VALUES:
                        y_out(s, b, VALUES[u])
                for g in range(3, NG):
                    y_out(s, b, g)
            for u in range(AHEAD):
                exp(0, 0, u)
            over_images(image_heads)(e)

            def move_tail(s, b):
                at = span(b, 1)
                e.wait_ge(S["tail_turned"], b + 1 + CREDIT)
                if full:
                    e.activation(self.a_rst[0:16, s, 0:1], self.a_rsc_all[0:16, at], ACT.Copy).then_inc(S["tail_moved"], 1)
                    e.activation(self.a_pext[0:16, s, 1:T], psT[0:16, s, 256:512], ACT.Copy).then_inc(S["tail_moved"], 1)
                    e.activation(self.a_pext[0:16, s, 0:1], self.a_pc0_all[0:16, at], ACT.Copy).then_inc(S["tail_moved"], 1)
                e.activation(self.a_rst[0:16, s, 1:T], psT[0:16, s, 0:256], ACT.Copy).then_inc(S["tail_moved"], 1)
            move_tail(0, 0)
            over_images(lambda s, b, more: move_tail(1 - s, b + 1) if more else None)(e)

        COLLECTED = 3 if full else 1
        TAIL_MOVED = 4 if full else 1

        def dve(e):
            own = Own(e, S["own"])
            credit(e, "moved", "pt", "pex", "rs", "yn", "onto_x", "ycls")
            e.wait_ge(self.attention_loaded, LOADED)
            e.wait_ge(S["w_high"], 1)
            e.tensor_tensor(whl[:, 1, 0:DT * NW], w[:, 0:DT * NW], whl[:, 0, 0:DT * NW].bitcast(F32), ALU.subtract).then_inc(S["w_low"], 1)
            if full:
                own.did(e.tensor_scalar(bb[:, 0:2], bb[:, 0:2], 0.25, None, ALU.mult))
                own.wait()
            else:
                e.tensor_copy(self.a_maskb[:], self.table("maskq").rearrange("p (i k) -> p i k", i=QT)).then_inc(S["prep"], 1)
                e.tensor_copy(self.a_identb[:], ident).then_inc(S["prep"], 1)

            def q_or_k(name, t, bank, n, dst):
                if name == "q":
                    return e.tensor_scalar(dst, bank[:, 0:n], 0.25, bb[:, t:t + 1], ALU.mult, ALU.add)
                return e.tensor_scalar(dst, bank[:, 0:n], bb[:, 2 + t:3 + t], None, ALU.add)

            def image_units(s, b, more):
                for n, (name, t, _) in enumerate(units):
                    e.wait_ge(S["proj"], b * NU + n + 1 + CREDIT)
                    bank = BANKS[(s * NU + n) % NBK]
                    at = span(b, 1)
                    if name == "v":
                        dst = v_all[:, at, t].rearrange("p o d -> p (o d)")
                        m = e.tensor_tensor(dst, bank[:, 0:D], bv[:], ALU.add) if full else e.tensor_copy(dst, bank[:, 0:D])
                    elif name == "vc":
                        m = e.tensor_tensor(self.a_vt[:, at].rearrange("p o d -> p (o d)"), bank[0:16, 0:D], bv[0:16, :], ALU.add)
                    elif full:
                        m = q_or_k(name, t, bank, 256, qk[:, t + (0 if name == "q" else 2), cols(b, 1, 256)])
                    else:
                        r = 0 if name[0] == "q" else 2
                        e.wait_ge(S["rope_add"], b * 4 + r + t - 1 + CREDIT)
                        tab = self.table(("c" if len(name) == 1 else "s") + name[0])
                        m = e.tensor_tensor(self.a_rope[:, t, len(name) - 1], bank[:, 0:256], tab, ALU.mult)
                    m.then_inc(S["moved"], 1)
            over_images(image_units)(e)
            for n, (name, t, _) in enumerate(CLS_UNITS):
                e.wait_ge(S["proj"], NB * NU + n + 1 + CREDIT)
                dst = qk[:, t + (0 if name == "q" else 2)].rearrange("p (b t) -> p b t", t=T)[:, :, 0]
                q_or_k(name, t, BANKS[n % NBK], NB, dst).then_inc(S["moved"], 1)

            def maximum(s, b, u):
                slot = unit_slot(s, u)
                e.wait_ge(S["scores"], b * NH + u + 1 + CREDIT)
                if u < HEADS:
                    m = e.tensor_reduce(nm[:, u, :], psS[:, 2 * slot:2 * slot + 2, 0:NK], AX, ALU.max, negate=True)
                else:
                    m = e.tensor_reduce(nm[0:16, u, 0:1], psS[0:16, 2 * slot, 0:NK], AX, ALU.max, negate=True)
                m.then_inc(S["max"], 1)

            def move_turned(s, b, u):
                k, slot = b * NH + u, unit_slot(s, u)
                e.wait_ge(S["turned"], k + 1 + CREDIT)
                if u == HEADS:
                    e.tensor_copy(self.a_pct[:, s].rearrange("p k h -> p (k h)"), psT[:, slot, 0:32]).then_inc(S["pt"], 1)
                    return
                if full:
                    e.tensor_copy(self.a_pex[:, :, u:u + 1], prob[:, slot, :, 0:1]).then_inc(S["pex"], 1)
                before = u // 4 - 2
                e.wait_ge(S["pv"], b * NG + (before + 1 if before >= 0 else before + 5 - NG) + CREDIT)
                e.tensor_copy(pt[:, u % 8], psT[:, slot, :]).then_inc(S["pt"], 1)

            def sums(s, b):
                e.wait_ge(S["exp"], b * NH + NH + CREDIT)
                at = span(b, 1)
                rs = self.a_rs_all[:, at].rearrange("p o i h -> p (o i) h")
                own.did(e.tensor_scalar(self.a_st[:], self.a_sum[:, s], SUM_GUARD, None, ALU.max))
                own.wait()
                if full:
                    own.did(e.reciprocal(self.a_rsc_all[0:16, at], self.a_rsc[:, s:s + 1]))
                    own.did(e.tensor_copy(self.a_pc0_all[0:16, at], self.a_pc[:, 0:1]))
                    e.wait_ge(S["pex"], b * HEADS + HEADS + CREDIT)
                    own.did(e.tensor_copy(self.a_pex_all[:, at].rearrange("p o i h -> p (o i) h"), self.a_pex[:]))
                    own.did(e.reciprocal(rs, self.a_st[:]))
                else:
                    own.did(e.reciprocal(self.a_st[:], self.a_st[:]))
                    own.wait()
                    own.did(e.tensor_tensor(rs, self.a_st[:], self.const("valid").unsqueeze(2).to_broadcast([P, QT, HEADS]), ALU.mult))
                own.wait()
                e.nop().then_inc(S["rs"], 1)

            def image_heads(s, b, more):
                for u in range(NH):
                    if u + AHEAD < NH or more:
                        maximum(*ahead_of(s, b, u))
                    move_turned(s, b, u)
                sums(s, b)
            e.wait_ge(S["moved"], ALL_UNITS + CREDIT)
            if not full:
                e.wait_ge(S["rope_add"], NB * 4 + CREDIT)
            for h in range(HEADS):
                e.tensor_scalar(self.a_qm[:, 0, h], qk[:, h // 8, 1:T], self.const("headmask")[:, h % 8:h % 8 + 1], None,
                                ALU.mult).then_inc(S["qm_first"], 1)
            e.wait_ge(S["prep"], NPREP)
            for u in range(AHEAD):
                maximum(0, 0, u)
            over_images(image_heads)(e, own, 5 if full else 3)

            def normalise(s, b):
                e.wait_ge(S["out"], b - 1 + CREDIT)
                if full:
                    e.wait_ge(S["ycls"], b - 1 + CREDIT)
                    e.tensor_tensor(self.a_yc[:, s], self.a_yc_all[:, span(b, 1)].rearrange("p o (g h) -> p (o g) h", h=16),
                                    self.const("clspick").rearrange("p (g h) -> p g h", h=16), ALU.mult).then_inc(S["yc"], 1)
                    e.wait_ge(S["yc"], b * 2 + 1)
                    e.tensor_reduce(qk[:, :, cols(b, 0, 1)], self.a_yc[:, s], AX, ALU.add).then_inc(S["yc"], 1)
                    e.wait_ge(S["yc"], b * 2 + 2)

                def divide(g):
                    if full:
                        e.wait_ge(S["yadd"], b * 4 + g + 1)
                        e.tensor_tensor(self.a_yn[:, s, g], qk[:, g, cols(b, 0, T)], psS[:, 2 + g % 2, 0:T], ALU.mult).then_inc(S["yn"], 1)
                    else:
                        e.tensor_tensor(self.a_yn[:, s, g, 1:T], qk[:, g, cols(b, 1, 256)], psS[:, g, 0:256], ALU.mult).then_inc(S["yn"], 1)
                for g in range(4):
                    e.wait_ge(S["spread"], b * 4 + g + 1 + CREDIT)
                    if full:
                        y = qk[:, g, cols(b, 0, T)]
                        e.tensor_tensor(y, y, psS[:, g % 2, 0:T], ALU.add).then_inc(S["yadd"], 1)
                    divide(g)

            def onto_x(s, b):
                e.wait_ge(S["out"], b + 1 + CREDIT)
                for i in range(QT):
                    n = b * 2 + i
                    dst = X[:, span(n, 1)].rearrange("p o d -> p (o d)")
                    e.tensor_tensor(dst, psY[:, i, 0:D], dst, ALU.add).then_inc(S["onto_x"], 1)
                if full:
                    e.wait_ge(S["onto_x"], b * 2 + 2 + CREDIT)
                    for i in range(QT):
                        n = b * 2 + i
                        dst = X[:, span(n, 1)].rearrange("p o d -> p (o d)")
                        e.tensor_tensor(dst, dst, self.a_bo[:], ALU.add)
                    e.wait_ge(S["yn"], b * 4 + 4 + CREDIT)
                    at = span(b, 1)
                    e.tensor_copy(self.a_ycls[:, :, at], self.a_yn[:, s, :, 0:1]).then_inc(S["ycls"], 1)

            def image_tail(s, b, more):
                normalise(s, b)
                onto_x(s, b)
            over_images(image_tail)(e)
            if full:
                e.wait_ge(S["out"], NB + 1 + CREDIT)
                dst = X[0:NB, NT - 1]
                own.did(e.tensor_tensor(dst, psY[0:NB, 0, 0:D], dst, ALU.add))
                own.wait()
                own.did(e.tensor_tensor(dst, dst, self.a_bo[0:NB], ALU.add))
        return {"pool": pool, "pe": pe, "act": act, "dve": dve}

    def router(self, L):
        A, psT, psS = self.A, self.psT, self.psS
        S = {n: self.sem(f"rt{L}_{n}") for n in ("logits", "own", "shift", "exp", "picked", "counted",
                                                   "placed")}

        def pe(e):
            for n in range(NT):
                m = e.transpose(psT[:, 0, E * n:E * n + E], self.g_lt[:, P * n:P * n + P], self.const("ident")[0:E, 0:E])
            m.then_inc(S["logits"], 1)
            e.wait_ge(S["picked"], 1)
            sel = self.g_sel[:].rearrange("p n e -> p (n e)")
            e.matmul(psS[:, 0, 0:NT * E], self.const("before"), sel, start=True, stop=True)
            e.matmul(psS[:, 1, 0:NT * E], self.const("ones"), sel, start=True, stop=True).then_inc(S["counted"], 1)

        def act(e):
            e.wait_ge(S["shift"], 1)
            e.activation(self.g_p[:], self.g_p[:], ACT.Exp).then_inc(S["exp"], 1)

        def dve(e):
            own = Own(e, S["own"])
            p, sel, m4, cmp_, tmp = self.g_p, self.g_sel, self.g_m, self.g_cmp, self.g_tmp

            def step(ins):
                own.did(ins)
                own.wait()

            def over_e(x, shape=(P, NT, E)):
                return x.unsqueeze(2).to_broadcast(list(shape))
            e.wait_ge(S["logits"], 1)
            logits = psT[:, 0, 0:E * NT].rearrange("p (n e) -> p n e", e=E)
            step(e.tensor_tensor(p[:], logits, self.r_b[:].unsqueeze(1).to_broadcast([P, NT, E]), ALU.add))
            step(e.tensor_reduce(m4[:, 0], p[:], AX, ALU.max))
            e.tensor_tensor(p[:], p[:], over_e(m4[:, 0]), ALU.subtract).then_inc(S["shift"], 1)
            e.wait_ge(S["exp"], 1)
            step(e.tensor_reduce(m4[:, 1], p[:], AX, ALU.add))
            step(e.reciprocal(m4[:, 2], m4[:, 1]))
            step(e.tensor_tensor(p[:], p[:], over_e(m4[:, 2]), ALU.mult))
            shape = [P, NT, E, E]
            mine = p[:].unsqueeze(3).to_broadcast(shape)
            other = p[:].unsqueeze(2).to_broadcast(shape)
            tri = self.const("tri").rearrange("p (a b) -> p a b", a=E)
            own.did(e.tensor_tensor(cmp_[:, 0], other, mine, ALU.is_gt))
            step(e.tensor_tensor(cmp_[:, 1], other, mine, ALU.is_equal))
            step(e.tensor_tensor(cmp_[:, 1], cmp_[:, 1], tri.unsqueeze(1).to_broadcast(shape), ALU.mult))
            step(e.tensor_tensor(cmp_[:, 0], cmp_[:, 0], cmp_[:, 1], ALU.add))
            step(e.tensor_reduce(tmp[:], cmp_[:, 0], AX, ALU.add))
            real = over_e(self.const("real"))
            for j in range(TOP):
                step(e.tensor_scalar(self.g_pick[:, j], tmp[:], float(j), None, ALU.is_equal))
                step(e.tensor_tensor(self.g_pick[:, j], self.g_pick[:, j], real, ALU.mult))
            e.tensor_tensor(sel[:], self.g_pick[:, 0], self.g_pick[:, 1], ALU.add).then_inc(S["picked"], 1)
            for j in range(TOP):
                step(e.tensor_tensor(tmp[:], p[:], self.g_pick[:, j], ALU.mult))
                step(e.tensor_reduce(self.gates[:, j], tmp[:], AX, ALU.add))
            if L == 0:
                own.did(e.tensor_scalar(self.gates[:, 0:TOP], self.gates[:, 0:TOP], 0.5, None, ALU.mult))
            e.wait_ge(S["counted"], 1)
            step(e.tensor_copy(self.g_tot[:].rearrange("p n e -> p (n e)"), psS[:, 1, 0:NT * E]))
            step(e.memset(self.g_carry[:, 0], 0.0))
            for n in range(NT):
                step(e.tensor_tensor(self.g_carry[:, n + 1], self.g_carry[:, n], self.g_tot[:, n], ALU.add))
            total = self.g_carry[:, NT]
            need, start = self.g_cnt[:, 0], self.g_cnt[:, 1]
            steps = cmp_[:, 0, 0, :, 0:STEPS]
            step(e.tensor_tensor(steps, total.unsqueeze(2).to_broadcast([P, E, STEPS]),
                                 self.const("steps").unsqueeze(1).to_broadcast([P, E, STEPS]), ALU.is_gt))
            step(e.tensor_reduce(need, steps, AX, ALU.add))
            lower = cmp_[:, 1, 0]
            step(e.tensor_tensor(lower, tri, need.unsqueeze(1).to_broadcast([P, E, E]), ALU.mult))
            step(e.tensor_reduce(start, lower, AX, ALU.add))
            step(e.tensor_tensor(self.g_big[:], start.unsqueeze(1).to_broadcast([P, ROUTED, E]),
                                 self.const("blocks").unsqueeze(2).to_broadcast([P, ROUTED, E]), ALU.is_le))
            started = tmp[:].rearrange("p n e -> p (n e)")[:, 0:ROUTED]
            step(e.tensor_reduce(started, self.g_big[:], AX, ALU.add))
            own.did(e.tensor_scalar(self.expert_of[:, FIRST:FIRST + ROUTED], started, -1.0, None, ALU.add))
            own.did(e.memset(self.expert_of[:, 0:FIRST], E))
            own.did(e.memset(self.expert_of[:, FIRST + ROUTED:BLOCKS], E))
            step(e.tensor_scalar(start, start, float(BL), None, ALU.mult))
            step(e.tensor_tensor(self.g_tot[:], self.g_carry[:, 0:NT], start.unsqueeze(1).to_broadcast([P, NT, E]), ALU.add))
            step(e.tensor_tensor(self.g_tot[:], self.g_tot[:], psS[:, 0, 0:NT * E].rearrange("p (n e) -> p n e", e=E), ALU.add))
            for j in range(TOP):
                step(e.tensor_tensor(tmp[:], self.g_tot[:], self.g_pick[:, j], ALU.mult))
                step(e.tensor_reduce(self.g_pos[:, j], tmp[:], AX, ALU.add))
            e.tensor_copy(self.where[:], self.g_pos[:]).then_inc(S["placed"], 1)
        return {"pe": pe, "act": act, "dve": dve}

    def expert_shape(self, L):
        return (8, 2048, 3) if L == 0 else (4, 1024, 2)

    def first_weights(self, L):
        _, PW, NP = self.expert_shape(L)
        came = [self.sem(f"fw{L}_came{j}") for j in range(NP)]
        high, low = self.sem(f"fw{L}_high"), self.sem(f"fw{L}_low")

        def sp(e):
            for j in range(NP):
                if j >= 2:
                    e.wait_ge(low, j - 1)
                e.dma_start(self.w_stage[:, j % 2, 0:PW], self.A[f"ffn{L}"][E, j]).then_inc(came[j], 16)

        def act(e, j):
            if j < NP:
                e.wait_ge(came[j], 16)
                e.activation(self.w_hi[:, 1, PW * j:PW * j + PW], self.w_stage[:, j % 2, 0:PW], ACT.Copy).then_inc(high, 1)

        def pool(e):
            for j in range(NP):
                e.wait_ge(high, j + 1)
                at = slice(PW * j, PW * j + PW)
                e.tensor_tensor(self.w_lo[:, 1, at], self.w_stage[:, j % 2, 0:PW], self.w_hi[:, 1, at].bitcast(F32),
                                ALU.subtract).then_inc(low, 1)
        return sp, act, pool

    def experts(self, L):
        A, X, psS, psT, psY = self.A, self.X, self.psS, self.psT, self.psY
        gated = L == 0
        FT, PW, NP = self.expert_shape(L)
        O2 = (NP - 1) * PW
        SHARED_GATE = 1.0 / 16 if L == 0 else 1.0
        CREDIT = 3
        TERMS = ((0, 0), (0, 1), (1, 0))
        names = ["xt", "x_in", "x_hi", "x_lo", "gu", "act", "hraw", "hhi", "h", "y", "y_moved", "biased", "added"]
        names += [f"{a}{j}" for a in ("w_in", "w_hi", "w_lo") for j in range(NP)]
        names += [f"{a}{s}" for a in ("b_in", "y_out") for s in range(2)]
        S = {n: self.sem(f"ex{L}_{n}") for n in names}
        w = (self.w_hi, self.w_lo)
        TAIL = FIRST + ROUTED
        I0, I1 = FIRST // 2, TAIL // 2
        LASTB = BLOCKS - 1

        def is_shared(t):
            return isinstance(t, int) and not FIRST <= t < TAIL

        def tiles(t):
            n = SUB * (t if t < FIRST else t - ROUTED)
            return range(n, min(n + SUB, NT))

        def columns(t):
            return P * len(tiles(t)) if is_shared(t) else BL

        def weights_slot(slot, t):
            return slot if not is_shared(t) else (1 if t < FIRST else 0)

        def sets(t):
            return TAIL - FIRST + 1 if isinstance(t, int) and t >= TAIL else t - FIRST + 1

        def stage_slot(j, slot):
            return (NP * slot + j) % 2

        def credit(e, *names):
            for name in names:
                e.nop().then_inc(S[name], CREDIT)

        def over_blocks(block, ahead):
            def run(e):
                ahead(0, 0)
                for i in range(I0):
                    block(0, i, lambda: ahead(1, i))
                    block(1, i, lambda: ahead(0, i + 1))
                with e.Fori(I0, I1 - 1) as i:
                    block(0, i, lambda: ahead(1, i))
                    block(1, i, lambda: ahead(0, i + 1))
                for i in range(I1 - 1, BLOCKS // 2):
                    block(0, i, lambda: ahead(1, i))
                    block(1, i, (lambda: ahead(0, i + 1)) if 2 * i + 1 < LASTB else lambda: None)
            return run

        def sp(e):
            for s in range(2):
                e.nop().then_inc(S[f"y_out{s}"], 16)

            def expert(t):
                return e.value_load(self.expert_of[0:1, span(t, 1)],
                                    min_val=0, max_val=E)

            def weights(slot, t, ex):
                for j in range(NP):
                    if j >= 2:
                        e.wait_ge(S[f"w_lo{j - 2}"], sets(t))
                    elif not isinstance(t, int) or t > FIRST:
                        e.wait_ge(S[f"w_lo{j - 2 + NP}"], sets(t) - 1)
                    e.dma_start(self.w_stage[:, stage_slot(j, slot), 0:PW],
                                A[f"ffn{L}"][bass.ds(ex, 1), j].rearrange("o p w -> (o p) w")).then_inc(S[f"w_in{j}"], 16)

            def rows_of(dram, t):
                at = t * BL - FIRST * BL
                return dram[span(at, BL)].rearrange("(s p) d -> p s d", p=P)

            def rows(t):
                e.wait_ge(S["xt"], t)
                e.dma_start(self.e_rows[:], rows_of(self.rows_in, t)).then_inc(S["x_in"], 16)

            def biases(slot, t, ex):
                if gated:
                    return
                if not (isinstance(t, int) and t < 2):
                    e.wait_ge(S["y_moved"], (t - 1) * 2 + CREDIT)
                e.dma_start(self.w_b1[:, slot], A["ffn_b1"][bass.ds(ex, 1)].rearrange("o p w -> (o p) w")).then_inc(S[f"b_in{slot}"], 16)
                e.dma_start(self.w_b2[:, slot], A["ffn_b2"][bass.ds(ex, 1)].to_broadcast([P, D])).then_inc(S[f"b_in{slot}"], 16)

            def store(slot, t):
                e.wait_ge(S["y_moved"], (t + 1) * 2 + CREDIT)
                e.dma_start(rows_of(self.rows_out, t), self.e_y[:, slot]).then_inc(S[f"y_out{slot}"], 16)

            for t in range(FIRST):
                biases(t % 2, t, expert(t))
            for t in range(FIRST, FIRST + 2):
                ex = expert(t)
                weights(t % 2, t, ex)
                if t == FIRST:
                    e.wait_ge(self.scattered, 16 * NT * TOP * (L + 1))
                rows(t)
                biases(t % 2, t, ex)
            with e.Fori(I0, I1 - 1) as i:
                for slot in range(2):
                    t = i * 2 + slot
                    ex = expert(t + 2)
                    weights(slot, t + 2, ex)
                    rows(t + 2)
                    store(slot, t)
                    biases(slot, t + 2, ex)
            weights(0, TAIL, expert(TAIL))
            for slot in range(2):
                store(slot, TAIL - 2 + slot)
            for t in range(TAIL, BLOCKS):
                biases(t % 2, t, expert(t))

        def pe(e):
            credit(e, "y")

            def turn(slot, i):
                t = i * 2 + slot
                if is_shared(t):
                    rows = [self.n_rows[:, n] for n in tiles(t)]
                else:
                    e.wait_ge(S["x_in"], (t - FIRST) * 16 + 16)
                    rows = [self.e_rows[:, sub] for sub in range(SUB)]
                e.wait_ge(S["x_lo"], t + CREDIT)
                for sub, row in enumerate(rows):
                    for dt in range(DT):
                        m = e.transpose(psT[:, dt, P * sub:P * sub + P], row[:, P * dt:P * dt + P], self.const("ident"))
                m.then_inc(S["xt"], 1)

            def block(slot, i, ahead):
                t = i * 2 + slot
                ws, cols = weights_slot(slot, t), columns(t)
                e.wait_ge(S["x_lo"], t + 1 + CREDIT)
                first = isinstance(t, int) and t < FIRST
                if not first:
                    for j in range(NP - 1):
                        e.wait_ge(S[f"w_lo{j}"], sets(t))
                for f in range(FT):
                    if gated:
                        e.wait_ge(S["hraw"], t * FT + f - 1 + CREDIT)
                    else:
                        e.wait_ge(S["act"], t * FT + f - 1 + CREDIT)
                    for j in range(NP - 1):
                        n = 0
                        for dt in range(DT):
                            for a, z in TERMS:
                                at = PW * j + (PW // DT) * dt + P * f
                                m = e.matmul(psS[:, 2 * j + f % 2, 0:cols], w[a][:, ws, at:at + P], self.e_x[:, slot, z, dt, 0:cols],
                                             start=n == 0, stop=n == 2 * DT + 1)
                                n += 1
                    m.then_inc(S["gu"], 1)
                ahead()
                if not first:
                    e.wait_ge(S[f"w_lo{NP - 1}"], sets(t))
                for sub in range(cols // P):
                    if sub % 2 == 0:
                        e.wait_ge(S["y_moved"], (t - 1) * 2 + sub // 2 + 1 + CREDIT)
                    for f in range(FT):
                        if sub == 0:
                            e.wait_ge(S["h"], t * FT + f + 1 + CREDIT)
                        for n, (a, z) in enumerate(TERMS):
                            at = O2 + D * f
                            m = e.matmul(psY[:, sub // 2, D * (sub % 2):D * (sub % 2) + D], self.e_hl[:, z, f, P * sub:P * sub + P],
                                         w[a][:, ws, at:at + D], start=f == 0 and n == 0, stop=f == FT - 1 and n == 2)
                    if sub % 2 == 1 or sub == SUB - 1:
                        m.then_inc(S["y"], 1)
            over_blocks(block, turn)(e)

        WHEN = {0: (0, 0), 1: (0, 1), 2: (1, 0), 3: (1, 1)}
        if NP == 3:
            WHEN.update({FT - 2: (2, 0), FT - 1: (2, 1)})

        def act(e):
            credit(e, "act")

            def split(j, half, slot, i):
                t = i * 2 + slot
                if half == 0:
                    e.wait_ge(S[f"w_in{j}"], sets(t) * 16)
                    e.wait_ge(S["y"], (t - 1) * 2 + CREDIT)
                at = half * (PW // 2)
                e.activation(self.w_hi[:, slot, PW * j + at:PW * j + at + PW // 2],
                             self.w_stage[:, stage_slot(j, slot), at:at + PW // 2], ACT.Copy).then_inc(S[f"w_hi{j}"], 1)

            def x_hi(slot, i):
                t = i * 2 + slot
                e.wait_ge(S["xt"], t + 1)
                cols = columns(t)
                e.activation(self.e_x[:, slot, 0, :, 0:cols], psT[:, :, 0:cols], ACT.Copy).then_inc(S["x_hi"], 1)

            def block(slot, i, ahead):
                t = i * 2 + slot
                cols = columns(t)
                new = not isinstance(t, int) or FIRST <= t + 1 <= TAIL
                nxt = (1, i) if slot == 0 else (0, i + 1)
                if not gated:
                    e.wait_ge(S[f"b_in{slot}"], i * 32 + 32)
                for f in range(FT):
                    e.wait_ge(S["gu"], t * FT + f + 1)
                    if gated:
                        e.wait_ge(S["hraw"], t * FT + f - 1 + CREDIT)
                        e.activation(self.e_act[:, f % 2, 0:cols], psS[:, f % 2, 0:cols], ACT.Silu).then_inc(S["act"], 1)
                    else:
                        e.wait_ge(S["h"], t * FT + f - 1 + CREDIT)
                        e.activation(self.e_h[:, f % 2, 0:cols], psS[:, f % 2, 0:cols], ACT.Gelu,
                                     bias=self.w_b1[:, slot, f:f + 1]).then_inc(S["act"], 1)
                    if new and f in WHEN:
                        split(*WHEN[f], *nxt)
                ahead()
            over_blocks(block, x_hi)(e)

        def pool(e):
            for n in range(NT):
                m = P if n < NT - 1 else NB
                for j in range(TOP):
                    e.indirect_dma_start(self.rows_in, bass.IndirectOffsetOnAxis(ap=self.where[0:m, j, n:n + 1], axis=0),
                                         self.n_rows[0:m, n, :], None).then_inc(self.scattered, 16)

            def split(slot, i):
                t = i * 2 + slot
                for j in range(NP):
                    for half in range(2):
                        e.wait_ge(S[f"w_hi{j}"], (sets(t) - 1) * 2 + half + 1)
                        e.nop().then_inc(self.paced, 1)
                        at = half * (PW // 2)
                        to = slice(PW * j + at, PW * j + at + PW // 2)
                        m = e.tensor_tensor(self.w_lo[:, slot, to], self.w_stage[:, stage_slot(j, slot), at:at + PW // 2],
                                            self.w_hi[:, slot, to].bitcast(F32), ALU.subtract)
                    m.then_inc(S[f"w_lo{j}"], 1)
            split(0, I0)
            with e.Fori(I0, I1 - 1) as i:
                split(1, i)
                split(0, i + 1)
            split(1, I1 - 1)
            split(0, I1)
            e.wait_ge(self.scattered, 16 * NT * TOP * (L + 1))
            for s in range(2):
                e.wait_ge(S[f"y_out{s}"], 16 * (ROUTED // 2) + 16)
            for k in range(TOP * NT):
                j, n = divmod(k, NT)
                m = P if n < NT - 1 else NB
                if k >= BACK:
                    e.wait_ge(S["added"], k - BACK + 1)
                e.indirect_dma_start(self.n_rows[0:m, k % BACK, :], None, self.rows_out,
                                     bass.IndirectOffsetOnAxis(ap=self.where[0:m, j, n:n + 1], axis=0)).then_inc(self.gathered[k % BACK], 16)

        def dve(e):
            credit(e, "hraw", "h", "x_lo", "y_moved")
            biased, added = Own(e, S["biased"]), Own(e, S["added"])

            def x_lo(slot, i):
                t = i * 2 + slot
                e.wait_ge(S["x_hi"], t + 1)
                cols = columns(t)
                e.tensor_tensor(self.e_x[:, slot, 1, :, 0:cols], psT[:, :, 0:cols], self.e_x[:, slot, 0, :, 0:cols].bitcast(F32),
                                ALU.subtract).then_inc(S["x_lo"], 1)

            def add_routed(last):
                for k in range(added.n, min(last, TOP * NT)):
                    j, n = divmod(k, NT)
                    m = P if n < NT - 1 else NB
                    a = -(-(TOP * NT - k % BACK) // BACK)
                    e.wait_ge(self.gathered[k % BACK], 16 * (L * a + k // BACK + 1))
                    added.wait()
                    added.did(e.scalar_tensor_tensor(X[0:m, n], self.n_rows[0:m, k % BACK], self.gates[0:m, j, n:n + 1], X[0:m, n],
                                                     ALU.mult, ALU.add))

            def block(slot, i, ahead):
                t = i * 2 + slot
                cols = columns(t)
                for f in range(FT):
                    k = t * FT + f
                    e.wait_ge(S["act"], k + 1 + CREDIT)
                    raw = self.e_h[:, f % 2, 0:cols]
                    if gated:
                        e.wait_ge(S["h"], k - 1 + CREDIT)
                        e.tensor_tensor(raw, self.e_act[:, f % 2, 0:cols], psS[:, 2 + f % 2, 0:cols], ALU.mult).then_inc(S["hraw"], 1)
                        e.wait_ge(S["hraw"], k + 1 + CREDIT)
                    if f == 0:
                        e.wait_ge(S["y"], t * 2 + CREDIT)
                    e.tensor_copy(self.e_hl[:, 0, f, 0:cols], raw).then_inc(S["hhi"], 1)
                    e.wait_ge(S["hhi"], k + 1)
                    e.tensor_tensor(self.e_hl[:, 1, f, 0:cols], raw, self.e_hl[:, 0, f, 0:cols].bitcast(F32),
                                    ALU.subtract).then_inc(S["h"], 1)
                    if isinstance(t, int) and t >= TAIL:
                        add_routed(2 * ((t - TAIL) * FT + f - 3))
                ahead()
                if not is_shared(t):
                    e.wait_ge(S[f"y_out{slot}"], (i - I0) * 16 + 16)
                    for bank in range(2):
                        e.wait_ge(S["y"], t * 2 + bank + 1 + CREDIT)
                        n = min(2, SUB - 2 * bank)
                        src = psY[:, bank, 0:n * D].rearrange("p (n d) -> p n d", d=D)
                        dst = self.e_y[:, slot, 2 * bank:2 * bank + n]
                        if gated:
                            m = e.tensor_copy(dst, src)
                        else:
                            m = e.tensor_tensor(dst, src, self.w_b2[:, slot].unsqueeze(1).to_broadcast([P, n, D]), ALU.add)
                        m.then_inc(S["y_moved"], 1)
                    return
                for bank, n0 in enumerate(range(tiles(t)[0], tiles(t)[-1] + 1, 2)):
                    n = min(2, tiles(t)[-1] + 1 - n0)
                    dst = X[:, n0:n0 + n]
                    added.wait()
                    if not gated:
                        biased.did(e.tensor_tensor(dst, dst, self.w_b2[:, slot].unsqueeze(1).to_broadcast([P, n, D]), ALU.add))
                        biased.wait()
                    e.wait_ge(S["y"], t * 2 + bank + 1 + CREDIT)
                    e.scalar_tensor_tensor(dst, psY[:, bank, 0:n * D].rearrange("p (n d) -> p n d", d=D), SHARED_GATE, dst,
                                           ALU.mult, ALU.add).then_inc(S["y_moved"], 1)
                    done = t * 2 + bank + 1 + CREDIT
                if t >= TAIL:
                    e.wait_ge(S["y_moved"], done)
            over_blocks(block, x_lo)(e)
            add_routed(TOP * NT)
        return {"sp": sp, "act": act, "pool": pool, "dve": dve, "pe": pe}

    def write_out(self):
        stored = self.sem("o_stored")

        def sp(e):
            for i in range(QT):
                e.dma_start(self.out[:, 1 + P * i:1 + P * i + P, :].rearrange("b p d -> p b d"),
                            self.X[:, i:NT - 1:QT]).then_inc(stored, 16)
            e.dma_start(self.out[:, 0, :], self.X[0:NB, NT - 1]).then_inc(stored, 16)
            e.wait_ge(stored, 48)
        return {"sp": sp}


def lay_out(x):
    f = lambda a: np.ascontiguousarray(a)
    n = {k: np.asarray(v) for k, v in x.items()}

    def by_pair(a):
        a = a.reshape(2, P, *a.shape[1:])
        return np.moveaxis(a, 1, -1)

    small = np.zeros((P, 5, P), np.float32)
    b = by_pair(n["L0_tok_B_ri"])
    small[:, 0:2] = b.reshape(P, 2, P)
    small[:, 2] = by_pair(n["L0_tok_inv_A_real"]).reshape(P, P)
    small[:, 3] = by_pair(n["L0_tok_A_imag"]).reshape(P, P)
    small[:, 4] = np.broadcast_to(n["L0_tok_log_dt"].reshape(2, 1, P), (2, 64, P)).reshape(P, P)
    c = n["x"].reshape(NB, 2, P, 64, 2).transpose(1, 3, 4, 0, 2).reshape(P, 2, NB, P)

    def down(w):
        return w.T.reshape(DT, P, w.shape[0]).transpose(1, 0, 2)

    def padded(w):
        r = np.zeros((4, GRP, 32, D), np.float32)
        r[:, :, 0:HD] = w.T.reshape(4, GRP, HD, D)
        return r.transpose(1, 2, 0, 3).reshape(P, 4, D)

    wa = n["L0_attn_w_attn"]
    wq, wk, wv = wa[0:D], wa[D:2 * D], wa[2 * D:]
    swap = np.arange(D).reshape(-1, 2)[:, ::-1].reshape(-1)
    a = {
        "consts": constants()[0], "rope_mask": constants()[1], "s4_small": small, "s4_c": c,
        "cls": n["cls_tok"].reshape(1, D),
        "w_qkv0": down(np.concatenate([wq, wq[swap], wk, wk[swap], wv])).reshape(P, -1),
        "w_qkv1": down(np.concatenate([n["L1_attn_Wq"], n["L1_attn_Wk"], n["L1_attn_Wv"]])).reshape(P, -1),
        "w_o0": padded(n["L0_attn_w_proj"]), "w_o1": padded(n["L1_attn_Wo"]),
        "a_bias": np.concatenate([n["L1_attn_" + k].reshape(DT, P).T for k in ("bq", "bk")], axis=1),
        "a_bv": n["L1_attn_bv"][None, :], "a_bo": n["L1_attn_bo"][None, :],
        "router0": down(n["L0_ffn_gate_W"]).reshape(P, DT * E),
        "router1": n["L1_ffn_router_w"].reshape(DT, P, E).transpose(1, 0, 2).reshape(P, DT * E),
        "router_b0": np.zeros((P, E), np.float32),
        "router_b1": np.broadcast_to(n["L1_ffn_router_b"][None, :], (P, E)),
    }
    def up(e, s):
        w = np.concatenate([e, s[None]])
        return w.reshape(9, DT, P, -1).transpose(0, 2, 1, 3).reshape(9, 1, P, -1)

    def back(e, s):
        w = np.concatenate([e, s[None]])
        return w.reshape(9, -1, P, D).transpose(0, 2, 1, 3).reshape(9, 1, P, -1)
    a["ffn0"] = np.concatenate([up(n["L0_ffn_w1_e"], n["L0_ffn_w1_s"].transpose(1, 0, 2).reshape(D, 1024)),
                                up(n["L0_ffn_w3_e"], n["L0_ffn_w3_s"].transpose(1, 0, 2).reshape(D, 1024)),
                                back(n["L0_ffn_w2_e"], n["L0_ffn_w2_s"].reshape(1024, D))], axis=1)
    a["ffn1"] = np.concatenate([up(n["L1_ffn_rw1"], n["L1_ffn_sw1"]), back(n["L1_ffn_rw2"], n["L1_ffn_sw2"])], axis=1)
    a["ffn_b1"] = np.concatenate([n["L1_ffn_rb1"], n["L1_ffn_sb1"][None]]).reshape(9, 4, P).transpose(0, 2, 1)
    a["ffn_b2"] = np.concatenate([n["L1_ffn_rb2"], n["L1_ffn_sb2"][None]])
    return {k: f(v) for k, v in a.items()}


def kernel(**inputs):
    import concourse.bacc as _bacc
    from concourse.bass_utils import run_bass_kernel_spmd as _run

    arrays = lay_out(inputs)
    nc = _bacc.Bacc("TRN2", target_bir_lowering=False, num_devices=1)
    args = {k: nc.dram_tensor("in_" + k, v.shape, F32, kind="ExternalInput").ap() for k, v in arrays.items()}
    out = nc.dram_tensor("out", (NB, T, D), F32, kind="ExternalOutput").ap()
    Tower(nc, args, out).build()
    r = _run(nc, [{"in_" + k: a for k, a in arrays.items()}], core_ids=[0])
    return r.results[0]["out"]
```
